# Optimizing a Trainium2 kernel written in Bass

```python
import numpy as np
import jax
import jax.numpy as jnp

def _softmax(x, axis=-1):
    return jax.nn.softmax(x, axis=axis)

def _gelu(x):
    return jax.nn.gelu(x, approximate=True)

def _silu(x):
    return jax.nn.silu(x)

def _sigmoid(x):
    return jax.nn.sigmoid(x)

def _layernorm(x, axis=-1, eps=1e-05):
    m = jnp.mean(x, axis=axis, keepdims=True)
    v = jnp.var(x, axis=axis, keepdims=True)
    return (x - m) / jnp.sqrt(v + eps)

def _scatter_add(tgt, idx, src, axis=0):
    return tgt.at[idx].add(src)

def _segment_sum(src, seg, n):
    return jax.ops.segment_sum(src, seg, n)
kernel_name = 'mk_cond_resid_d2_seqx_r4_dddb3f'

def setup_inputs(seed: int=0):
    np.random.seed(seed)
    _w = jnp.asarray

    def _rec_inputs():
        import jax
        import jax.numpy as jnp
        _rk = jax.random.key(seed)
        x = 7.22e-05 + 1 * jax.random.normal(jax.random.fold_in(_rk, 1), (16, 256, 256), jnp.float32)
        _lenS = 256 - jax.random.randint(jax.random.fold_in(_rk, 7), (16,), 0, max(1, 256 // 4) + 1, jnp.int32)
        _lenS2 = 256 - jax.random.randint(jax.random.fold_in(_rk, 8), (16,), 0, max(1, 256 // 4) + 1, jnp.int32)
        fside_BxSxS_0 = 4.13588e-05 + 0.999923 * jax.random.normal(jax.random.fold_in(_rk, 11), (16, 256, 256), jnp.float32)
        itok_B_18_1004 = jax.random.randint(jax.random.fold_in(_rk, 12), (16,), 18, 1005, jnp.int32)
        condB_tauraws = -5.74692 + 0.777674 * jax.random.normal(jax.random.fold_in(_rk, 13), (16,), jnp.float32)
        cond_256 = -0.000235209 + 0.019331 * jax.random.normal(jax.random.fold_in(_rk, 14), (16, 64), jnp.float32)
        condB_bn2 = jnp.zeros((16,), jnp.float32)
        cond_1024 = -4.10585e-05 + 0.0199478 * jax.random.normal(jax.random.fold_in(_rk, 16), (16, 256), jnp.float32)
        return (x, fside_BxSxS_0, itok_B_18_1004, condB_tauraws, cond_256, condB_bn2, cond_1024)
    x, fside_BxSxS_0, itok_B_18_1004, condB_tauraws, cond_256, condB_bn2, cond_1024 = _rec_inputs()

    def _L0_cond_setup():
        import jax, jax.numpy as jnp
        import numpy as np
        B, L1, L2, DIN, DOUT, H = (8, 256, 256, 256, 256, 16)
        DH = DOUT // H
        SCALE = 1.0 / np.sqrt(DH).astype(np.float32)
        key = jax.random.key(seed)
        ks = jax.random.split(key, 13)
        s = 0.02
        return {'seq1': jax.random.normal(ks[0], (B, L1, DIN), jnp.float32), 'seq2': jax.random.normal(ks[1], (B, L2, DIN), jnp.float32), 'seq_len1': jax.random.randint(ks[2], (B,), 1, L1 + 1, jnp.int32), 'Wq': jax.random.normal(ks[3], (DIN, DOUT), jnp.float32) * s, 'bq': jnp.zeros((DOUT,), jnp.float32), 'Wk': jax.random.normal(ks[4], (DIN, DOUT), jnp.float32) * s, 'bk': jnp.zeros((DOUT,), jnp.float32), 'Wv': jax.random.normal(ks[5], (DIN, DOUT), jnp.float32) * s, 'bv': jnp.zeros((DOUT,), jnp.float32), 'Wo': jax.random.normal(ks[6], (DOUT, DOUT), jnp.float32) * s, 'bo': jnp.zeros((DOUT,), jnp.float32), 'b_prev': jax.random.normal(ks[7], (1, 1, DIN), jnp.float32) * s, 'b_self': jax.random.normal(ks[8], (1, 1, DIN), jnp.float32) * s}
    _L0_cond_all = _L0_cond_setup()
    _L0_cond_in = {k: v for k, v in _L0_cond_all.items() if k in ('Wq', 'bq', 'Wk', 'bk', 'Wv', 'bv', 'Wo', 'bo', 'b_prev', 'b_self')}
    del _L0_cond_all

    def _L1_cond_setup():
        import jax, jax.numpy as jnp
        import numpy as np
        import math
        B, T, E, D = (4, 512, 256, 4)

        def _tau_init(t):
            a = 0.1 ** (1.0 / max(t - 1, 1))
            tt = -math.log(max(a, 1e-10))
            return math.log(math.exp(tt) - 1 + 1e-10)

        def causal_ema(b, tau_raw):
            alpha = jnp.exp(-jax.nn.softplus(tau_raw)).astype(b.dtype)

            def step(h, bt):
                h = alpha * h + bt
                return (h, h)
            h0 = jnp.zeros((b.shape[0], b.shape[2]), b.dtype)
            _, hs = jax.lax.scan(step, h0, jnp.swapaxes(b, 0, 1))
            return jnp.swapaxes(hs, 0, 1)
        key = jax.random.key(seed)
        ks = jax.random.split(key, 10)
        s = 0.02
        return {'x': jax.random.normal(ks[0], (B, T, E), jnp.float32), 'tau_ctx': jnp.float32(_tau_init(max(T // 2, 4))), 'tau_raws': jnp.array([_tau_init(max(T // 2 ** i, 2)) for i in range(D)], jnp.float32), 'Wg': jax.random.normal(ks[1], (E, 2 * E), jnp.float32) * s, 'bg': jnp.full((E,), -0.5, jnp.float32), 'Wn1': jax.random.normal(ks[2], (E // 4, E), jnp.float32) * s, 'bn1': jnp.zeros((E // 4,), jnp.float32), 'Wn2': jax.random.normal(ks[3], (D, E // 4), jnp.float32) * s, 'bn2': jnp.zeros((D,), jnp.float32), 'blend': jax.random.normal(ks[4], (D, E), jnp.float32) * s, 'Wsoma': jax.random.normal(ks[5], (E, E), jnp.float32) * s, 'bsoma': jnp.zeros((E,), jnp.float32), 'Wtemp': jax.random.normal(ks[6], (E, E), jnp.float32) * s, 'btemp': jnp.zeros((E,), jnp.float32), 'Wout': jax.random.normal(ks[7], (E, E), jnp.float32) * s, 'gamma': jnp.ones((E,), jnp.float32), 'beta': jnp.zeros((E,), jnp.float32)}
    _L1_cond_all = _L1_cond_setup()
    _L1_cond_in = {k: v for k, v in _L1_cond_all.items() if k in ('tau_ctx', 'Wg', 'bg', 'Wn1', 'bn1', 'Wsoma', 'bsoma', 'Wtemp', 'btemp', 'Wout', 'gamma', 'beta')}
    del _L1_cond_all
    return {'x': x, 'fside_BxSxS_0': fside_BxSxS_0, 'itok_B_18_1004': itok_B_18_1004, 'condB_tauraws': condB_tauraws, 'cond_256': cond_256, 'condB_bn2': condB_bn2, 'cond_1024': cond_1024, 'L0_cond_Wq': _L0_cond_in['Wq'], 'L0_cond_bq': _L0_cond_in['bq'], 'L0_cond_Wk': _L0_cond_in['Wk'], 'L0_cond_bk': _L0_cond_in['bk'], 'L0_cond_Wv': _L0_cond_in['Wv'], 'L0_cond_bv': _L0_cond_in['bv'], 'L0_cond_Wo': _L0_cond_in['Wo'], 'L0_cond_bo': _L0_cond_in['bo'], 'L0_cond_b_prev': _L0_cond_in['b_prev'], 'L0_cond_b_self': _L0_cond_in['b_self'], 'L1_cond_tau_ctx': _L1_cond_in['tau_ctx'], 'L1_cond_Wg': _L1_cond_in['Wg'], 'L1_cond_bg': _L1_cond_in['bg'], 'L1_cond_Wn1': _L1_cond_in['Wn1'], 'L1_cond_bn1': _L1_cond_in['bn1'], 'L1_cond_Wsoma': _L1_cond_in['Wsoma'], 'L1_cond_bsoma': _L1_cond_in['bsoma'], 'L1_cond_Wtemp': _L1_cond_in['Wtemp'], 'L1_cond_btemp': _L1_cond_in['btemp'], 'L1_cond_Wout': _L1_cond_in['Wout'], 'L1_cond_gamma': _L1_cond_in['gamma'], 'L1_cond_beta': _L1_cond_in['beta']}

def reference(x, fside_BxSxS_0, itok_B_18_1004, condB_tauraws, cond_256, condB_bn2, cond_1024, L0_cond_Wq, L0_cond_bq, L0_cond_Wk, L0_cond_bk, L0_cond_Wv, L0_cond_bv, L0_cond_Wo, L0_cond_bo, L0_cond_b_prev, L0_cond_b_self, L1_cond_tau_ctx, L1_cond_Wg, L1_cond_bg, L1_cond_Wn1, L1_cond_bn1, L1_cond_Wsoma, L1_cond_bsoma, L1_cond_Wtemp, L1_cond_btemp, L1_cond_Wout, L1_cond_gamma, L1_cond_beta):
    import jax
    import jax.numpy as jnp

    def _L0_cond_ref(seq1, seq2, seq_len1, Wq, bq, Wk, bk, Wv, bv, Wo, bo, b_prev, b_self):
        import jax, jax.numpy as jnp
        import numpy as np
        B, L1, L2, DIN, DOUT, H = (8, 256, 256, 256, 256, 16)
        DH = DOUT // H
        SCALE = 1.0 / np.sqrt(DH).astype(np.float32)
        b, l1, _ = seq1.shape
        l2 = seq2.shape[1]
        query = seq2 + b_self
        key = jnp.concatenate([seq1 + b_prev, seq2 + b_self], 1)
        value = jnp.concatenate([seq1, seq2], 1)
        q = (query @ Wq + bq).reshape(b, l2, H, DH).transpose(0, 2, 1, 3)
        k = (key @ Wk + bk).reshape(b, l1 + l2, H, DH).transpose(0, 2, 1, 3)
        v = (value @ Wv + bv).reshape(b, l1 + l2, H, DH).transpose(0, 2, 1, 3)
        score_prev = jnp.einsum('bhqd,bhkd->bhqk', q, k[:, :, :l1]) * SCALE
        score_self = (q * k[:, :, l1:]).sum(-1, keepdims=True) * SCALE
        mask = jnp.arange(l1)[None, :] < seq_len1[:, None]
        score_prev = jnp.where(mask[:, None, None, :], score_prev, -jnp.inf)
        score = jnp.concatenate([score_prev, score_self], -1)
        weights = jax.nn.softmax(score, axis=-1)
        attn = jnp.einsum('bhqk,bhkd->bhqd', weights[..., :-1], v[:, :, :l1])
        attn = attn + weights[..., -1:] * v[:, :, l1:]
        attn = attn.transpose(0, 2, 1, 3).reshape(b, l2, H * DH)
        return attn @ Wo + bo

    def _L1_cond_ref(x, tau_ctx, tau_raws, Wg, bg, Wn1, bn1, Wn2, bn2, blend, Wsoma, bsoma, Wtemp, btemp, Wout, gamma, beta):
        import jax, jax.numpy as jnp
        import numpy as np
        import math
        B, T, E, D = (4, 512, 256, 4)

        def _tau_init(t):
            a = 0.1 ** (1.0 / max(t - 1, 1))
            tt = -math.log(max(a, 1e-10))
            return math.log(math.exp(tt) - 1 + 1e-10)

        def causal_ema(b, tau_raw):
            alpha = jnp.exp(-jax.nn.softplus(tau_raw)).astype(b.dtype)

            def step(h, bt):
                h = alpha * h + bt
                return (h, h)
            h0 = jnp.zeros((b.shape[0], b.shape[2]), b.dtype)
            _, hs = jax.lax.scan(step, h0, jnp.swapaxes(b, 0, 1))
            return jnp.swapaxes(hs, 0, 1)
        ctx = causal_ema(x, tau_ctx)
        gate_in = jnp.concatenate([x, ctx], axis=-1)
        wg = jax.nn.sigmoid(jnp.einsum('btc,ec->bte', gate_in, Wg) + bg)
        gated = x * wg
        h1 = jax.nn.gelu(jnp.einsum('btc,hc->bth', x, Wn1) + bn1, approximate=False)
        mod = 0.5 + jax.nn.sigmoid(jnp.einsum('bth,dh->btd', h1, Wn2) + bn2)
        traces = jax.vmap(lambda tau, m: causal_ema(gated * m[..., None], tau))(tau_raws, jnp.moveaxis(mod, -1, 0))
        blend_w = jax.nn.softmax(blend, axis=0)
        temporal = jnp.einsum('dbtc,dc->btc', traces, blend_w)
        gate = jax.nn.sigmoid(jnp.einsum('btc,ec->bte', temporal, Wtemp) + btemp)
        soma = jax.nn.gelu(jnp.einsum('btc,ec->bte', x, Wsoma) + bsoma, approximate=False)
        out = jnp.einsum('btc,ec->bte', soma * gate, Wout)
        mu = out.mean(-1, keepdims=True)
        var = out.var(-1, keepdims=True)
        return (out - mu) / jnp.sqrt(var + 1e-05) * gamma + beta
    x = x + _L0_cond_ref(x, fside_BxSxS_0, itok_B_18_1004, L0_cond_Wq, L0_cond_bq, L0_cond_Wk, L0_cond_bk, L0_cond_Wv, L0_cond_bv, L0_cond_Wo, L0_cond_bo, L0_cond_b_prev, L0_cond_b_self)
    x = x + _L1_cond_ref(x, L1_cond_tau_ctx, condB_tauraws, L1_cond_Wg, L1_cond_bg, L1_cond_Wn1, L1_cond_bn1, cond_256, condB_bn2, cond_1024, L1_cond_Wsoma, L1_cond_bsoma, L1_cond_Wtemp, L1_cond_btemp, L1_cond_Wout, L1_cond_gamma, L1_cond_beta)
    return x

_drawn_inputs = setup_inputs


def setup_inputs(seed=0):
    import zlib

    import numpy as np

    out = dict(_drawn_inputs(seed))
    spreads = {'condB_bn2': (0.0, 2.0),
     'L0_cond_bq': (0.0, 0.8),
     'L0_cond_bk': (0.0, 2.0),
     'L0_cond_bv': (0.0, 0.1),
     'L0_cond_bo': (0.0, 0.1),
     'L1_cond_bg': (-0.5, 0.6),
     'L1_cond_bn1': (0.0, 2.0),
     'L1_cond_bsoma': (0.0, 0.1),
     'L1_cond_btemp': (0.0, 0.33),
     'L1_cond_gamma': (1.0, 0.2),
     'L1_cond_beta': (0.0, 0.1)}
    factors = {'fside_BxSxS_0': 8.0,
     'condB_tauraws': 8.0,
     'cond_256': 8.0,
     'cond_1024': 64.0,
     'L0_cond_Wq': 8.0,
     'L0_cond_Wk': 8.0,
     'L0_cond_b_prev': 8.0,
     'L0_cond_b_self': 8.0,
     'L1_cond_Wn1': 8.0}
    for name, (base, spread) in spreads.items():
        noise = np.random.default_rng([zlib.crc32(name.encode()), seed]).standard_normal(out[name].shape)
        drawn = base * np.exp(spread * noise) if base else spread * noise
        out[name] = jnp.asarray(drawn.astype(out[name].dtype))
    for name, factor in factors.items():
        out[name] = (out[name] * factor).astype(out[name].dtype)
    return out
```

```python
from contextlib import ExitStack

import numpy as np

import concourse.bass as bass
from concourse import mybir

ALU = mybir.AluOpType
ACT = mybir.ActivationFunctionType
AX = mybir.AxisListType
F32 = mybir.dt.float32
BF16 = mybir.dt.bfloat16

P = 128
B, T, E, H = 16, 256, 256, 16
DH = E // H
NB = E // P
D = 16
HID = 64
CH = 8
NCH = T // CH
NEAR_AT = (14, 15, 17, 19, 21, 22, 25, 27)
SB = 4
SCALE = 1.0 / float(np.sqrt(DH))
EPS = 1e-5
MASKED = -1e30
KROWS = 96
PARTS = ((0, 0), (0, 1), (1, 0), (1, 1), (0, 2), (2, 0))

FIRST, LOOP_FIRST, PAIRS, LAST = -1, 5, (B - 1 - 5) // 2, B + 2
STEPS = 32
M_AT = 3
A_AT = 22
A_NOW = STEPS - A_AT


class Step:

    def __init__(self, k, c):
        self.k, self.c, self.par = k, c, c % 2

    def __add__(self, lag):
        return Step(self.k, self.c + lag)

    def number(self):
        return self.c if self.k is None else self.k * 2 + self.c

    def half(self):
        return self.c // 2 if self.k is None else self.k + self.c // 2

    def valid(self):
        return self.k is not None or 0 <= self.c < B


def iterations(eng, body):
    for c in range(FIRST, LOOP_FIRST):
        body(Step(None, c))
    with eng.Fori(0, PAIRS) as k:
        body(Step(k, LOOP_FIRST))
        body(Step(k, LOOP_FIRST + 1))
    for c in range(LOOP_FIRST + 2 * PAIRS, LAST + 1):
        body(Step(None, c))


class Signal:

    def __init__(self, sem, per=1):
        self.sem, self.per = sem, per

    def at(self, batch, nth=None):
        return batch.number() * self.per + (self.per if nth is None else nth)


def wait(eng, signal, batch, nth=None):
    if batch.k is None and batch.c < 0:
        return
    eng.wait_ge(signal.sem, signal.at(batch, nth))


def wait_dma(eng, pair, batch, per):
    if batch.k is None and batch.c < 0:
        return
    eng.wait_ge(pair[batch.par], batch.half() * per + per)


class Banks:

    def __init__(self, tiles, uses):
        self.tiles, self.uses = tiles, uses
        self.pos = {use[0]: n for n, use in enumerate(uses)}

    def bank(self, name):
        return self.tiles[self.pos[name] % len(self.tiles)]

    def wait_free(self, eng, name, i):
        at, n = self.pos[name], len(self.tiles)
        same = [q for q in range(len(self.uses)) if q % n == at % n]
        before = [(q, 0) for q in same if q < at]
        while True:
            if not before:
                i, before = i + -1, [(q, 0) for q in same]
                if i.k is None and i.c < FIRST:
                    return
            q = before.pop()[0]
            _, lag, signal, nth = self.uses[q]
            if (i + lag).valid():
                return wait(eng, signal, i + lag, nth)


DVE_SP1, DVE_SP2, DVE_SP3, DVE_EXP, DVE_BLEND, DVE_MASK, DVE_DONE = 1, 2, 4, 7, 12, 19, 43
ACT_DONE, POOL_DONE = 7, 12


def build(nc, d, out):
    ctx = ExitStack()
    with ctx:
        def sb(name, shape, dt=F32):
            return ctx.enter_context(nc.sbuf_tensor(name, shape, dt))

        def two(name, shape, dt=F32):
            return [sb(f"{name}{p}", shape, dt) for p in range(2)]

        def psum(name, shape):
            return ctx.enter_context(nc.psum_tensor(name, shape, F32))

        def sem(name):
            return ctx.enter_context(nc.semaphore(name))

        def signal(name, per=1):
            return Signal(sem(name), per)

        wq, wk, wv, wo = (sb(n, [P, NB, E]) for n in ("wq", "wk", "wv", "wo"))
        wg = sb("wg", [P, 2 * NB, E])
        wn1 = sb("wn1", [P, NB, HID])
        wn2 = sb("wn2", [P, P])
        wsoma, wtemp, wout = (sb(n, [P, NB, E]) for n in ("wsoma", "wtemp", "wout"))
        cols = sb("cols", [P, 26])
        bv_row, gamma_row, beta_row = (sb(n, [P, E]) for n in ("bv_row", "gamma_row", "beta_row"))
        ident = sb("ident", [P, P])
        ident_b = sb("ident_b", [P, P], BF16)
        bias_q, bias_kp, bias_ks = (sb(n, [P, NB]) for n in ("bias_q", "bias_kp", "bias_ks"))
        half_b = sb("half_b", [P, 5])
        taus, sp, sp_t, sp_u = (sb(n, [P, D + 2]) for n in ("taus", "sp", "sp_t", "sp_u"))
        neg_sp = sb("neg_sp", [P, 1])
        decay = sb("decay", [P, T])
        far_in = sb("far_in", [P, 6 * CH, D])
        far_out = sb("far_out", [P, 2, P])
        pow_col = sb("pow_col", [P, CH])
        blend_t = sb("blend_t", [P, NB, D])
        blend_m, blend_s = sb("blend_m", [P, NB]), sb("blend_s", [P, NB])
        blend_8 = sb("blend_8", [P, NB, 8, D])
        blend = sb("blend", [P, E])
        near_w = sb("near_w", [P, CH, E], BF16)
        consts = sb("consts", [P, 2 * 6 * CH * D + 4 * P + CH + 3])
        iota_k, lens_i, lens = sb("iota_k", [B, T]), sb("lens_i", [B, 1], mybir.dt.int32), sb("lens", [B, 1])
        mask_rows = sb("mask_rows", [B, T], BF16)
        minus_half = sb("minus_half", [P, NB])
        mask_dram = nc.dram_tensor("mask_scratch", (B, T), BF16, kind="Internal").ap()

        nA = 6 * CH * D
        c_far_e = consts[:, 0:nA].rearrange("p (j d) -> p j d", d=D)
        c_far_m = consts[:, nA:2 * nA].rearrange("p (j d) -> p j d", d=D)
        c_out_e = consts[:, 2 * nA:2 * nA + 2 * P].rearrange("p (a t) -> p a t", a=2)
        c_out_m = consts[:, 2 * nA + 2 * P:2 * nA + 4 * P].rearrange("p (a t) -> p a t", a=2)
        c_dist = consts[:, 2 * nA + 4 * P:2 * nA + 4 * P + CH]
        c_slot = consts[:, 2 * nA + 4 * P + CH:2 * nA + 4 * P + CH + 3]

        def col(name, n=0):
            at = {"bq": 0, "bk": 2, "b_self": 4, "b_prev": 6, "bo": 8, "bg": 10, "bsoma": 12, "btemp": 14,
                  "bn1": 16, "bn2": 17}[name] + n
            return cols[:, at:at + 1]

        xt, x2t, xe = two("xt", [P, NB, T]), two("x2t", [P, NB, T]), two("xe", [P, NB, T])
        qf, kf = sb("qf", [P, NB, T]), sb("kf", [P, NB, T])
        q_res, k_res = sb("q_res", [P, NB, T]), sb("k_res", [P, NB, T])
        q_part = [sb(f"q_part{n}", [P, NB, T], BF16) for n in range(3)]
        k_part = [sb(f"k_part{n}", [P, NB, T], BF16) for n in range(3)]
        q_stack, k_stack = two("q_stack", [P, H, T], BF16), two("k_stack", [P, H, T], BF16)
        self_prod = sb("self_prod", [P, NB, T])
        self_score = two("self_score", [P, NB, H])
        v_ones = two("v_ones", [P, NB, H, 32])
        v_self = two("v_self", [P, NB, E])
        row_max, top, neg_res = sb("row_max", [P, NB, H]), sb("top", [P, NB, H]), sb("neg_res", [P, NB, H])
        neg_part = sb("neg_part", [P, NB, 3, H], BF16)
        neg_t = sb("neg_t", [3 * H, T], BF16)
        self_diff, self_p = sb("self_diff", [P, NB, H]), sb("self_p", [P, NB, H])
        self_pv = sb("self_pv", [P, NB, E])
        probs = sb("probs", [P, 8, NB, T])
        o_t = sb("o_t", [P, 4, T])
        den, rden = sb("den", [P, NB, H]), sb("rden", [P, NB, H])
        num, attn, attn_t = sb("num", [P, NB, E]), sb("attn", [P, NB, E]), sb("attn_t", [P, NB, T])
        x1t = two("x1t", [P, NB, T])
        ctx_t = sb("ctx_t", [P, NB, T])
        gate_g, gated, gated_n = sb("gate_g", [P, NB, T]), sb("gated", [P, NB, T]), sb("gated_n", [P, NB, E])
        hid = sb("hid", [P, T])
        mod, mod_res, mod_mid = sb("mod", [P, T]), sb("mod_res", [P, T]), sb("mod_mid", [P, T], BF16)
        mod_th = sb("mod_th", [P, T])
        mod_stack = sb("mod_stack", [P, T], BF16)
        mod_n = sb("mod_n", [P, NB, D])
        state_in = sb("state_in", [P, 6 * CH, D])
        states = sb("states", [P, SB, E])
        near_p = two("near_p", [P, NB * NCH, CH])
        near_sum = sb("near_sum", [P, NB, T])
        far_n = sb("far_n", [P, NB, E])
        temporal = sb("temporal", [P, NB, T])
        gate_t, soma, mixed = sb("gate_t", [P, NB, T]), sb("soma", [P, NB, T]), sb("mixed", [P, NB, T])
        x1_beta = sb("x1_beta", [P, NB, E])
        stats, mean_var = sb("stats", [P, NB, 6]), sb("mean_var", [P, NB, 2])
        var_eps, rstd = sb("var_eps", [P, NB]), sb("rstd", [P, NB])
        centred = sb("centred", [P, NB, E])
        result = two("result", [P, NB, E])

        near_f, near_r = (probs[:, 4 * n:4 * n + 4, :, :].rearrange("p a n t -> p (a n) t") for n in range(2))
        near_h, near_m = (t[:, :, :].rearrange("p a t -> p (a t)").bitcast(BF16).rearrange("p (n c) -> p n c", n=CH)
                          for t in (o_t, states))

        s_psum = [psum(f"s_psum{n}", [P, 512]) for n in range(2)]
        o_psum = [psum(f"o_psum{n}", [P, 512]) for n in range(2)]
        side_psum = [psum(f"side_psum{n}", [P, 512]) for n in range(4)]

        loaded, set_dve, set_act, set_pe, set_pool = (sem(n) for n in ("loaded", "set_dve", "set_act", "set_pe",
                                                                       "set_pool"))
        mask_stored = sem("mask_stored")
        pe_passed, dve_passed, pool_passed, sp_passed = (sem(n + "_passed") for n in ("pe", "dve", "pool", "sp"))
        x_in = [sem(f"x_in{p}") for p in range(2)]
        xe_in = [sem(f"xe_in{p}") for p in range(2)]
        q_stacked = [sem(f"q_stacked{p}") for p in range(2)]
        k_stacked = [sem(f"k_stacked{p}") for p in range(2)]
        max_stacked = [sem(f"max_stacked{p}") for p in range(2)]
        stored = [sem(f"stored{p}") for p in range(2)]
        NQ, NK, NM, NX = 16 * 2 * len(PARTS), 16 * (2 * len(PARTS) + 1), 16 * 3, 16 * 2
        pe_wg, pe_q, pe_k, pe_ks, pe_vp, pe_vs, pe_prn, pe_gn, pe_h1, pe_soma, pe_x1n, pe_mod, pe_modn, pe_at, \
            pe_wo, pe_y, pe_yt, pe_nm, pe_gate, pe_out = (signal("pe_" + n) for n in (
                "wg", "q", "k", "ks", "vp", "vs", "prn", "gn", "h1", "soma", "x1n", "mod", "modn", "at", "wo",
                "y", "yt", "nm", "gate", "out"))
        pe_on, pe_far, pe_near = signal("pe_on", 2), signal("pe_far", 2), signal("pe_near", CH)
        pe_max, pe_score, pe_av = signal("pe_max", H), signal("pe_score", H), signal("pe_av", 4)
        q_ready, k_ready = signal("q_ready"), signal("k_ready")
        q_high, k_high, q_mid, k_mid = (signal(n) for n in ("q_high", "k_high", "q_mid", "k_mid"))
        probs_ready, o_ready, attn_t_ready = signal("probs_ready", H), signal("o_ready", 2), signal("attn_t_ready")
        gate_g_ready, hid_ready, mod_th_ready, gated_n_ready, far_n_ready, gate_t_ready, soma_ready, neg_t_ready, \
            self_p_ready = (signal(n + "_ready") for n in (
                "gate_g", "hid", "mod_th", "gated_n", "far_n", "gate_t", "soma", "neg_t", "self_p"))
        max_ready = signal("max_ready", H)
        neg_chain = signal("neg_chain", 6)
        gated_ready, self_prod_ready, self_score_ready, v_ready, v_self_ready, mod_n_ready, x1_ready, ctx_ready, \
            temporal_ready, mixed_ready, x1_beta_ready, result_ready = (signal(n + "_ready") for n in (
                "gated", "self_prod", "self_score", "v", "v_self", "mod_n", "x1", "ctx", "temporal", "mixed",
                "x1_beta", "result"))
        states_ready = signal("states_ready", 2)
        num_chain = signal("num_chain", 5)
        near_prod = signal("near_prod", CH)
        norm_chain = signal("norm_chain", 7)
        q_res_ready, k_res_ready, q_low, k_low, mod_ready, state_in_ready, attn_ready, self_pv_ready, rstd_ready = (
            signal(n) for n in ("q_res_ready", "k_res_ready", "q_low", "k_low", "mod_ready", "state_in_ready",
                                "attn_ready", "self_pv_ready", "rstd_ready"))
        mod_chain = signal("mod_chain", 5)
        near_added = signal("near_added", CH - 1)

        side = Banks(side_psum, [
            ("wg", -2, gate_g_ready, 1), ("gate", -3, gate_t_ready, 1), ("q", 1, q_ready, 1),
            ("gn", -2, gated_n_ready, 1), ("k", 1, k_ready, 1), ("h1", -2, hid_ready, 1), ("out", -3, norm_chain, 7),
            ("soma", -2, soma_ready, 1), ("on0", -1, num_chain, 2), ("on1", -1, num_chain, 4),
            ("mod", -2, mod_th_ready, 1), ("x1n", -2, x1_beta_ready, 1), ("modn", -2, mod_n_ready, 1),
            ("near0", -2, near_prod, 1), ("at", -1, attn_t_ready, 1), ("near1", -2, near_prod, 2),
            ("wo", -1, x1_ready, 1), ("near2", -2, near_prod, 3), ("far0", -2, states_ready, 1),
            ("far1", -2, states_ready, 2), ("near3", -2, near_prod, 4), ("nm", 0, neg_t_ready, 1),
            ("y", -2, far_n_ready, 1), ("near4", -2, near_prod, 5), ("near5", -2, near_prod, 6),
            ("ks", 1, self_prod_ready, 1), ("near6", -2, near_prod, 7), ("vs", 1, v_self_ready, 1),
            ("near7", -2, near_prod, 8), ("yt", -2, temporal_ready, 1), ("vp", 1, v_ready, 1),
            ("prn", 1, self_score_ready, 1)])
        score_uses = []
        for u in range(STEPS):
            if u < H - A_NOW:
                score_uses.append((f"a{A_NOW + u}", -1, probs_ready, A_NOW + u + 1))
            if M_AT <= u < M_AT + H:
                score_uses.append((f"m{u - M_AT}", 0, max_ready, u - M_AT + 1))
            if u >= A_AT:
                score_uses.append((f"a{u - A_AT}", 0, probs_ready, u - A_AT + 1))
        score = Banks(s_psum, score_uses)

        block = ctx.enter_context(nc.Block())
        loads = [(wq[:, :, :], d["wq"]), (wk[:, :, :], d["wk"]), (wv[:, :, :], d["wv"]), (wo[:, :, :], d["wo"]),
                 (wg[:, :, :], d["wg"]), (wn1[:, :, :], d["wn1"]), (wn2[0:HID, :], d["wn2"]),
                 (wsoma[:, :, :], d["wsoma"]), (wtemp[:, :, :], d["wtemp"]), (wout[:, :, :], d["wout"]),
                 (cols[:, :], d["cols"]), (bv_row[:, :], d["bv"]), (gamma_row[:, :], d["gamma"]),
                 (beta_row[:, :], d["beta"]), (taus[:, :], d["taus"]), (blend_t[:, :, :], d["blend"]),
                 (consts[:, :], d["consts"]), (ident[:, :], d["ident"]), (ident_b[:, :], d["ident_b"]),
                 (iota_k[:, :], d["iota"]), (lens_i[:, :], d["lens"])]

        def passed_by(eng, count):
            eng.sem_inc(count, 1)

        @block.sync
        def _(sp_eng):
            for dst, src in loads:
                sp_eng.dma_start(dst, src).then_inc(loaded, 16)
            sp_eng.wait_ge(set_dve, DVE_MASK)
            sp_eng.dma_start(mask_dram, mask_rows[:, :]).then_inc(mask_stored, 16)
            sp_eng.wait_ge(mask_stored, 16)

            def body(i):
                b = i + 1
                if b.valid():
                    for s in (pe_vp, pe_vs):
                        wait(sp_eng, s, b + -2)
                    passed_by(sp_eng, sp_passed)
                    sp_eng.dma_start(x2t[b.par][:, :, :], d["x2t"][b.number()]).then_inc(x_in[b.par], 16)
                    sp_eng.dma_start(xt[b.par][:, :, :], d["xt"][b.number()]).then_inc(x_in[b.par], 16)
                b = i
                if b.valid():
                    wait(sp_eng, x1_ready, b + -2)
                    passed_by(sp_eng, sp_passed)
                    sp_eng.dma_start(xe[b.par][:, :, :], d["xt"][b.number()]).then_inc(xe_in[b.par], 16)
                b = i + 1
                if b.valid():
                    wait(sp_eng, pe_score, b + -2)
                    passed_by(sp_eng, sp_passed)
                    for part, stack, ready, dsem, side_of in ((q_part, q_stack, (q_high, q_mid, q_low), q_stacked, 0),
                                                              (k_part, k_stack, (k_high, k_mid, k_low), k_stacked, 1)):
                        for n in range(3):
                            wait(sp_eng, ready[n], b)
                            for row, pair in enumerate(PARTS):
                                if pair[side_of] != n:
                                    continue
                                for e in range(NB):
                                    sp_eng.dma_start(stack[b.par][16 * row:16 * row + 16, 8 * e:8 * e + 8, :],
                                                     part[n][:, e, :]).then_inc(dsem[b.par], 16)
                    sp_eng.dma_start(k_stack[b.par][KROWS:KROWS + 1, :, :],
                                     d["mask"](mask_dram, b.number())).then_inc(k_stacked[b.par], 16)
                b = i + -3
                if b.valid():
                    wait(sp_eng, result_ready, b)
                    passed_by(sp_eng, sp_passed)
                    sp_eng.dma_start(out[b.number()], result[b.par][:, :, :]).then_inc(stored[b.par], 16)
                b = i
                if b.valid():
                    wait(sp_eng, neg_t_ready, b)
                    for n in range(3):
                        sp_eng.dma_start(q_stack[b.par][KROWS + 1 + n:KROWS + 2 + n, :, :],
                                         neg_t[16 * n:16 * n + 16, :]).then_inc(max_stacked[b.par], 16)

            iterations(sp_eng, body)
            for p in range(2):
                sp_eng.wait_ge(stored[p], 16 * (B // 2))

        @block.tensor
        def _(pe):
            mm, tr = nc.tensor.matmul, nc.tensor.transpose

            def product(dst, lhs, rhs, kbs, start=True):
                for k in kbs:
                    last = mm(dst, lhs(k), rhs(k), start=(k == kbs[0]), stop=(k == kbs[-1]))
                return last

            def blk(n):
                return slice(P * n, P * n + P)

            pe.wait_ge(loaded, 16 * len(loads))
            ps = side_psum[0]
            for n, (w, c) in enumerate(((wq, "b_self"), (wk, "b_prev"), (wk, "b_self"))):
                for e in range(NB):
                    last = product(ps[:, 2 * n + e:2 * n + e + 1], lambda k: w[:, k, blk(e)],
                                   lambda k: col(c, k), (0, 1))
            last.then_inc(set_pe, 1)
            pe.wait_ge(set_dve, DVE_BLEND)
            for e in range(NB):
                last = tr(side_psum[1][:, blk(e)], blend_8[:, e, :, :].rearrange("p r d -> p (r d)"), ident[:, :])
            last.then_inc(set_pe, 1)
            pe.wait_ge(set_dve, DVE_DONE)
            pe.wait_ge(set_pool, POOL_DONE)
            pe.wait_ge(set_act, ACT_DONE)

            def projected(name, done, b, weights, rows, i):
                side.wait_free(pe, name, i)
                ps = side.bank(name)
                for e in range(NB):
                    last = product(ps[:, 256 * e:256 * e + 256], lambda k: weights[:, k, blk(e)],
                                   rows, range(NB))
                last.then_inc(done.sem, 1)

            def natural(name, done, rows, weights, i):
                side.wait_free(pe, name, i)
                ps = side.bank(name)
                for t in range(NB):
                    last = product(ps[:, 256 * t:256 * t + 256], lambda k: rows[:, k, blk(t)],
                                   lambda k: weights[:, k, :], (0, 1))
                last.then_inc(done.sem, 1)

            def flipped(name, done, src, i):
                side.wait_free(pe, name, i)
                ps = side.bank(name)
                for a in range(NB):
                    for c in range(NB):
                        last = tr(ps[:, 256 * a + P * c:256 * a + P * c + P], src[:, c, blk(a)], ident[:, :])
                last.then_inc(done.sem, 1)

            def max_scores(b, h, i):
                if h == 0:
                    wait_dma(pe, q_stacked, b, NQ)
                    wait_dma(pe, k_stacked, b, NK)
                score.wait_free(pe, f"m{h}", i)
                ps = score.bank(f"m{h}")
                for t in range(NB):
                    last = mm(ps[:, 256 * t:256 * t + 256], q_stack[b.par][0:KROWS + 1, h, blk(t)],
                              k_stack[b.par][0:KROWS + 1, h, :], start=True, stop=True)
                last.then_inc(pe_max.sem, 1)

            def attend_scores(b, h, i):
                if h == 0:
                    wait_dma(pe, max_stacked, b, NM)
                score.wait_free(pe, f"a{h}", i)
                ps = score.bank(f"a{h}")
                for k in range(NB):
                    last = mm(ps[:, 256 * k:256 * k + 256], k_stack[b.par][0:KROWS + 4, h, blk(k)],
                              q_stack[b.par][0:KROWS + 4, h, :], start=True, stop=True)
                last.then_inc(pe_score.sem, 1)

            def attend_values(b, g):
                wait(pe, probs_ready, b, 4 * g + 4)
                if g == 0:
                    wait(pe, v_ready, b)
                if g % 2 == 0:
                    wait(pe, o_ready, b + -1, g // 2 + 1)
                for k in range(NB):
                    for j in range(4):
                        h = 4 * g + j
                        last = mm(o_psum[g // 2][32 * j:32 * j + 32, 256 * (g % 2):256 * (g % 2) + 256],
                                  v_ones[b.par][:, k, h, :], probs[:, h % 8, k, :], start=(k == 0), stop=(k == NB - 1))
                last.then_inc(pe_av.sem, 1)

            def near(b, n, i):
                if n == 0:
                    wait(pe, mod_chain, b)
                side.wait_free(pe, f"near{n}", i)
                w = NCH * (CH - n)
                rhs = mod_stack[:, :].rearrange("p (j r) -> p j r", r=CH)[:, :, 0:CH - n]
                for c in range(NB):
                    last = mm(side.bank(f"near{n}")[:, w * c:w * c + w], near_w[:, n, blk(c)], rhs, start=True, stop=True)
                last.then_inc(pe_near.sem, 1)

            def body(i):
                bp, bm, bt, bx, bz = i + 1, i, i + -1, i + -2, i + -3
                for u in range(STEPS):
                    if u < H - A_NOW and bt.valid():
                        attend_scores(bt, A_NOW + u, i)
                    if M_AT <= u < M_AT + H and bm.valid():
                        max_scores(bm, u - M_AT, i)
                    if u >= A_AT and bm.valid():
                        attend_scores(bm, u - A_AT, i)
                    if u == 0 and bx.valid():
                        wait(pe, ctx_ready, bx)
                        side.wait_free(pe, "wg", i)
                        for e in range(NB):
                            last = product(side.bank("wg")[:, 256 * e:256 * e + 256], lambda k: wg[:, k, blk(e)],
                                           lambda k: x1t[bx.par][:, k, :] if k < NB else ctx_t[:, k - NB, :],
                                           range(2 * NB))
                        last.then_inc(pe_wg.sem, 1)
                    if u == 2 and bz.valid():
                        wait(pe, temporal_ready, bz)
                        projected("gate", pe_gate, bz, wtemp, lambda k: temporal[:, k, :], i)
                    if u == 3 and bp.valid():
                        wait_dma(pe, x_in, bp, NX)
                        projected("q", pe_q, bp, wq, lambda k: x2t[bp.par][:, k, :], i)
                    if u == 4 and bt.valid():
                        attend_values(bt, 2)
                    if u == 5 and bx.valid():
                        wait(pe, gated_ready, bx)
                        flipped("gn", pe_gn, gated, i)
                    if u == 6 and bp.valid():
                        projected("k", pe_k, bp, wk, lambda k: xt[bp.par][:, k, :], i)
                    if u == 7:
                        if bt.valid():
                            attend_values(bt, 3)
                        if bx.valid():
                            side.wait_free(pe, "h1", i)
                            product(side.bank("h1")[0:HID, 0:T], lambda k: wn1[:, k, :],
                                    lambda k: x1t[bx.par][:, k, :], (0, 1)).then_inc(pe_h1.sem, 1)
                    if u == 8 and bz.valid():
                        wait(pe, mixed_ready, bz)
                        natural("out", pe_out, mixed, wout, i)
                    if u == 9 and bx.valid():
                        projected("soma", pe_soma, bx, wsoma, lambda k: x1t[bx.par][:, k, :], i)
                    if u == 10 and bt.valid():
                        wait(pe, o_ready, bt)
                        for t in range(NB):
                            side.wait_free(pe, f"on{t}", i)
                            for g in range(4):
                                last = tr(side.bank(f"on{t}")[:, blk(g)], o_t[:, g, blk(t)], ident[:, :])
                            last.then_inc(pe_on.sem, 1)
                    if u == 10 and bx.valid():
                        wait(pe, hid_ready, bx)
                        side.wait_free(pe, "mod", i)
                        mm(side.bank("mod")[:, 0:T], wn2[:, :], hid[:, :], start=True,
                           stop=True).then_inc(pe_mod.sem, 1)
                    if u == 12 and bx.valid():
                        flipped("x1n", pe_x1n, x1t[bx.par], i)
                    if u == 13 and bx.valid():
                        wait(pe, mod_ready, bx)
                        side.wait_free(pe, "modn", i)
                        passed_by(pe, pe_passed)
                        for t in range(NB):
                            last = tr(side.bank("modn")[:, D * t:D * t + D], mod[0:D, blk(t)], ident[0:D, 0:D])
                        last.then_inc(pe_modn.sem, 1)
                    if u == 14:
                        if bx.valid():
                            near(bx, 0, i)
                        if bt.valid():
                            wait(pe, attn_ready, bt)
                            flipped("at", pe_at, attn, i)
                    if u == 15 and bx.valid():
                        near(bx, 1, i)
                    if u == 16 and bt.valid():
                        wait(pe, attn_t_ready, bt)
                        projected("wo", pe_wo, bt, wo, lambda k: attn_t[:, k, :], i)
                    if u == 17 and bx.valid():
                        near(bx, 2, i)
                    if u == 18 and bx.valid():
                        wait(pe, state_in_ready, bx)
                        wait(pe, gated_n_ready, bx)
                        for n in range(2):
                            side.wait_free(pe, f"far{n}", i)
                            for a in range(2):
                                last = product(
                                    side.bank(f"far{n}")[:, 256 * a:256 * a + 256],
                                    lambda k: state_in[:, 8 * (2 * n + a + 2 * k):8 * (2 * n + a + 2 * k) + 8, :]
                                    .rearrange("p j d -> p (j d)"),
                                    lambda k: gated_n[:, k, :], range(n + 1))
                            last.then_inc(pe_far.sem, 1)
                    if u == 19 and bx.valid():
                        near(bx, 3, i)
                    if u == 20 and bm.valid():
                        wait(pe, neg_chain, bm)
                        side.wait_free(pe, "nm", i)
                        passed_by(pe, pe_passed)
                        for t in range(NB):
                            last = tr(side.bank("nm")[0:3 * H, P // 2 * t:P // 2 * t + P // 2].bitcast(BF16),
                                      neg_part[:, t, :, :].rearrange("p n h -> p (n h)"), ident_b[:, :])
                        last.then_inc(pe_nm.sem, 1)
                    if u == 21 and bx.valid():
                        wait(pe, states_ready, bx)
                        side.wait_free(pe, "y", i)
                        for t in range(NB):
                            for a in range(2):
                                last = mm(side.bank("y")[:, 256 * t:256 * t + 256], far_out[:, a, :],
                                          states[:, 2 * t + a, :], start=(a == 0), stop=(a == 1))
                        last.then_inc(pe_y.sem, 1)
                        near(bx, 4, i)
                    if u == 22 and bx.valid():
                        near(bx, 5, i)
                    if u == 23 and bp.valid():
                        projected("ks", pe_ks, bp, wk, lambda k: x2t[bp.par][:, k, :], i)
                    if u == 25:
                        if bx.valid():
                            near(bx, 6, i)
                        if bp.valid():
                            natural("vs", pe_vs, x2t[bp.par], wv, i)
                    if u == 27:
                        if bm.valid():
                            attend_values(bm, 0)
                        if bx.valid():
                            near(bx, 7, i)
                            wait(pe, far_n_ready, bx)
                            flipped("yt", pe_yt, far_n, i)
                    if u == 28 and bp.valid():
                        natural("vp", pe_vp, xt[bp.par], wv, i)
                    if u == 30 and bp.valid():
                        wait(pe, self_prod_ready, bp)
                        flipped("prn", pe_prn, self_prod, i)
                    if u == 31 and bm.valid():
                        attend_values(bm, 1)

            iterations(pe, body)

        def halves(bank):
            return bank[:, :].rearrange("p (n t) -> p n t", n=NB)

        def over_blocks(row):
            return row[:, :].unsqueeze(1).to_broadcast([P, NB, E])

        @block.scalar
        def _(act):
            fn = nc.scalar.activation
            done = [0]

            def mark(ins):
                done[0] += 1
                ins.then_inc(set_act, 1)

            act.wait_ge(set_dve, DVE_SP1)
            mark(fn(sp_u[:, :], sp_t[:, :], ACT.Exp))
            act.wait_ge(set_dve, DVE_SP2)
            mark(fn(sp_t[:, :], sp_u[:, :], ACT.Ln))
            act.wait_ge(set_dve, DVE_SP3)
            mark(fn(sp_u[:, 0:1], sp[:, D + 1:D + 2], ACT.Exp, scale=-1.0))
            mark(fn(pow_col[:, :], c_dist, ACT.Exp, scale=neg_sp[:, 0:1]))
            mark(fn(far_out[:, :, :], c_out_e, ACT.Exp, scale=neg_sp[:, 0:1]))
            act.wait_ge(set_dve, DVE_EXP)
            mark(fn(far_in[:, :, :], far_in[:, :, :], ACT.Exp, scale=-1.0))
            mark(fn(blend_t[:, :, :], blend_t[:, :, :], ACT.Exp))
            assert done[0] == ACT_DONE
            act.wait_ge(set_dve, DVE_DONE)

            def attend(b, h):
                wait(act, pe_score, b, h + 1)
                if h >= 8:
                    wait(act, pe_av, b, (h - 8) // 4 + 1)
                else:
                    wait(act, pe_av, b + -1, h // 4 + 3)
                fn(probs[:, h % 8, :, :], halves(score.bank(f"a{h}")), ACT.Exp).then_inc(probs_ready.sem, 1)

            def body(i):
                bp, bm, bt, bx, bz = i + 1, i, i + -1, i + -2, i + -3
                for u in range(STEPS):
                    if u < H - A_NOW and bt.valid():
                        attend(bt, A_NOW + u)
                    if u >= A_AT and bm.valid():
                        attend(bm, u - A_AT)
                    if u == 1 and bx.valid():
                        wait(act, pe_wg, bx)
                        for e in range(NB):
                            last = fn(gate_g[:, e, :], halves(side.bank("wg"))[:, e, :], ACT.Tanh,
                                      bias=half_b[:, e:e + 1], scale=0.5)
                        last.then_inc(gate_g_ready.sem, 1)
                    if u == 4 and bp.valid():
                        wait(act, pe_q, bp)
                        wait_dma(act, q_stacked, bp + -1, NQ)
                        for e in range(NB):
                            last = fn(qf[:, e, :], halves(side.bank("q"))[:, e, :], ACT.Identity,
                                      bias=bias_q[:, e:e + 1], scale=SCALE)
                        last.then_inc(q_ready.sem, 1)
                        wait(act, q_ready, bp)
                        fn(q_part[0][:, :, :], qf[:, :, :], ACT.Copy).then_inc(q_high.sem, 1)
                    if u == 6 and bx.valid():
                        wait(act, pe_gn, bx)
                        fn(gated_n[:, :, :], halves(side.bank("gn")), ACT.Copy).then_inc(gated_n_ready.sem, 1)
                    if u == 7 and bp.valid():
                        wait(act, pe_k, bp)
                        wait_dma(act, k_stacked, bp + -1, NK)
                        for e in range(NB):
                            last = fn(kf[:, e, :], halves(side.bank("k"))[:, e, :], ACT.Identity,
                                      bias=bias_kp[:, e:e + 1])
                        last.then_inc(k_ready.sem, 1)
                        wait(act, k_ready, bp)
                        fn(k_part[0][:, :, :], kf[:, :, :], ACT.Copy).then_inc(k_high.sem, 1)
                    if u == 8 and bp.valid():
                        wait(act, q_res_ready, bp)
                        fn(q_part[1][:, :, :], q_res[:, :, :], ACT.Copy).then_inc(q_mid.sem, 1)
                    if u == 8 and bx.valid():
                        wait(act, pe_h1, bx)
                        fn(hid[0:HID, :], side.bank("h1")[0:HID, 0:T], ACT.Gelu,
                           bias=col("bn1")[0:HID, :]).then_inc(hid_ready.sem, 1)
                    if u == 9 and bt.valid():
                        for n in range(2):
                            wait(act, pe_av, bt, 2 * n + 2)
                            fn(o_t[:, 2 * n:2 * n + 2, :], halves(o_psum[n]), ACT.Copy).then_inc(o_ready.sem, 1)
                    if u == 9 and bp.valid():
                        wait(act, k_res_ready, bp)
                        fn(k_part[1][:, :, :], k_res[:, :, :], ACT.Copy).then_inc(k_mid.sem, 1)
                    if u == 10 and bx.valid():
                        wait(act, pe_soma, bx)
                        wait(act, mixed_ready, bx + -1)
                        for e in range(NB):
                            last = fn(soma[:, e, :], halves(side.bank("soma"))[:, e, :], ACT.Gelu,
                                      bias=col("bsoma", e))
                        last.then_inc(soma_ready.sem, 1)
                    if u == 11 and bx.valid():
                        wait(act, pe_mod, bx)
                        fn(mod_th[:, :], side.bank("mod")[:, 0:T], ACT.Tanh, bias=half_b[:, 4:5],
                           scale=0.5).then_inc(mod_th_ready.sem, 1)
                    if u == 15 and bt.valid():
                        wait(act, pe_at, bt)
                        fn(attn_t[:, :, :], halves(side.bank("at")), ACT.Copy).then_inc(attn_t_ready.sem, 1)
                    if u == 22 and bx.valid():
                        wait(act, pe_y, bx)
                        fn(far_n[:, :, :], halves(side.bank("y")), ACT.Copy).then_inc(far_n_ready.sem, 1)
                    if u == 21 and bm.valid():
                        wait(act, pe_nm, bm)
                        wait_dma(act, max_stacked, bm + -1, NM)
                        fn(neg_t[:, :], side.bank("nm")[0:3 * H, 0:P].bitcast(BF16), ACT.Copy)\
                            .then_inc(neg_t_ready.sem, 1)
                        wait(act, neg_chain, bm, 3)
                        fn(self_p[:, :, :], self_diff[:, :, :], ACT.Exp).then_inc(self_p_ready.sem, 1)
                    if u == 3 and bz.valid():
                        wait(act, pe_gate, bz)
                        for e in range(NB):
                            last = fn(gate_t[:, e, :], halves(side.bank("gate"))[:, e, :], ACT.Tanh,
                                      bias=half_b[:, 2 + e:3 + e], scale=0.5)
                        last.then_inc(gate_t_ready.sem, 1)

            iterations(act, body)

        @block.vector
        def _(dve):
            v = nc.vector
            done = [0]

            def step(ins):
                done[0] += 1
                ins.then_inc(set_dve, 1)
                dve.wait_ge(set_dve, done[0])

            def at(mark):
                assert done[0] == mark, (done[0], mark)

            dve.wait_ge(loaded, 16 * len(loads))
            step(v.scalar_tensor_tensor(sp_t[:, :], taus[:, :], -1.0, taus[:, :], ALU.mult, ALU.min))
            at(DVE_SP1)
            dve.wait_ge(set_act, 1)
            step(v.tensor_scalar(sp_u[:, :], sp_u[:, :], 1.0, None, ALU.add))
            at(DVE_SP2)
            dve.wait_ge(set_act, 2)
            step(v.scalar_tensor_tensor(sp[:, :], taus[:, :], 0.0, sp_t[:, :], ALU.max, ALU.add))
            step(v.tensor_scalar(neg_sp[:, :], sp[:, D:D + 1], -1.0, None, ALU.mult))
            at(DVE_SP3)
            step(v.tensor_tensor(far_in[:, :, :], c_far_e, sp[:, 0:D].unsqueeze(1).to_broadcast([P, 6 * CH, D]),
                                 ALU.mult))
            step(v.reduce_max(blend_m[:, :], blend_t[:, :, :], AX.X))
            step(v.tensor_tensor(blend_t[:, :, :], blend_t[:, :, :],
                                 blend_m[:, :].unsqueeze(2).to_broadcast([P, NB, D]), ALU.subtract))
            at(DVE_EXP)
            dve.wait_ge(set_act, ACT_DONE)
            step(v.reduce_sum(blend_s[:, :], blend_t[:, :, :], AX.X))
            step(v.reciprocal(blend_s[:, :], blend_s[:, :]))
            step(v.tensor_scalar(blend_s[:, :], blend_s[:, :], 0.5, None, ALU.mult))
            step(v.tensor_tensor(blend_t[:, :, :], blend_t[:, :, :],
                                 blend_s[:, :].unsqueeze(2).to_broadcast([P, NB, D]), ALU.mult))
            step(v.tensor_copy(blend_8[:, :, :, :], blend_t[:, :, :].unsqueeze(2).to_broadcast([P, NB, 8, D])))
            at(DVE_BLEND)
            step(v.memset(decay[:, :], 0.0))
            step(v.tensor_scalar(decay[:, :], decay[:, :], sp_u[:, 0:1], None, ALU.add))
            step(v.tensor_tensor(far_out[:, :, :], far_out[:, :, :], c_out_m, ALU.mult))
            step(v.tensor_tensor(far_in[:, :, :], far_in[:, :, :], c_far_m, ALU.mult))
            step(v.tensor_scalar(wout[:, :, :], wout[:, :, :], 0.5, None, ALU.mult))
            step(v.tensor_copy(lens[:, :], lens_i[:, :]))
            step(v.tensor_scalar(mask_rows[:, :], iota_k[:, :], lens[:, 0:1], MASKED, ALU.is_ge, ALU.mult))
            at(DVE_MASK)
            step(v.tensor_scalar(half_b[:, 0:2], cols[:, 10:12], 0.5, None, ALU.mult))
            step(v.tensor_scalar(half_b[:, 2:4], cols[:, 14:16], 0.5, None, ALU.mult))
            step(v.tensor_scalar(half_b[:, 4:5], col("bn2"), 0.5, None, ALU.mult))
            dve.wait_ge(set_pe, 1)
            step(v.tensor_tensor(bias_q[:, :], side_psum[0][:, 0:2], cols[:, 0:2], ALU.add))
            step(v.tensor_scalar(bias_q[:, :], bias_q[:, :], SCALE, None, ALU.mult))
            step(v.tensor_tensor(bias_kp[:, :], side_psum[0][:, 2:4], cols[:, 2:4], ALU.add))
            step(v.tensor_tensor(bias_ks[:, :], side_psum[0][:, 4:6], cols[:, 2:4], ALU.add))
            dve.wait_ge(set_pe, 2)
            step(v.tensor_copy(blend[:, :], side_psum[1][:, 0:E]))
            for n in range(CH):
                step(v.tensor_scalar(near_f[:, n, :], blend[:, :], pow_col[:, n:n + 1], None, ALU.mult))
            step(v.tensor_copy(near_h[:, :, :], near_f[:, :, :]))
            step(v.tensor_tensor(near_r[:, :, :], near_f[:, :, :], near_h[:, :, :], ALU.subtract))
            step(v.tensor_copy(near_m[:, :, :], near_r[:, :, :]))
            step(v.tensor_tensor(near_r[:, :, :], near_r[:, :, :], near_m[:, :, :], ALU.subtract))
            step(v.tensor_scalar(near_f[:, :, :], near_h[:, :, :], c_slot[:, 0:1], None, ALU.mult))
            step(v.scalar_tensor_tensor(near_f[:, :, :], near_m[:, :, :], c_slot[:, 1:2], near_f[:, :, :],
                                        ALU.mult, ALU.add))
            step(v.scalar_tensor_tensor(near_w[:, :, :], near_r[:, :, :], c_slot[:, 2:3], near_f[:, :, :],
                                        ALU.mult, ALU.add))
            dve.wait_ge(set_pool, POOL_DONE)
            at(DVE_DONE - 1)
            step(v.memset(top[:, :, :], 0.0))
            at(DVE_DONE)

            def add_bias_v(dst, name, done_, b):
                v.tensor_tensor(dst, halves(side.bank(name)).rearrange("p n (h d) -> p n h d", d=DH),
                                over_blocks(bv_row).rearrange("p n (h d) -> p n h d", d=DH),
                                ALU.add).then_inc(done_.sem, 1)

            def near(b, n):
                wait(dve, pe_near, b, n + 1)
                if n == 0:
                    v.tensor_tensor(near_sum[:, :, :], gated[:, :, :], halves(side.bank("near0")),
                                    ALU.mult).then_inc(near_prod.sem, 1)
                    return
                if n >= 3:
                    wait(dve, near_added, b, n - 2)
                w = NB * NCH * (CH - n)
                v.tensor_tensor(near_p[n % 2][:, :, 0:CH - n],
                                gated[:, :, :].rearrange("p c (j r) -> p (c j) r", r=CH)[:, :, 0:CH - n],
                                side.bank(f"near{n}")[:, 0:w].rearrange("p (j r) -> p j r", r=CH - n),
                                ALU.mult).then_inc(near_prod.sem, 1)

            def body(i):
                bp, bm, bt, bx, bz = i + 1, i, i + -1, i + -2, i + -3
                for u in range(STEPS):
                    if M_AT <= u < M_AT + H and bm.valid():
                        h = u - M_AT
                        wait(dve, pe_max, bm, h + 1)
                        v.reduce_max(row_max[:, :, h], halves(score.bank(f"m{h}")), AX.X).then_inc(max_ready.sem, 1)
                    if u == 3 and bx.valid():
                        wait(dve, gate_g_ready, bx)
                        v.scalar_tensor_tensor(gated[:, :, :], gate_g[:, :, :], 1.0, x1t[bx.par][:, :, :],
                                               ALU.add, ALU.mult).then_inc(gated_ready.sem, 1)
                    if u == 24 and bp.valid():
                        wait(dve, pe_ks, bp)
                        wait(dve, q_ready, bp)
                        for e in range(NB):
                            last = v.scalar_tensor_tensor(self_prod[:, e, :], halves(side.bank("ks"))[:, e, :],
                                                          bias_ks[:, e:e + 1], qf[:, e, :], ALU.add, ALU.mult)
                        last.then_inc(self_prod_ready.sem, 1)
                    if u == 9 and bz.valid():
                        wait(dve, pe_out, bz)
                        for t in range(NB):
                            v.bn_stats(stats[:, t, :], halves(side.bank("out"))[:, t, :]).then_inc(norm_chain.sem, 1)
                        wait(dve, norm_chain, bz, 2)
                        passed_by(dve, dve_passed)
                        for t in range(NB):
                            v.bn_aggr(mean_var[:, t, :], stats[:, t, :]).then_inc(norm_chain.sem, 1)
                        wait(dve, norm_chain, bz, 4)
                        v.tensor_scalar(var_eps[:, :], mean_var[:, :, 1], EPS, None,
                                        ALU.add).then_inc(norm_chain.sem, 1)
                        for t in range(NB):
                            v.scalar_tensor_tensor(centred[:, t, :], halves(side.bank("out"))[:, t, :],
                                                   mean_var[:, t, 0:1], gamma_row[:, :], ALU.subtract,
                                                   ALU.mult).then_inc(norm_chain.sem, 1)
                    if u == 12 and bz.valid():
                        wait(dve, rstd_ready, bz)
                        wait(dve, norm_chain, bz)
                        wait(dve, x1_beta_ready, bz)
                        wait_dma(dve, stored, bz + -2, 16)
                        for t in range(NB):
                            last = v.scalar_tensor_tensor(result[bz.par][:, t, :], centred[:, t, :], rstd[:, t:t + 1],
                                                          x1_beta[:, t, :], ALU.mult, ALU.add)
                        last.then_inc(result_ready.sem, 1)
                    if u == 13 and bx.valid():
                        wait(dve, pe_x1n, bx)
                        wait(dve, result_ready, bx + -1)
                        v.tensor_tensor(x1_beta[:, :, :], halves(side.bank("x1n")), over_blocks(beta_row),
                                        ALU.add).then_inc(x1_beta_ready.sem, 1)
                    if u == 11 and bt.valid():
                        wait(dve, self_pv_ready, bt)
                        for t in range(NB):
                            wait(dve, pe_on, bt, t + 1)
                            o = side.bank(f"on{t}")[:, :].rearrange("p (h c) -> p h c", c=32)
                            v.tensor_tensor(num[:, t, :].rearrange("p (h d) -> p h d", d=DH), o[:, :, 0:DH],
                                            self_pv[:, t, :].rearrange("p (h d) -> p h d", d=DH),
                                            ALU.add).then_inc(num_chain.sem, 1)
                            v.tensor_tensor(den[:, t, :], o[:, :, DH], self_p[:, t, :],
                                            ALU.add).then_inc(num_chain.sem, 1)
                        wait(dve, num_chain, bt, 4)
                        v.reciprocal(rden[:, :, :], den[:, :, :]).then_inc(num_chain.sem, 1)
                    if u == 14 and bx.valid():
                        wait(dve, pe_modn, bx)
                        v.tensor_copy(mod_n[:, :, :], side.bank("modn")[:, 0:NB * D].rearrange(
                            "p (t d) -> p t d", d=D)).then_inc(mod_n_ready.sem, 1)
                    if u == 29 and bp.valid():
                        wait(dve, pe_vp, bp)
                        add_bias_v(v_ones[bp.par][:, :, :, 0:DH], "vp", v_ready, bp)
                    if u in NEAR_AT and bx.valid():
                        near(bx, NEAR_AT.index(u))
                    if u == 20 and bx.valid():
                        for n in range(2):
                            wait(dve, pe_far, bx, n + 1)
                            v.tensor_tensor(states[:, 2 * n:2 * n + 2, :], halves(side.bank(f"far{n}")),
                                            over_blocks(blend), ALU.mult).then_inc(states_ready.sem, 1)
                    if u == 17 and bt.valid():
                        wait(dve, pe_wo, bt)
                        wait_dma(dve, xe_in, bt, 16)
                        for c in range(NB):
                            last = v.scalar_tensor_tensor(x1t[bt.par][:, c, :], halves(side.bank("wo"))[:, c, :],
                                                          col("bo", c), xe[bt.par][:, c, :], ALU.add, ALU.add)
                        last.then_inc(x1_ready.sem, 1)
                    if u == 18 and bt.valid():
                        wait(dve, x1_ready, bt)
                        for c in range(NB):
                            last = v.tensor_tensor_scan(ctx_t[:, c, :], decay[:, :], x1t[bt.par][:, c, :], 0.0,
                                                        ALU.mult, ALU.add)
                        last.then_inc(ctx_ready.sem, 1)
                    if u == 19 and bm.valid():
                        wait(dve, max_ready, bm)
                        wait(dve, self_score_ready, bm)
                        v.tensor_tensor(top[:, :, :], row_max[:, :, :], self_score[bm.par][:, :, :],
                                        ALU.max).then_inc(neg_chain.sem, 1)
                        wait(dve, neg_chain, bm, 1)
                        v.tensor_scalar(neg_part[:, :, 0, :], top[:, :, :], -1.0, None,
                                        ALU.mult).then_inc(neg_chain.sem, 1)
                        v.tensor_tensor(self_diff[:, :, :], self_score[bm.par][:, :, :], top[:, :, :],
                                        ALU.subtract).then_inc(neg_chain.sem, 1)
                        wait(dve, neg_chain, bm, 3)
                        v.scalar_tensor_tensor(neg_res[:, :, :], top[:, :, :], -1.0, neg_part[:, :, 0, :],
                                               ALU.mult, ALU.subtract).then_inc(neg_chain.sem, 1)
                        wait(dve, neg_chain, bm, 4)
                        v.tensor_copy(neg_part[:, :, 1, :], neg_res[:, :, :]).then_inc(neg_chain.sem, 1)
                        wait(dve, neg_chain, bm, 5)
                        v.tensor_tensor(neg_part[:, :, 2, :], neg_res[:, :, :], neg_part[:, :, 1, :],
                                        ALU.subtract).then_inc(neg_chain.sem, 1)
                    if u == 30 and bx.valid():
                        wait(dve, pe_yt, bx)
                        wait(dve, near_added, bx)
                        v.tensor_tensor(temporal[:, :, :], near_sum[:, :, :], halves(side.bank("yt")),
                                        ALU.add).then_inc(temporal_ready.sem, 1)
                    if u == 26 and bp.valid():
                        wait(dve, pe_vs, bp)
                        add_bias_v(v_self[bp.par][:, :, :].rearrange("p n (h d) -> p n h d", d=DH), "vs",
                                   v_self_ready, bp)
                    if u == 4 and bz.valid():
                        wait(dve, gate_t_ready, bz)
                        wait(dve, soma_ready, bz)
                        v.scalar_tensor_tensor(mixed[:, :, :], gate_t[:, :, :], 1.0, soma[:, :, :],
                                               ALU.add, ALU.mult).then_inc(mixed_ready.sem, 1)
                    if u == 31 and bp.valid():
                        wait(dve, pe_prn, bp)
                        v.reduce_sum(self_score[bp.par][:, :, :].rearrange("p t (e h) -> p (t e) h", e=NB),
                                     side.bank("prn")[:, :].rearrange("p (x d h) -> p x h d", d=DH, h=8),
                                     AX.X).then_inc(self_score_ready.sem, 1)

            iterations(dve, body)

        @block.gpsimd
        def _(pool):
            g = nc.gpsimd
            done = [0]

            def step(ins):
                done[0] += 1
                ins.then_inc(set_pool, 1)
                pool.wait_ge(set_pool, done[0])

            step(g.memset(wn2[HID:P, :], 0.0))
            step(g.memset(hid[HID:P, :], 0.0))
            step(g.memset(minus_half[:, :], -0.5))
            for p in range(2):
                step(g.memset(v_ones[p][:, :, :, :], 0.0))
                step(g.memset(q_stack[p][KROWS:P, :, :], 1.0))
                step(g.memset(k_stack[p][KROWS:P, :, :], 1.0))
            for p in range(2):
                step(g.memset(v_ones[p][:, :, :, DH:DH + 1], 1.0))
            step(g.memset(mod_res[:, :], 0.0))
            pool.wait_ge(set_dve, DVE_DONE)
            assert done[0] == POOL_DONE

            def residual(dst, whole, part, done_, b):
                g.tensor_tensor(dst[:, :, :], whole[:, :, :], part[:, :, :], ALU.subtract).then_inc(done_.sem, 1)

            def near_add(b, n):
                wait(pool, near_prod, b, n + 1)
                if n > 1:
                    wait(pool, near_added, b, n - 1)
                rows = near_sum[:, :, :].rearrange("p c (j r) -> p (c j) r", r=CH)[:, :, n:CH]
                g.tensor_tensor(rows, rows, near_p[n % 2][:, :, 0:CH - n], ALU.add).then_inc(near_added.sem, 1)

            def body(i):
                bp, bm, bt, bx, bz = i + 1, i, i + -1, i + -2, i + -3
                for u in range(STEPS):
                    if u == 5 and bp.valid():
                        wait(pool, q_high, bp)
                        residual(q_res, qf, q_part[0], q_res_ready, bp)
                    if u == 8 and bp.valid():
                        wait(pool, k_high, bp)
                        residual(k_res, kf, k_part[0], k_res_ready, bp)
                    if u == 9 and bp.valid():
                        wait(pool, q_mid, bp)
                        wait(pool, q_res_ready, bp)
                        residual(q_part[2], q_res, q_part[1], q_low, bp)
                    if u == 10 and bp.valid():
                        wait(pool, k_mid, bp)
                        wait(pool, k_res_ready, bp)
                        residual(k_part[2], k_res, k_part[1], k_low, bp)
                    if u == 12 and bx.valid():
                        wait(pool, mod_th_ready, bx)
                        passed_by(pool, pool_passed)
                        g.tensor_scalar(mod[:, :], mod_th[:, :], 0.5, 1.0, ALU.mult, ALU.add)\
                            .then_inc(mod_ready.sem, 1)
                        wait(pool, mod_ready, bx)
                        passed_by(pool, pool_passed)
                        g.tensor_scalar(mod_stack[:, :], mod[:, :], 1.0, 0.0, ALU.mult, ALU.add)\
                            .then_inc(mod_chain.sem, 1)
                        wait(pool, mod_chain, bx, 1)
                        g.tensor_tensor(mod_res[96:P, :], mod[96:P, :], mod_stack[96:P, :], ALU.subtract)\
                            .then_inc(mod_chain.sem, 1)
                        wait(pool, mod_chain, bx, 2)
                        g.tensor_tensor(mod_stack[32:64, :], mod[32:64, :], mod_stack[32:64, :], ALU.subtract)\
                            .then_inc(mod_chain.sem, 1)
                        wait(pool, mod_chain, bx, 3)
                        passed_by(pool, pool_passed)
                        g.tensor_scalar(mod_mid[96:P, :], mod_res[96:P, :], 1.0, 0.0, ALU.mult, ALU.add)\
                            .then_inc(mod_chain.sem, 1)
                        wait(pool, mod_chain, bx, 4)
                        g.tensor_tensor(mod_stack[96:P, :], mod_res[96:P, :], mod_mid[96:P, :], ALU.subtract)\
                            .then_inc(mod_chain.sem, 1)
                        wait(pool, mod_chain, bx)
                    if u == 12 and bt.valid():
                        wait(pool, num_chain, bt)
                        heads = num[:, :, :].rearrange("p t (h d) -> p (t h) d", d=DH)
                        g.tensor_tensor(attn[:, :, :].rearrange("p t (h d) -> p (t h) d", d=DH), heads,
                                        rden[:, :, :].rearrange("p t h -> p (t h)").unsqueeze(2)
                                        .to_broadcast([P, NB * H, DH]), ALU.mult).then_inc(attn_ready.sem, 1)
                    if u == 15 and bx.valid():
                        wait(pool, mod_n_ready, bx)
                        for k, (lo, hi) in enumerate(((0, 4 * CH), (4 * CH, 6 * CH))):
                            last = g.tensor_tensor(state_in[:, lo:hi, :], far_in[:, lo:hi, :],
                                                   mod_n[:, k, :].unsqueeze(1).to_broadcast([P, hi - lo, D]), ALU.mult)
                        last.then_inc(state_in_ready.sem, 1)
                    if u in NEAR_AT[1:] and bx.valid():
                        near_add(bx, NEAR_AT.index(u))
                    if u == 24 and bm.valid():
                        wait(pool, self_p_ready, bm)
                        wait(pool, v_self_ready, bm)
                        g.tensor_tensor(self_pv[:, :, :].rearrange("p t (h d) -> p (t h) d", d=DH),
                                        v_self[bm.par][:, :, :].rearrange("p t (h d) -> p (t h) d", d=DH),
                                        self_p[:, :, :].rearrange("p t h -> p (t h)").unsqueeze(2)
                                        .to_broadcast([P, NB * H, DH]), ALU.mult).then_inc(self_pv_ready.sem, 1)
                    if u == 11 and bz.valid():
                        wait(pool, norm_chain, bz, 5)
                        g.tensor_tensor(rstd[:, :], var_eps[:, :], minus_half[:, :], ALU.pow)\
                            .then_inc(rstd_ready.sem, 1)

            iterations(pool, body)


def constants():
    far_e, far_m = np.zeros((P, 6, CH, 1), np.float32), np.zeros((P, 6, CH, 1), np.float32)
    for blk in range(6):
        i, k = (blk, 0) if blk < SB else (blk - 2, 1)
        start = CH * (CH * i + np.arange(CH))[None, :]
        e = start - 1 - (P * k + np.arange(P)[:, None])
        far_e[:, blk, :, 0], far_m[:, blk, :, 0] = np.maximum(e, 0), e >= 0
    far_e, far_m = (np.broadcast_to(a, (P, 6, CH, D)).reshape(P, -1) for a in (far_e, far_m))
    chunk = (np.arange(P) // D)[:, None]
    out_e, out_m = np.zeros((P, 2, P), np.float32), np.zeros((P, 2, P), np.float32)
    for a in range(2):
        e = np.arange(P)[None, :] - (P // 2 * a + CH * chunk) + 1
        inside = (e >= 1) & (e <= CH)
        out_e[:, a, :], out_m[:, a, :] = np.where(inside, e, 0), inside
    dist = np.broadcast_to(np.arange(CH, dtype=np.float32), (P, CH))
    slot = np.arange(P) // D
    slots = np.stack([np.isin(slot, s) for s in ((0, 2, 6), (1, 3), (4,))], 1)
    return np.concatenate([far_e, far_m, out_e.reshape(P, -1), out_m.reshape(P, -1), dist, slots], 1)\
        .astype(np.float32)


def kernel(**inputs):
    import concourse.bacc as bacc
    from concourse.bass_utils import run_bass_kernel_spmd
    a = {k: np.asarray(v) for k, v in inputs.items()}

    def blocks(w):
        return np.ascontiguousarray(w.reshape(-1, P, w.shape[1]).transpose(1, 0, 2))

    def column(v):
        return v.reshape(-1, P).T

    order = np.arange(E).reshape(NB, H // NB, DH).transpose(0, 2, 1).reshape(-1)
    row = {n: np.ascontiguousarray(np.broadcast_to(a[k], (P, E))) for n, k in
           (("bv", "L0_cond_bv"), ("gamma", "L1_cond_gamma"), ("beta", "L1_cond_beta"))}
    cols = np.zeros((P, 26), np.float32)
    for at, v in ((0, a["L0_cond_bq"][order]), (2, a["L0_cond_bk"][order]), (4, a["L0_cond_b_self"].reshape(-1)),
                  (6, a["L0_cond_b_prev"].reshape(-1)), (8, a["L0_cond_bo"]), (10, a["L1_cond_bg"]),
                  (12, a["L1_cond_bsoma"]), (14, a["L1_cond_btemp"])):
        cols[:, at:at + 2] = column(v)
    cols[0:HID, 16] = a["L1_cond_bn1"]
    cols[:, 17] = np.tile(a["condB_bn2"], P // D)
    tau = a["condB_tauraws"]
    taus = np.concatenate([np.broadcast_to(tau, (P, D)), np.tile(tau, P // D)[:, None],
                           np.broadcast_to(a["L1_cond_tau_ctx"], (P, 1))], 1)

    def rows_t(x):
        return np.ascontiguousarray(x.reshape(B, T, NB, P).transpose(0, 3, 2, 1))

    import ml_dtypes
    feeds = {
        "xt": rows_t(a["x"]), "x2t": rows_t(a["fside_BxSxS_0"]),
        "wq": blocks(a["L0_cond_Wq"][:, order]), "wk": blocks(a["L0_cond_Wk"][:, order]),
        "wv": blocks(a["L0_cond_Wv"]), "wo": blocks(a["L0_cond_Wo"]), "wg": blocks(a["L1_cond_Wg"].T),
        "wn1": blocks(a["L1_cond_Wn1"].T), "wn2": np.ascontiguousarray(np.tile(a["cond_256"].T, (1, P // D))),
        "wsoma": blocks(a["L1_cond_Wsoma"].T), "wtemp": blocks(a["L1_cond_Wtemp"].T),
        "wout": blocks(a["L1_cond_Wout"].T), "cols": cols, **row, "taus": np.ascontiguousarray(taus),
        "blend": blocks(a["cond_1024"].T), "consts": constants(), "ident": np.eye(P, dtype=np.float32),
        "ident_b": np.eye(P, dtype=ml_dtypes.bfloat16),
        "iota": np.ascontiguousarray(np.broadcast_to(np.arange(T, dtype=np.float32), (B, T))),
        "lens": np.ascontiguousarray(a["itok_B_18_1004"].reshape(B, 1)),
    }
    nc = bacc.Bacc("TRN2", target_bir_lowering=False, num_devices=1)
    d = {k: nc.dram_tensor(f"in_{k}", v.shape, mybir.dt.from_np(v.dtype), kind="ExternalInput").ap()
         for k, v in feeds.items()}
    d["mask"] = lambda rows, b: rows[b].unsqueeze(0).unsqueeze(1).to_broadcast([1, H, T])
    out = nc.dram_tensor("out", (B, P, NB, E), F32, kind="ExternalOutput").ap()
    build(nc, d, out)
    r = run_bass_kernel_spmd(nc, [{f"in_{k}": v for k, v in feeds.items()}], core_ids=[0])
    got = np.asarray(r.results[0]["out"])
    return np.ascontiguousarray(got.transpose(0, 2, 1, 3).reshape(B, T, E))
```

```python
from contextlib import ExitStack

import numpy as np

import concourse.bass as bass
from concourse import mybir

ALU = mybir.AluOpType
ACT = mybir.ActivationFunctionType
AX = mybir.AxisListType
F32 = mybir.dt.float32
BF16 = mybir.dt.bfloat16

P = 128
B, T, E, H = 16, 256, 256, 16
DH = E // H
NB = E // P
D = 16
HID = 64
CH = 8
NCH = T // CH
NEAR_AT = (5, 6, 8, 11, 13, 15, 16, 17)
SB = 4
SCALE = 1.0 / float(np.sqrt(DH))
EPS = 1e-5
MASKED = -1e30
KROWS = 96
PARTS = ((0, 0), (0, 1), (1, 0), (1, 1), (0, 2), (2, 0))

FIRST, LOOP_FIRST, PAIRS, LAST = -1, 5, (B - 1 - 5) // 2, B + 2
STEPS = 32
M_AT = 1
A_AT = 22
A_NOW = STEPS - A_AT


class Step:

    def __init__(self, k, c):
        self.k, self.c, self.par = k, c, c % 2

    def __add__(self, lag):
        return Step(self.k, self.c + lag)

    def number(self):
        return self.c if self.k is None else self.k * 2 + self.c

    def half(self):
        return self.c // 2 if self.k is None else self.k + self.c // 2

    def valid(self):
        return self.k is not None or 0 <= self.c < B

    def first(self):
        return self.before(FIRST + 1)

    def before(self, c):
        return self.k is None and self.c < c

    def is_number(self, c):
        return self.k is None and self.c == c


def iterations(eng, body, before):
    for c in range(FIRST, LOOP_FIRST):
        if c in before:
            before[c]()
        body(Step(None, c))
    with eng.Fori(0, PAIRS) as k:
        body(Step(k, LOOP_FIRST))
        body(Step(k, LOOP_FIRST + 1))
    for c in range(LOOP_FIRST + 2 * PAIRS, LAST + 1):
        body(Step(None, c))


class Signal:

    def __init__(self, sem, per=1):
        self.sem, self.per = sem, per

    def at(self, batch, nth=None):
        return batch.number() * self.per + (self.per if nth is None else nth)


def wait(eng, signal, batch, nth=None):
    if batch.k is None and batch.c < 0:
        return
    eng.wait_ge(signal.sem, signal.at(batch, nth))


def wait_dma(eng, pair, batch, per):
    if batch.k is None and batch.c < 0:
        return
    eng.wait_ge(pair[batch.par], batch.half() * per + per)


class Banks:

    def __init__(self, tiles, uses):
        self.tiles, self.uses = tiles, uses
        self.pos = {use[0]: n for n, use in enumerate(uses)}

    def bank(self, name):
        return self.tiles[self.pos[name] % len(self.tiles)]

    def wait_free(self, eng, name, i):
        at, n = self.pos[name], len(self.tiles)
        same = [q for q in range(len(self.uses)) if q % n == at % n]
        before = [(q, 0) for q in same if q < at]
        while True:
            if not before:
                i, before = i + -1, [(q, 0) for q in same]
                if i.k is None and i.c < FIRST:
                    return
            q = before.pop()[0]
            _, lag, signal, nth = self.uses[q]
            if (i + lag).valid():
                return wait(eng, signal, i + lag, nth)


DVE_BIAS, DVE_MASK, DVE_SP1, DVE_SP2, DVE_EXP, DVE_BLEND, DVE_DECAY, DVE_DONE = 4, 6, 7, 8, 13, 18, 26, 52
ACT_DONE, POOL_DONE = 7, 12


def build(nc, d, out):
    ctx = ExitStack()
    with ctx:
        def sb(name, shape, dt=F32):
            return ctx.enter_context(nc.sbuf_tensor(name, shape, dt))

        def two(name, shape, dt=F32):
            return [sb(f"{name}{p}", shape, dt) for p in range(2)]

        def psum(name, shape):
            return ctx.enter_context(nc.psum_tensor(name, shape, F32))

        def sem(name):
            return ctx.enter_context(nc.semaphore(name))

        def signal(name, per=1):
            return Signal(sem(name), per)

        wq, wk, wv, wo = (sb(n, [P, NB, E]) for n in ("wq", "wk", "wv", "wo"))
        wg = sb("wg", [P, 2 * NB, E])
        wn1 = sb("wn1", [P, NB, HID])
        wn2 = sb("wn2", [P, P])
        wsoma, wtemp, wout = (sb(n, [P, NB, E]) for n in ("wsoma", "wtemp", "wout"))
        cols = sb("cols", [P, 18 + D + 2])
        taus = cols[:, 18:18 + D + 2]
        bv_row = sb("bv_row", [P, E])
        gamma_beta = sb("gamma_beta", [P, 2, E])
        gamma_row, beta_row = gamma_beta[:, 0, :], gamma_beta[:, 1, :]
        ident = sb("ident", [P, P])
        ident_b = sb("ident_b", [P, P], BF16)
        bias_q, bias_kp, bias_ks = (sb(n, [P, NB]) for n in ("bias_q", "bias_kp", "bias_ks"))
        half_b = sb("half_b", [P, 5])
        sp, sp_t, sp_u = (sb(n, [P, D + 2]) for n in ("sp", "sp_t", "sp_u"))
        neg_sp = sb("neg_sp", [P, 1])
        decay = sb("decay", [P, T])
        far_in = sb("far_in", [P, 6 * CH, D])
        far_out = sb("far_out", [P, 2, P])
        pow_col = sb("pow_col", [P, CH])
        blend_t = sb("blend_t", [P, NB, D])
        blend_m, blend_s = sb("blend_m", [P, NB]), sb("blend_s", [P, NB])
        blend_8 = sb("blend_8", [P, NB, 8, D])
        blend = sb("blend", [P, E])
        near_w = sb("near_w", [P, CH, E], BF16)
        consts = sb("consts", [P, 2 * 6 * CH * D + 4 * P + CH + 3])
        iota_k, lens_i, lens = sb("iota_k", [B, T]), sb("lens_i", [B, 1], mybir.dt.int32), sb("lens", [B, 1])
        mask_rows = sb("mask_rows", [B, T], BF16)
        minus_half = sb("minus_half", [P, NB])
        mask_dram = nc.dram_tensor("mask_scratch", (B, T), BF16, kind="Internal").ap()

        nA = 6 * CH * D
        c_far_e = consts[:, 0:nA].rearrange("p (j d) -> p j d", d=D)
        c_far_m = consts[:, nA:2 * nA].rearrange("p (j d) -> p j d", d=D)
        c_out_e = consts[:, 2 * nA:2 * nA + 2 * P].rearrange("p (a t) -> p a t", a=2)
        c_out_m = consts[:, 2 * nA + 2 * P:2 * nA + 4 * P].rearrange("p (a t) -> p a t", a=2)
        c_dist = consts[:, 2 * nA + 4 * P:2 * nA + 4 * P + CH]
        c_slot = consts[:, 2 * nA + 4 * P + CH:2 * nA + 4 * P + CH + 3]

        def col(name, n=0):
            at = {"bq": 0, "bk": 2, "b_self": 4, "b_prev": 6, "bo": 8, "bg": 10, "bsoma": 12, "btemp": 14,
                  "bn1": 16, "bn2": 17}[name] + n
            return cols[:, at:at + 1]

        xt, x2t, xe = two("xt", [P, NB, T]), two("x2t", [P, NB, T]), two("xe", [P, NB, T])
        qf, kf = sb("qf", [P, NB, T]), sb("kf", [P, NB, T])
        q_res, k_res = sb("q_res", [P, NB, T]), sb("k_res", [P, NB, T])
        q_part = [sb(f"q_part{n}", [P, NB, T], BF16) for n in range(3)]
        k_part = [sb(f"k_part{n}", [P, NB, T], BF16) for n in range(3)]
        q_stack, k_stack = two("q_stack", [P, H, T], BF16), two("k_stack", [P, H, T], BF16)
        self_prod = sb("self_prod", [P, NB, T])
        self_score = two("self_score", [P, NB, H])
        v_ones = two("v_ones", [P, NB, H, 32])
        v_self = two("v_self", [P, NB, E])
        row_max, top, neg_res = sb("row_max", [P, NB, H]), sb("top", [P, NB, H]), sb("neg_res", [P, NB, H])
        neg_part = sb("neg_part", [P, NB, 3, H], BF16)
        neg_t = sb("neg_t", [3 * H, T], BF16)
        self_diff, self_p = sb("self_diff", [P, NB, H]), sb("self_p", [P, NB, H])
        self_pv = sb("self_pv", [P, NB, E])
        probs = sb("probs", [P, 8, NB, T])
        o_t = sb("o_t", [P, 4, T])
        den, rden = sb("den", [P, NB, H]), sb("rden", [P, NB, H])
        num, attn, attn_t = sb("num", [P, NB, E]), sb("attn", [P, NB, E]), sb("attn_t", [P, NB, T])
        x1t = two("x1t", [P, NB, T])
        ctx_t = sb("ctx_t", [P, NB, T])
        gate_g, gated, gated_n = sb("gate_g", [P, NB, T]), sb("gated", [P, NB, T]), sb("gated_n", [P, NB, E])
        hid = sb("hid", [P, T])
        mod, mod_res, mod_mid = sb("mod", [P, T]), sb("mod_res", [P, T]), sb("mod_mid", [P, T], BF16)
        mod_th = sb("mod_th", [P, T])
        mod_stack = sb("mod_stack", [P, T], BF16)
        mod_n = sb("mod_n", [P, NB, D])
        state_in = sb("state_in", [P, 6 * CH, D])
        states = sb("states", [P, SB, E])
        near_p = two("near_p", [P, NB * NCH, CH])
        near_sum = sb("near_sum", [P, NB, T])
        far_n = sb("far_n", [P, NB, E])
        temporal = sb("temporal", [P, NB, T])
        gate_t, soma, mixed = sb("gate_t", [P, NB, T]), sb("soma", [P, NB, T]), sb("mixed", [P, NB, T])
        x1_beta = sb("x1_beta", [P, NB, E])
        stats, mean_var = sb("stats", [P, NB, 6]), sb("mean_var", [P, NB, 2])
        var_eps, rstd = sb("var_eps", [P, NB]), sb("rstd", [P, NB])
        centred = sb("centred", [P, NB, E])
        result = two("result", [P, NB, E])

        near_f, near_r = gated, gate_g
        near_h, near_m = (t[:, 0, :].bitcast(BF16).rearrange("p (n c) -> p n c", n=2) for t in (near_sum, temporal))

        s_psum = [psum(f"s_psum{n}", [P, 512]) for n in range(2)]
        o_psum = [psum(f"o_psum{n}", [P, 512]) for n in range(2)]
        side_psum = [psum(f"side_psum{n}", [P, 512]) for n in range(4)]

        loaded_1st, loaded_2nd, loaded_3rd, loaded_4th = (sem("loaded_" + n) for n in ("1st", "2nd", "3rd", "4th"))
        set_dve, set_act, set_pe, set_pool = (sem(n) for n in ("set_dve", "set_act", "set_pe", "set_pool"))
        mask_stored = sem("mask_stored")
        pe_passed, dve_passed, pool_passed, sp_passed = (sem(n + "_passed") for n in ("pe", "dve", "pool", "sp"))
        x_in = [sem(f"x_in{p}") for p in range(2)]
        xe_in = [sem(f"xe_in{p}") for p in range(2)]
        q_stacked = [sem(f"q_stacked{p}") for p in range(2)]
        k_stacked = [sem(f"k_stacked{p}") for p in range(2)]
        max_stacked = [sem(f"max_stacked{p}") for p in range(2)]
        stored = [sem(f"stored{p}") for p in range(2)]
        NQ, NK, NM, NX = 16 * 2 * len(PARTS), 16 * (2 * len(PARTS) + 1), 16 * 3, 16 * 2
        pe_wg, pe_q, pe_k, pe_ks, pe_vp, pe_vs, pe_prn, pe_gn, pe_h1, pe_soma, pe_x1n, pe_mod, pe_modn, pe_at, \
            pe_wo, pe_y, pe_yt, pe_nm, pe_gate, pe_out = (signal("pe_" + n) for n in (
                "wg", "q", "k", "ks", "vp", "vs", "prn", "gn", "h1", "soma", "x1n", "mod", "modn", "at", "wo",
                "y", "yt", "nm", "gate", "out"))
        pe_on, pe_far, pe_near = signal("pe_on", 2), signal("pe_far", 2), signal("pe_near", CH)
        pe_max, pe_score, pe_av = signal("pe_max", H), signal("pe_score", H), signal("pe_av", 4)
        q_ready, k_ready = signal("q_ready"), signal("k_ready")
        q_high, k_high, q_mid, k_mid = (signal(n) for n in ("q_high", "k_high", "q_mid", "k_mid"))
        probs_ready, o_ready, attn_t_ready = signal("probs_ready", H), signal("o_ready", 2), signal("attn_t_ready")
        gate_g_ready, hid_ready, mod_th_ready, gated_n_ready, far_n_ready, gate_t_ready, soma_ready, neg_t_ready, \
            self_p_ready = (signal(n + "_ready") for n in (
                "gate_g", "hid", "mod_th", "gated_n", "far_n", "gate_t", "soma", "neg_t", "self_p"))
        max_ready = signal("max_ready", H)
        neg_chain = signal("neg_chain", 6)
        gated_ready, self_prod_ready, self_score_ready, v_ready, v_self_ready, mod_n_ready, x1_ready, ctx_ready, \
            temporal_ready, mixed_ready, x1_beta_ready, result_ready = (signal(n + "_ready") for n in (
                "gated", "self_prod", "self_score", "v", "v_self", "mod_n", "x1", "ctx", "temporal", "mixed",
                "x1_beta", "result"))
        states_ready = signal("states_ready", 2)
        num_chain = signal("num_chain", 5)
        near_prod = signal("near_prod", CH)
        norm_chain = signal("norm_chain", 7)
        q_res_ready, k_res_ready, q_low, k_low, mod_ready, state_in_ready, attn_ready, self_pv_ready, rstd_ready = (
            signal(n) for n in ("q_res_ready", "k_res_ready", "q_low", "k_low", "mod_ready", "state_in_ready",
                                "attn_ready", "self_pv_ready", "rstd_ready"))
        mod_chain = signal("mod_chain", 5)
        near_added = signal("near_added", CH - 1)

        side = Banks(side_psum, [
            ("wg", -2, gate_g_ready, 1), ("q", 1, q_ready, 1), ("k", 1, k_ready, 1), ("gn", -2, gated_n_ready, 1),
            ("x1n", -2, x1_beta_ready, 1), ("near0", -2, near_prod, 1), ("ks", 1, self_prod_ready, 1),
            ("near1", -2, near_prod, 2), ("near2", -2, near_prod, 3), ("on0", -1, num_chain, 2),
            ("on1", -1, num_chain, 4), ("far0", -2, states_ready, 1), ("far1", -2, states_ready, 2),
            ("near3", -2, near_prod, 4), ("at", -1, attn_t_ready, 1), ("y", -2, far_n_ready, 1),
            ("near4", -2, near_prod, 5), ("wo", -1, x1_ready, 1), ("near5", -2, near_prod, 6),
            ("vs", 1, v_self_ready, 1), ("near6", -2, near_prod, 7), ("h1", -1, hid_ready, 1),
            ("near7", -2, near_prod, 8), ("vp", 1, v_ready, 1), ("yt", -2, temporal_ready, 1),
            ("mod", -1, mod_th_ready, 1), ("nm", 0, neg_t_ready, 1), ("soma", -2, soma_ready, 1),
            ("gate", -2, gate_t_ready, 1), ("modn", -1, mod_n_ready, 1), ("prn", 1, self_score_ready, 1),
            ("out", -2, norm_chain, 7)])
        score_uses = []
        for u in range(STEPS):
            if u < H - A_NOW:
                score_uses.append((f"a{A_NOW + u}", -1, probs_ready, A_NOW + u + 1))
            if M_AT <= u < M_AT + H:
                score_uses.append((f"m{u - M_AT}", 0, max_ready, u - M_AT + 1))
            if u >= A_AT:
                score_uses.append((f"a{u - A_AT}", 0, probs_ready, u - A_AT + 1))
        score = Banks(s_psum, score_uses)

        block = ctx.enter_context(nc.Block())
        loads_1st = [(cols[:, :], d["cols"]), (wq[:, :, :], d["wq"]), (wk[:, :, :], d["wk"])]
        loads_2nd = [(iota_k[:, :], d["iota"]), (lens_i[:, :], d["lens"]), (wv[:, :, :], d["wv"]),
                     (bv_row[:, :], d["bv"]), (ident[:, :], d["ident"])]
        loads_3rd = [(blend_t[:, :, :], d["blend"]), (consts[:, :], d["consts"]), (ident_b[:, :], d["ident_b"])]
        loads_4th = [(wo[:, :, :], d["wo"]), (wn1[:, :, :], d["wn1"]), (wn2[0:HID, :], d["wn2"]),
                     (wg[:, :, :], d["wg"]), (wsoma[:, :, :], d["wsoma"]), (wtemp[:, :, :], d["wtemp"]),
                     (wout[:, :, :], d["wout"]), (gamma_beta[:, :, :], d["gamma_beta"])]
        LOADED_1ST, LOADED_2ND, LOADED_3RD, LOADED_4TH = (16 * len(l) for l in (loads_1st, loads_2nd, loads_3rd,
                                                                                loads_4th))

        def passed_by(eng, count):
            eng.sem_inc(count, 1)

        @block.sync
        def _(sp_eng):
            def load_x(b):
                sp_eng.dma_start(x2t[b.par][:, :, :], d["x2t"][b.number()]).then_inc(x_in[b.par], 16)
                sp_eng.dma_start(xt[b.par][:, :, :], d["xt"][b.number()]).then_inc(x_in[b.par], 16)

            def load_rest():
                for dst, src in loads_4th:
                    sp_eng.dma_start(dst, src).then_inc(loaded_4th, 16)

            for dst, src in loads_1st:
                sp_eng.dma_start(dst, src).then_inc(loaded_1st, 16)
            load_x(Step(None, 0))
            for dst, src in loads_2nd:
                sp_eng.dma_start(dst, src).then_inc(loaded_2nd, 16)
            for dst, src in loads_3rd:
                sp_eng.dma_start(dst, src).then_inc(loaded_3rd, 16)
            load_x(Step(None, 1))
            sp_eng.wait_ge(set_dve, DVE_MASK)
            sp_eng.dma_start(mask_dram, mask_rows[:, :]).then_inc(mask_stored, 16)

            def body(i):
                b = i + 1
                if b.valid() and not i.before(1):
                    for s in (pe_vp, pe_vs):
                        wait(sp_eng, s, b + -2)
                    passed_by(sp_eng, sp_passed)
                    load_x(b)
                b = i
                if b.valid():
                    wait(sp_eng, x1_ready, b + -2)
                    passed_by(sp_eng, sp_passed)
                    sp_eng.dma_start(xe[b.par][:, :, :], d["xt"][b.number()]).then_inc(xe_in[b.par], 16)
                b = i + 1
                if b.valid():
                    wait(sp_eng, pe_score, b + -2)
                    passed_by(sp_eng, sp_passed)
                    for part, stack, ready, dsem, side_of in ((q_part, q_stack, (q_high, q_mid, q_low), q_stacked, 0),
                                                              (k_part, k_stack, (k_high, k_mid, k_low), k_stacked, 1)):
                        for n in range(3):
                            wait(sp_eng, ready[n], b)
                            for row, pair in enumerate(PARTS):
                                if pair[side_of] != n:
                                    continue
                                for e in range(NB):
                                    sp_eng.dma_start(stack[b.par][16 * row:16 * row + 16, 8 * e:8 * e + 8, :],
                                                     part[n][:, e, :]).then_inc(dsem[b.par], 16)
                    if i.first():
                        sp_eng.wait_ge(mask_stored, 16)
                    sp_eng.dma_start(k_stack[b.par][KROWS:KROWS + 1, :, :],
                                     d["mask"](mask_dram, b.number())).then_inc(k_stacked[b.par], 16)
                b = i + -3
                if b.valid():
                    wait(sp_eng, result_ready, b)
                    passed_by(sp_eng, sp_passed)
                    sp_eng.dma_start(out[b.number()], result[b.par][:, :, :]).then_inc(stored[b.par], 16)
                b = i
                if b.valid():
                    wait(sp_eng, neg_t_ready, b)
                    for n in range(3):
                        sp_eng.dma_start(q_stack[b.par][KROWS + 1 + n:KROWS + 2 + n, :, :],
                                         neg_t[16 * n:16 * n + 16, :]).then_inc(max_stacked[b.par], 16)

            iterations(sp_eng, body, {0: load_rest})
            for p in range(2):
                sp_eng.wait_ge(stored[p], 16 * (B // 2))

        @block.tensor
        def _(pe):
            mm, tr = nc.tensor.matmul, nc.tensor.transpose

            def product(dst, lhs, rhs, kbs, start=True):
                for k in kbs:
                    last = mm(dst, lhs(k), rhs(k), start=(k == kbs[0]), stop=(k == kbs[-1]))
                return last

            def blk(n):
                return slice(P * n, P * n + P)

            pe.wait_ge(loaded_1st, LOADED_1ST)
            for n, (w, c) in enumerate(((wq, "b_self"), (wk, "b_prev"), (wk, "b_self"))):
                for e in range(NB):
                    last = product(o_psum[0][:, 2 * n + e:2 * n + e + 1], lambda k: w[:, k, blk(e)],
                                   lambda k: col(c, k), (0, 1))
            last.then_inc(set_pe, 1)

            def blend_by_trace():
                pe.wait_ge(set_dve, DVE_BLEND)
                for e in range(NB):
                    last = tr(o_psum[1][:, blk(e)], blend_8[:, e, :, :].rearrange("p r d -> p (r d)"), ident[:, :])
                last.then_inc(set_pe, 1)
                pe.wait_ge(set_pool, POOL_DONE)
                pe.wait_ge(loaded_3rd, LOADED_3RD)

            def decays_ready():
                pe.wait_ge(set_dve, DVE_DECAY)
                pe.wait_ge(loaded_4th, LOADED_4TH)

            def near_weights_ready():
                pe.wait_ge(set_dve, DVE_DONE)
                pe.wait_ge(set_act, ACT_DONE)

            def projected(name, done, b, weights, rows, i):
                side.wait_free(pe, name, i)
                ps = side.bank(name)
                for e in range(NB):
                    last = product(ps[:, 256 * e:256 * e + 256], lambda k: weights[:, k, blk(e)],
                                   rows, range(NB))
                last.then_inc(done.sem, 1)

            def natural(name, done, rows, weights, i):
                side.wait_free(pe, name, i)
                ps = side.bank(name)
                for t in range(NB):
                    last = product(ps[:, 256 * t:256 * t + 256], lambda k: rows[:, k, blk(t)],
                                   lambda k: weights[:, k, :], (0, 1))
                last.then_inc(done.sem, 1)

            def flipped(name, done, src, i):
                side.wait_free(pe, name, i)
                ps = side.bank(name)
                for a in range(NB):
                    for c in range(NB):
                        last = tr(ps[:, 256 * a + P * c:256 * a + P * c + P], src[:, c, blk(a)], ident[:, :])
                last.then_inc(done.sem, 1)

            def max_scores(b, h, i):
                if h == 0:
                    wait_dma(pe, q_stacked, b, NQ)
                    wait_dma(pe, k_stacked, b, NK)
                score.wait_free(pe, f"m{h}", i)
                ps = score.bank(f"m{h}")
                for t in range(NB):
                    last = mm(ps[:, 256 * t:256 * t + 256], q_stack[b.par][0:KROWS + 1, h, blk(t)],
                              k_stack[b.par][0:KROWS + 1, h, :], start=True, stop=True)
                last.then_inc(pe_max.sem, 1)

            def attend_scores(b, h, i):
                if h == 0:
                    wait_dma(pe, max_stacked, b, NM)
                score.wait_free(pe, f"a{h}", i)
                ps = score.bank(f"a{h}")
                for k in range(NB):
                    last = mm(ps[:, 256 * k:256 * k + 256], k_stack[b.par][0:KROWS + 4, h, blk(k)],
                              q_stack[b.par][0:KROWS + 4, h, :], start=True, stop=True)
                last.then_inc(pe_score.sem, 1)

            def attend_values(b, g):
                wait(pe, probs_ready, b, 4 * g + 4)
                if g == 0:
                    wait(pe, v_ready, b)
                if g % 2 == 0:
                    wait(pe, o_ready, b + -1, g // 2 + 1)
                for k in range(NB):
                    for j in range(4):
                        h = 4 * g + j
                        last = mm(o_psum[g // 2][32 * j:32 * j + 32, 256 * (g % 2):256 * (g % 2) + 256],
                                  v_ones[b.par][:, k, h, :], probs[:, h % 8, k, :], start=(k == 0), stop=(k == NB - 1))
                last.then_inc(pe_av.sem, 1)

            def near(b, n, i):
                if n == 0:
                    wait(pe, mod_chain, b)
                side.wait_free(pe, f"near{n}", i)
                w = NCH * (CH - n)
                rhs = mod_stack[:, :].rearrange("p (j r) -> p j r", r=CH)[:, :, 0:CH - n]
                for c in range(NB):
                    last = mm(side.bank(f"near{n}")[:, w * c:w * c + w], near_w[:, n, blk(c)], rhs, start=True, stop=True)
                last.then_inc(pe_near.sem, 1)

            def body(i):
                bp, bm, bt, bx, bz = i + 1, i, i + -1, i + -2, i + -3
                for u in range(STEPS):
                    if u < H - A_NOW and bt.valid():
                        attend_scores(bt, A_NOW + u, i)
                    if M_AT <= u < M_AT + H and bm.valid():
                        max_scores(bm, u - M_AT, i)
                    if u >= A_AT and bm.valid():
                        attend_scores(bm, u - A_AT, i)
                    if u in (0, 1) and bx.valid():
                        if u == 0:
                            wait(pe, ctx_ready, bx)
                            side.wait_free(pe, "wg", i)
                        last = product(side.bank("wg")[:, 256 * u:256 * u + 256], lambda k: wg[:, k, blk(u)],
                                       lambda k: x1t[bx.par][:, k, :] if k < NB else ctx_t[:, k - NB, :],
                                       range(2 * NB))
                        if u == 1:
                            last.then_inc(pe_wg.sem, 1)
                    if u == 2 and bp.valid():
                        wait_dma(pe, x_in, bp, NX)
                        projected("q", pe_q, bp, wq, lambda k: x2t[bp.par][:, k, :], i)
                    if u == 3 and bt.valid():
                        attend_values(bt, 2)
                    if u == 4 and bp.valid():
                        projected("k", pe_k, bp, wk, lambda k: xt[bp.par][:, k, :], i)
                    if u == 4 and bx.valid():
                        wait(pe, gated_ready, bx)
                        flipped("gn", pe_gn, gated, i)
                    if u == 5 and bx.valid():
                        flipped("x1n", pe_x1n, x1t[bx.par], i)
                    if u == 6 and bp.valid():
                        if i.first():
                            pe.wait_ge(loaded_2nd, LOADED_2ND)
                        projected("ks", pe_ks, bp, wk, lambda k: x2t[bp.par][:, k, :], i)
                    if u == 7 and bt.valid():
                        attend_values(bt, 3)
                    if u == 9 and bt.valid():
                        wait(pe, o_ready, bt)
                        for t in range(NB):
                            side.wait_free(pe, f"on{t}", i)
                            for g in range(4):
                                last = tr(side.bank(f"on{t}")[:, blk(g)], o_t[:, g, blk(t)], ident[:, :])
                            last.then_inc(pe_on.sem, 1)
                    if u == 10 and bx.valid():
                        wait(pe, state_in_ready, bx)
                        wait(pe, gated_n_ready, bx)
                        for n in range(2):
                            side.wait_free(pe, f"far{n}", i)
                            for a in range(2):
                                last = product(
                                    side.bank(f"far{n}")[:, 256 * a:256 * a + 256],
                                    lambda k: state_in[:, 8 * (2 * n + a + 2 * k):8 * (2 * n + a + 2 * k) + 8, :]
                                    .rearrange("p j d -> p (j d)"),
                                    lambda k: gated_n[:, k, :], range(n + 1))
                            last.then_inc(pe_far.sem, 1)
                    if u in NEAR_AT and bx.valid():
                        near(bx, NEAR_AT.index(u), i)
                    if u == 11 and bt.valid():
                        wait(pe, attn_ready, bt)
                        flipped("at", pe_at, attn, i)
                    if u == 12 and bx.valid():
                        wait(pe, states_ready, bx)
                        side.wait_free(pe, "y", i)
                        for t in range(NB):
                            for a in range(2):
                                last = mm(side.bank("y")[:, 256 * t:256 * t + 256], far_out[:, a, :],
                                          states[:, 2 * t + a, :], start=(a == 0), stop=(a == 1))
                        last.then_inc(pe_y.sem, 1)
                    if u == 14 and bt.valid():
                        wait(pe, attn_t_ready, bt)
                        projected("wo", pe_wo, bt, wo, lambda k: attn_t[:, k, :], i)
                    if u == 15 and bp.valid():
                        natural("vs", pe_vs, x2t[bp.par], wv, i)
                    if u == 16 and bt.valid():
                        wait(pe, x1_ready, bt)
                        side.wait_free(pe, "h1", i)
                        product(side.bank("h1")[0:HID, 0:T], lambda k: wn1[:, k, :],
                                lambda k: x1t[bt.par][:, k, :], (0, 1)).then_inc(pe_h1.sem, 1)
                    if u == 17 and bp.valid():
                        natural("vp", pe_vp, xt[bp.par], wv, i)
                    if u == 17 and bx.valid():
                        wait(pe, far_n_ready, bx)
                        flipped("yt", pe_yt, far_n, i)
                    if u == 18 and bt.valid():
                        wait(pe, hid_ready, bt)
                        side.wait_free(pe, "mod", i)
                        mm(side.bank("mod")[:, 0:T], wn2[:, :], hid[:, :], start=True,
                           stop=True).then_inc(pe_mod.sem, 1)
                    if u == 19 and bm.valid():
                        wait(pe, neg_chain, bm)
                        side.wait_free(pe, "nm", i)
                        passed_by(pe, pe_passed)
                        for t in range(NB):
                            last = tr(side.bank("nm")[0:3 * H, P // 2 * t:P // 2 * t + P // 2].bitcast(BF16),
                                      neg_part[:, t, :, :].rearrange("p n h -> p (n h)"), ident_b[:, :])
                        last.then_inc(pe_nm.sem, 1)
                    if u == 20 and bx.valid():
                        projected("soma", pe_soma, bx, wsoma, lambda k: x1t[bx.par][:, k, :], i)
                    if u == 21 and bx.valid():
                        wait(pe, temporal_ready, bx)
                        projected("gate", pe_gate, bx, wtemp, lambda k: temporal[:, k, :], i)
                    if u == 24 and bt.valid():
                        wait(pe, mod_ready, bt)
                        side.wait_free(pe, "modn", i)
                        passed_by(pe, pe_passed)
                        for t in range(NB):
                            last = tr(side.bank("modn")[:, D * t:D * t + D], mod[0:D, blk(t)], ident[0:D, 0:D])
                        last.then_inc(pe_modn.sem, 1)
                    if u == 25 and bp.valid():
                        wait(pe, self_prod_ready, bp)
                        flipped("prn", pe_prn, self_prod, i)
                    if u == 27 and bm.valid():
                        attend_values(bm, 0)
                    if u == 28 and bx.valid():
                        wait(pe, mixed_ready, bx)
                        natural("out", pe_out, mixed, wout, i)
                    if u == 31 and bm.valid():
                        attend_values(bm, 1)

            iterations(pe, body, {0: blend_by_trace, 1: decays_ready, 2: near_weights_ready})

        def halves(bank):
            return bank[:, :].rearrange("p (n t) -> p n t", n=NB)

        def over_blocks(row):
            return row[:, :].unsqueeze(1).to_broadcast([P, NB, E])

        @block.scalar
        def _(act):
            fn = nc.scalar.activation
            done = [0]

            def mark(ins):
                done[0] += 1
                ins.then_inc(set_act, 1)

            def decays():
                act.wait_ge(set_dve, DVE_SP1)
                mark(fn(sp_u[:, :], sp_t[:, :], ACT.Exp))
                act.wait_ge(set_dve, DVE_SP2)
                mark(fn(sp_t[:, :], sp_u[:, :], ACT.Ln))
                act.wait_ge(set_dve, DVE_EXP)
                mark(fn(sp_u[:, 0:1], sp[:, D + 1:D + 2], ACT.Exp, scale=-1.0))
                mark(fn(pow_col[:, :], c_dist, ACT.Exp, scale=neg_sp[:, 0:1]))
                mark(fn(far_out[:, :, :], c_out_e, ACT.Exp, scale=neg_sp[:, 0:1]))
                mark(fn(far_in[:, :, :], far_in[:, :, :], ACT.Exp, scale=-1.0))
                mark(fn(blend_t[:, :, :], blend_t[:, :, :], ACT.Exp))
                assert done[0] == ACT_DONE

            def near_weights_made():
                act.wait_ge(set_dve, DVE_DONE)

            act.wait_ge(set_dve, DVE_BIAS)

            def attend(b, h):
                wait(act, pe_score, b, h + 1)
                if h >= 8:
                    wait(act, pe_av, b, (h - 8) // 4 + 1)
                else:
                    wait(act, pe_av, b + -1, h // 4 + 3)
                fn(probs[:, h % 8, :, :], halves(score.bank(f"a{h}")), ACT.Exp).then_inc(probs_ready.sem, 1)

            def body(i):
                bp, bm, bt, bx, bz = i + 1, i, i + -1, i + -2, i + -3
                for u in range(STEPS):
                    if u < H - A_NOW and bt.valid():
                        attend(bt, A_NOW + u)
                    if u >= A_AT and bm.valid():
                        attend(bm, u - A_AT)
                    if u == 2 and bx.valid():
                        wait(act, pe_wg, bx)
                        for e in range(NB):
                            last = fn(gate_g[:, e, :], halves(side.bank("wg"))[:, e, :], ACT.Tanh,
                                      bias=half_b[:, e:e + 1], scale=0.5)
                        last.then_inc(gate_g_ready.sem, 1)
                    if u == 3 and bp.valid():
                        wait(act, pe_q, bp)
                        wait_dma(act, q_stacked, bp + -1, NQ)
                        for e in range(NB):
                            last = fn(qf[:, e, :], halves(side.bank("q"))[:, e, :], ACT.Identity,
                                      bias=bias_q[:, e:e + 1], scale=SCALE)
                        last.then_inc(q_ready.sem, 1)
                        wait(act, q_ready, bp)
                        fn(q_part[0][:, :, :], qf[:, :, :], ACT.Copy).then_inc(q_high.sem, 1)
                    if u == 5 and bp.valid():
                        wait(act, pe_k, bp)
                        wait_dma(act, k_stacked, bp + -1, NK)
                        for e in range(NB):
                            last = fn(kf[:, e, :], halves(side.bank("k"))[:, e, :], ACT.Identity,
                                      bias=bias_kp[:, e:e + 1])
                        last.then_inc(k_ready.sem, 1)
                        wait(act, k_ready, bp)
                        fn(k_part[0][:, :, :], kf[:, :, :], ACT.Copy).then_inc(k_high.sem, 1)
                    if u == 5 and bx.valid():
                        wait(act, pe_gn, bx)
                        fn(gated_n[:, :, :], halves(side.bank("gn")), ACT.Copy).then_inc(gated_n_ready.sem, 1)
                    if u == 5 and bp.valid():
                        wait(act, q_res_ready, bp)
                        fn(q_part[1][:, :, :], q_res[:, :, :], ACT.Copy).then_inc(q_mid.sem, 1)
                    if u == 17 and bt.valid():
                        wait(act, pe_h1, bt)
                        fn(hid[0:HID, :], side.bank("h1")[0:HID, 0:T], ACT.Gelu,
                           bias=col("bn1")[0:HID, :]).then_inc(hid_ready.sem, 1)
                    if u in (1, 8) and bt.valid():
                        n = u // 8
                        wait(act, pe_av, bt, 2 * n + 2)
                        if n == 0:
                            wait(act, pe_on, bt + -1)
                        fn(o_t[:, 2 * n:2 * n + 2, :], halves(o_psum[n]), ACT.Copy).then_inc(o_ready.sem, 1)
                    if u == 21 and bx.valid():
                        wait(act, pe_soma, bx)
                        wait(act, mixed_ready, bx + -1)
                        for e in range(NB):
                            last = fn(soma[:, e, :], halves(side.bank("soma"))[:, e, :], ACT.Gelu,
                                      bias=col("bsoma", e))
                        last.then_inc(soma_ready.sem, 1)
                    if u == 19 and bt.valid():
                        wait(act, pe_mod, bt)
                        fn(mod_th[:, :], side.bank("mod")[:, 0:T], ACT.Tanh, bias=half_b[:, 4:5],
                           scale=0.5).then_inc(mod_th_ready.sem, 1)
                    if u == 10 and bp.valid():
                        wait(act, k_res_ready, bp)
                        fn(k_part[1][:, :, :], k_res[:, :, :], ACT.Copy).then_inc(k_mid.sem, 1)
                    if u == 12 and bt.valid():
                        wait(act, pe_at, bt)
                        fn(attn_t[:, :, :], halves(side.bank("at")), ACT.Copy).then_inc(attn_t_ready.sem, 1)
                    if u == 13 and bx.valid():
                        wait(act, pe_y, bx)
                        fn(far_n[:, :, :], halves(side.bank("y")), ACT.Copy).then_inc(far_n_ready.sem, 1)
                    if u == 20 and bm.valid():
                        wait(act, pe_nm, bm)
                        wait_dma(act, max_stacked, bm + -1, NM)
                        fn(neg_t[:, :], side.bank("nm")[0:3 * H, 0:P].bitcast(BF16), ACT.Copy)\
                            .then_inc(neg_t_ready.sem, 1)
                        wait(act, neg_chain, bm, 3)
                        fn(self_p[:, :, :], self_diff[:, :, :], ACT.Exp).then_inc(self_p_ready.sem, 1)
                    if u == 22 and bx.valid():
                        wait(act, pe_gate, bx)
                        for e in range(NB):
                            last = fn(gate_t[:, e, :], halves(side.bank("gate"))[:, e, :], ACT.Tanh,
                                      bias=half_b[:, 2 + e:3 + e], scale=0.5)
                        last.then_inc(gate_t_ready.sem, 1)

            iterations(act, body, {0: decays, 2: near_weights_made})

        @block.vector
        def _(dve):
            v = nc.vector
            done = [0]

            def step(ins):
                done[0] += 1
                ins.then_inc(set_dve, 1)
                dve.wait_ge(set_dve, done[0])

            def at(mark):
                assert done[0] == mark, (done[0], mark)

            dve.wait_ge(loaded_1st, LOADED_1ST)
            dve.wait_ge(set_pe, 1)
            step(v.tensor_tensor(bias_q[:, :], o_psum[0][:, 0:2], cols[:, 0:2], ALU.add))
            step(v.tensor_scalar(bias_q[:, :], bias_q[:, :], SCALE, None, ALU.mult))
            step(v.tensor_tensor(bias_kp[:, :], o_psum[0][:, 2:4], cols[:, 2:4], ALU.add))
            step(v.tensor_tensor(bias_ks[:, :], o_psum[0][:, 4:6], cols[:, 2:4], ALU.add))
            at(DVE_BIAS)
            dve.wait_ge(loaded_2nd, LOADED_2ND)
            step(v.tensor_copy(lens[:, :], lens_i[:, :]))
            step(v.tensor_scalar(mask_rows[:, :], iota_k[:, :], lens[:, 0:1], MASKED, ALU.is_ge, ALU.mult))
            at(DVE_MASK)
            dve.wait_ge(set_pool, POOL_DONE)

            def decays():
                dve.wait_ge(loaded_3rd, LOADED_3RD)
                step(v.scalar_tensor_tensor(sp_t[:, :], taus[:, :], -1.0, taus[:, :], ALU.mult, ALU.min))
                at(DVE_SP1)
                dve.wait_ge(set_act, 1)
                step(v.tensor_scalar(sp_u[:, :], sp_u[:, :], 1.0, None, ALU.add))
                at(DVE_SP2)
                dve.wait_ge(set_act, 2)
                step(v.scalar_tensor_tensor(sp[:, :], taus[:, :], 0.0, sp_t[:, :], ALU.max, ALU.add))
                step(v.tensor_scalar(neg_sp[:, :], sp[:, D:D + 1], -1.0, None, ALU.mult))
                step(v.tensor_tensor(far_in[:, :, :], c_far_e, sp[:, 0:D].unsqueeze(1).to_broadcast([P, 6 * CH, D]),
                                     ALU.mult))
                step(v.reduce_max(blend_m[:, :], blend_t[:, :, :], AX.X))
                step(v.tensor_tensor(blend_t[:, :, :], blend_t[:, :, :],
                                     blend_m[:, :].unsqueeze(2).to_broadcast([P, NB, D]), ALU.subtract))
                at(DVE_EXP)
                dve.wait_ge(set_act, ACT_DONE)
                step(v.reduce_sum(blend_s[:, :], blend_t[:, :, :], AX.X))
                step(v.reciprocal(blend_s[:, :], blend_s[:, :]))
                step(v.tensor_scalar(blend_s[:, :], blend_s[:, :], 0.5, None, ALU.mult))
                step(v.tensor_tensor(blend_t[:, :, :], blend_t[:, :, :],
                                     blend_s[:, :].unsqueeze(2).to_broadcast([P, NB, D]), ALU.mult))
                step(v.tensor_copy(blend_8[:, :, :, :], blend_t[:, :, :].unsqueeze(2).to_broadcast([P, NB, 8, D])))
                at(DVE_BLEND)
                step(v.memset(decay[:, :], 0.0))
                step(v.tensor_scalar(decay[:, :], decay[:, :], sp_u[:, 0:1], None, ALU.add))
                step(v.tensor_tensor(far_out[:, :, :], far_out[:, :, :], c_out_m, ALU.mult))
                step(v.tensor_tensor(far_in[:, :, :], far_in[:, :, :], c_far_m, ALU.mult))
                step(v.tensor_scalar(half_b[:, 0:2], cols[:, 10:12], 0.5, None, ALU.mult))
                step(v.tensor_scalar(half_b[:, 2:4], cols[:, 14:16], 0.5, None, ALU.mult))
                step(v.tensor_scalar(half_b[:, 4:5], col("bn2"), 0.5, None, ALU.mult))
                dve.wait_ge(set_pe, 2)
                step(v.tensor_copy(blend[:, :], o_psum[1][:, 0:E]))
                at(DVE_DECAY)

            def near_weights():
                dve.wait_ge(loaded_4th, LOADED_4TH)
                step(v.tensor_scalar(wout[:, :, :], wout[:, :, :], 0.5, None, ALU.mult))
                step(v.tensor_scalar(pow_col[:, :], pow_col[:, :], c_slot[:, 0:1], None, ALU.mult))
                for pair in range(CH // 2):
                    for n in range(2):
                        step(v.tensor_scalar(near_f[:, n, :], blend[:, :], pow_col[:, 2 * pair + n:2 * pair + n + 1],
                                             None, ALU.mult))
                    step(v.tensor_copy(near_h[:, :, :], near_f[:, :, :]))
                    step(v.scalar_tensor_tensor(near_r[:, :, :], near_h[:, :, :], c_slot[:, 1:2], near_f[:, :, :],
                                                ALU.mult, ALU.add))
                    step(v.tensor_copy(near_m[:, :, :], near_r[:, :, :]))
                    step(v.scalar_tensor_tensor(near_w[:, 2 * pair:2 * pair + 2, :], near_m[:, :, :], c_slot[:, 2:3],
                                                near_r[:, :, :], ALU.mult, ALU.add))
                at(DVE_DONE)

            def add_bias_v(dst, name, done_, b):
                v.tensor_tensor(dst, halves(side.bank(name)).rearrange("p n (h d) -> p n h d", d=DH),
                                over_blocks(bv_row).rearrange("p n (h d) -> p n h d", d=DH),
                                ALU.add).then_inc(done_.sem, 1)

            def near(b, n):
                wait(dve, pe_near, b, n + 1)
                if n == 0:
                    v.tensor_tensor(near_sum[:, :, :], gated[:, :, :], halves(side.bank("near0")),
                                    ALU.mult).then_inc(near_prod.sem, 1)
                    return
                if n >= 3:
                    wait(dve, near_added, b, n - 2)
                w = NB * NCH * (CH - n)
                v.tensor_tensor(near_p[n % 2][:, :, 0:CH - n],
                                gated[:, :, :].rearrange("p c (j r) -> p (c j) r", r=CH)[:, :, 0:CH - n],
                                side.bank(f"near{n}")[:, 0:w].rearrange("p (j r) -> p j r", r=CH - n),
                                ALU.mult).then_inc(near_prod.sem, 1)

            def body(i):
                bp, bm, bt, bx, bz = i + 1, i, i + -1, i + -2, i + -3
                for u in range(STEPS):
                    if u == 19 and i.is_number(0):
                        near_weights()
                    if M_AT <= u < M_AT + H and bm.valid():
                        h = u - M_AT
                        wait(dve, pe_max, bm, h + 1)
                        v.reduce_max(row_max[:, :, h], halves(score.bank(f"m{h}")), AX.X).then_inc(max_ready.sem, 1)
                    if u == 17 and bm.valid():
                        wait(dve, max_ready, bm)
                        wait(dve, self_score_ready, bm)
                        v.tensor_tensor(top[:, :, :], row_max[:, :, :], self_score[bm.par][:, :, :],
                                        ALU.max).then_inc(neg_chain.sem, 1)
                        wait(dve, neg_chain, bm, 1)
                        v.tensor_scalar(neg_part[:, :, 0, :], top[:, :, :], -1.0, None,
                                        ALU.mult).then_inc(neg_chain.sem, 1)
                        v.tensor_tensor(self_diff[:, :, :], self_score[bm.par][:, :, :], top[:, :, :],
                                        ALU.subtract).then_inc(neg_chain.sem, 1)
                        wait(dve, neg_chain, bm, 3)
                        v.scalar_tensor_tensor(neg_res[:, :, :], top[:, :, :], -1.0, neg_part[:, :, 0, :],
                                               ALU.mult, ALU.subtract).then_inc(neg_chain.sem, 1)
                        wait(dve, neg_chain, bm, 4)
                        v.tensor_copy(neg_part[:, :, 1, :], neg_res[:, :, :]).then_inc(neg_chain.sem, 1)
                        wait(dve, neg_chain, bm, 5)
                        v.tensor_tensor(neg_part[:, :, 2, :], neg_res[:, :, :], neg_part[:, :, 1, :],
                                        ALU.subtract).then_inc(neg_chain.sem, 1)
                    if u == 3 and bx.valid():
                        wait(dve, gate_g_ready, bx)
                        v.scalar_tensor_tensor(gated[:, :, :], gate_g[:, :, :], 1.0, x1t[bx.par][:, :, :],
                                               ALU.add, ALU.mult).then_inc(gated_ready.sem, 1)
                    if u == 7 and bp.valid():
                        wait(dve, pe_ks, bp)
                        wait(dve, q_ready, bp)
                        for e in range(NB):
                            last = v.scalar_tensor_tensor(self_prod[:, e, :], halves(side.bank("ks"))[:, e, :],
                                                          bias_ks[:, e:e + 1], qf[:, e, :], ALU.add, ALU.mult)
                        last.then_inc(self_prod_ready.sem, 1)
                    if u == 29 and bx.valid():
                        wait(dve, pe_out, bx)
                        for t in range(NB):
                            v.bn_stats(stats[:, t, :], halves(side.bank("out"))[:, t, :]).then_inc(norm_chain.sem, 1)
                        wait(dve, norm_chain, bx, 2)
                        passed_by(dve, dve_passed)
                        for t in range(NB):
                            v.bn_aggr(mean_var[:, t, :], stats[:, t, :]).then_inc(norm_chain.sem, 1)
                        wait(dve, norm_chain, bx, 4)
                        v.tensor_scalar(var_eps[:, :], mean_var[:, :, 1], EPS, None,
                                        ALU.add).then_inc(norm_chain.sem, 1)
                        for t in range(NB):
                            v.scalar_tensor_tensor(centred[:, t, :], halves(side.bank("out"))[:, t, :],
                                                   mean_var[:, t, 0:1], gamma_row[:, :], ALU.subtract,
                                                   ALU.mult).then_inc(norm_chain.sem, 1)
                    if u == 0 and bz.valid():
                        wait(dve, rstd_ready, bz)
                        wait(dve, norm_chain, bz)
                        wait(dve, x1_beta_ready, bz)
                        wait_dma(dve, stored, bz + -2, 16)
                        for t in range(NB):
                            last = v.scalar_tensor_tensor(result[bz.par][:, t, :], centred[:, t, :], rstd[:, t:t + 1],
                                                          x1_beta[:, t, :], ALU.mult, ALU.add)
                        last.then_inc(result_ready.sem, 1)
                    if u == 6 and bx.valid():
                        wait(dve, pe_x1n, bx)
                        wait(dve, result_ready, bx + -1)
                        v.tensor_tensor(x1_beta[:, :, :], halves(side.bank("x1n")), over_blocks(beta_row),
                                        ALU.add).then_inc(x1_beta_ready.sem, 1)
                    if u == 9 and bt.valid():
                        wait(dve, self_pv_ready, bt)
                        for t in range(NB):
                            wait(dve, pe_on, bt, t + 1)
                            o = side.bank(f"on{t}")[:, :].rearrange("p (h c) -> p h c", c=32)
                            v.tensor_tensor(num[:, t, :].rearrange("p (h d) -> p h d", d=DH), o[:, :, 0:DH],
                                            self_pv[:, t, :].rearrange("p (h d) -> p h d", d=DH),
                                            ALU.add).then_inc(num_chain.sem, 1)
                            v.tensor_tensor(den[:, t, :], o[:, :, DH], self_p[:, t, :],
                                            ALU.add).then_inc(num_chain.sem, 1)
                        wait(dve, num_chain, bt, 4)
                        v.reciprocal(rden[:, :, :], den[:, :, :]).then_inc(num_chain.sem, 1)
                    if u == 25 and bt.valid():
                        wait(dve, pe_modn, bt)
                        v.tensor_copy(mod_n[:, :, :], side.bank("modn")[:, 0:NB * D].rearrange(
                            "p (t d) -> p t d", d=D)).then_inc(mod_n_ready.sem, 1)
                    if u == 18 and bp.valid():
                        wait(dve, pe_vp, bp)
                        add_bias_v(v_ones[bp.par][:, :, :, 0:DH], "vp", v_ready, bp)
                    if u in NEAR_AT and bx.valid():
                        near(bx, NEAR_AT.index(u))
                    if u == 10 and bx.valid():
                        for n in range(2):
                            wait(dve, pe_far, bx, n + 1)
                            v.tensor_tensor(states[:, 2 * n:2 * n + 2, :], halves(side.bank(f"far{n}")),
                                            over_blocks(blend), ALU.mult).then_inc(states_ready.sem, 1)
                    if u == 15 and bt.valid():
                        wait(dve, pe_wo, bt)
                        wait_dma(dve, xe_in, bt, 16)
                        for c in range(NB):
                            last = v.scalar_tensor_tensor(x1t[bt.par][:, c, :], halves(side.bank("wo"))[:, c, :],
                                                          col("bo", c), xe[bt.par][:, c, :], ALU.add, ALU.add)
                        last.then_inc(x1_ready.sem, 1)
                    if u == 20 and bt.valid():
                        wait(dve, x1_ready, bt)
                        for c in range(NB):
                            last = v.tensor_tensor_scan(ctx_t[:, c, :], decay[:, :], x1t[bt.par][:, c, :], 0.0,
                                                        ALU.mult, ALU.add)
                        last.then_inc(ctx_ready.sem, 1)
                    if u == 19 and bx.valid():
                        wait(dve, pe_yt, bx)
                        wait(dve, near_added, bx)
                        v.tensor_tensor(temporal[:, :, :], near_sum[:, :, :], halves(side.bank("yt")),
                                        ALU.add).then_inc(temporal_ready.sem, 1)
                    if u == 16 and bp.valid():
                        wait(dve, pe_vs, bp)
                        add_bias_v(v_self[bp.par][:, :, :].rearrange("p n (h d) -> p n h d", d=DH), "vs",
                                   v_self_ready, bp)
                    if u == 23 and bx.valid():
                        wait(dve, gate_t_ready, bx)
                        wait(dve, soma_ready, bx)
                        v.scalar_tensor_tensor(mixed[:, :, :], gate_t[:, :, :], 1.0, soma[:, :, :],
                                               ALU.add, ALU.mult).then_inc(mixed_ready.sem, 1)
                    if u == 26 and bp.valid():
                        wait(dve, pe_prn, bp)
                        v.reduce_sum(self_score[bp.par][:, :, :].rearrange("p t (e h) -> p (t e) h", e=NB),
                                     side.bank("prn")[:, :].rearrange("p (x d h) -> p x h d", d=DH, h=8),
                                     AX.X).then_inc(self_score_ready.sem, 1)

            iterations(dve, body, {0: decays})

        @block.gpsimd
        def _(pool):
            g = nc.gpsimd
            done = [0]

            def step(ins):
                done[0] += 1
                ins.then_inc(set_pool, 1)
                pool.wait_ge(set_pool, done[0])

            step(g.memset(wn2[HID:P, :], 0.0))
            step(g.memset(hid[HID:P, :], 0.0))
            step(g.memset(minus_half[:, :], -0.5))
            for p in range(2):
                step(g.memset(v_ones[p][:, :, :, :], 0.0))
                step(g.memset(q_stack[p][KROWS:P, :, :], 1.0))
                step(g.memset(k_stack[p][KROWS:P, :, :], 1.0))
            for p in range(2):
                step(g.memset(v_ones[p][:, :, :, DH:DH + 1], 1.0))
            step(g.memset(mod_res[:, :], 0.0))
            assert done[0] == POOL_DONE

            def residual(dst, whole, part, done_, b):
                g.tensor_tensor(dst[:, :, :], whole[:, :, :], part[:, :, :], ALU.subtract).then_inc(done_.sem, 1)

            def near_add(b, n):
                wait(pool, near_prod, b, n + 1)
                if n > 1:
                    wait(pool, near_added, b, n - 1)
                rows = near_sum[:, :, :].rearrange("p c (j r) -> p (c j) r", r=CH)[:, :, n:CH]
                g.tensor_tensor(rows, rows, near_p[n % 2][:, :, 0:CH - n], ALU.add).then_inc(near_added.sem, 1)

            def body(i):
                bp, bm, bt, bx, bz = i + 1, i, i + -1, i + -2, i + -3
                for u in range(STEPS):
                    if u == 4 and bp.valid():
                        wait(pool, q_high, bp)
                        residual(q_res, qf, q_part[0], q_res_ready, bp)
                    if u == 7 and bp.valid():
                        wait(pool, k_high, bp)
                        residual(k_res, kf, k_part[0], k_res_ready, bp)
                    if u == 6 and bp.valid():
                        wait(pool, q_mid, bp)
                        wait(pool, q_res_ready, bp)
                        residual(q_part[2], q_res, q_part[1], q_low, bp)
                    if u == 10 and bt.valid():
                        wait(pool, num_chain, bt)
                        heads = num[:, :, :].rearrange("p t (h d) -> p (t h) d", d=DH)
                        g.tensor_tensor(attn[:, :, :].rearrange("p t (h d) -> p (t h) d", d=DH), heads,
                                        rden[:, :, :].rearrange("p t h -> p (t h)").unsqueeze(2)
                                        .to_broadcast([P, NB * H, DH]), ALU.mult).then_inc(attn_ready.sem, 1)
                    if u == 11 and bp.valid():
                        wait(pool, k_mid, bp)
                        wait(pool, k_res_ready, bp)
                        residual(k_part[2], k_res, k_part[1], k_low, bp)
                    if u == 26 and bt.valid():
                        wait(pool, mod_n_ready, bt)
                        for k, (lo, hi) in enumerate(((0, 4 * CH), (4 * CH, 6 * CH))):
                            last = g.tensor_tensor(state_in[:, lo:hi, :], far_in[:, lo:hi, :],
                                                   mod_n[:, k, :].unsqueeze(1).to_broadcast([P, hi - lo, D]), ALU.mult)
                        last.then_inc(state_in_ready.sem, 1)
                    if u in NEAR_AT[1:] and bx.valid():
                        near_add(bx, NEAR_AT.index(u))
                    if u == 20 and bt.valid():
                        wait(pool, mod_th_ready, bt)
                        passed_by(pool, pool_passed)
                        g.tensor_scalar(mod[:, :], mod_th[:, :], 0.5, 1.0, ALU.mult, ALU.add)\
                            .then_inc(mod_ready.sem, 1)
                        wait(pool, mod_ready, bt)
                        passed_by(pool, pool_passed)
                        g.tensor_scalar(mod_stack[:, :], mod[:, :], 1.0, 0.0, ALU.mult, ALU.add)\
                            .then_inc(mod_chain.sem, 1)
                        wait(pool, mod_chain, bt, 1)
                        g.tensor_tensor(mod_res[96:P, :], mod[96:P, :], mod_stack[96:P, :], ALU.subtract)\
                            .then_inc(mod_chain.sem, 1)
                        wait(pool, mod_chain, bt, 2)
                        g.tensor_tensor(mod_stack[32:64, :], mod[32:64, :], mod_stack[32:64, :], ALU.subtract)\
                            .then_inc(mod_chain.sem, 1)
                        wait(pool, mod_chain, bt, 3)
                        passed_by(pool, pool_passed)
                        g.tensor_scalar(mod_mid[96:P, :], mod_res[96:P, :], 1.0, 0.0, ALU.mult, ALU.add)\
                            .then_inc(mod_chain.sem, 1)
                        wait(pool, mod_chain, bt, 4)
                        g.tensor_tensor(mod_stack[96:P, :], mod_res[96:P, :], mod_mid[96:P, :], ALU.subtract)\
                            .then_inc(mod_chain.sem, 1)
                        wait(pool, mod_chain, bt)
                    if u == 27 and bm.valid():
                        wait(pool, self_p_ready, bm)
                        wait(pool, v_self_ready, bm)
                        g.tensor_tensor(self_pv[:, :, :].rearrange("p t (h d) -> p (t h) d", d=DH),
                                        v_self[bm.par][:, :, :].rearrange("p t (h d) -> p (t h) d", d=DH),
                                        self_p[:, :, :].rearrange("p t h -> p (t h)").unsqueeze(2)
                                        .to_broadcast([P, NB * H, DH]), ALU.mult).then_inc(self_pv_ready.sem, 1)
                    if u == 29 and bx.valid():
                        wait(pool, norm_chain, bx, 5)
                        g.tensor_tensor(rstd[:, :], var_eps[:, :], minus_half[:, :], ALU.pow)\
                            .then_inc(rstd_ready.sem, 1)

            iterations(pool, body, {})


def constants():
    far_e, far_m = np.zeros((P, 6, CH, 1), np.float32), np.zeros((P, 6, CH, 1), np.float32)
    for blk in range(6):
        i, k = (blk, 0) if blk < SB else (blk - 2, 1)
        start = CH * (CH * i + np.arange(CH))[None, :]
        e = start - 1 - (P * k + np.arange(P)[:, None])
        far_e[:, blk, :, 0], far_m[:, blk, :, 0] = np.maximum(e, 0), e >= 0
    far_e, far_m = (np.broadcast_to(a, (P, 6, CH, D)).reshape(P, -1) for a in (far_e, far_m))
    chunk = (np.arange(P) // D)[:, None]
    out_e, out_m = np.zeros((P, 2, P), np.float32), np.zeros((P, 2, P), np.float32)
    for a in range(2):
        e = np.arange(P)[None, :] - (P // 2 * a + CH * chunk) + 1
        inside = (e >= 1) & (e <= CH)
        out_e[:, a, :], out_m[:, a, :] = np.where(inside, e, 0), inside
    dist = np.broadcast_to(np.arange(CH, dtype=np.float32), (P, CH))
    slot = np.arange(P) // D
    slots = np.stack([sign * np.isin(slot, s) for sign, s in ((1, (0, 1, 2, 3, 4, 6)), (-1, (1, 3, 4)), (-1, (4,)))], 1)
    return np.concatenate([far_e, far_m, out_e.reshape(P, -1), out_m.reshape(P, -1), dist, slots], 1)\
        .astype(np.float32)


def kernel(**inputs):
    import concourse.bacc as bacc
    from concourse.bass_utils import run_bass_kernel_spmd
    a = {k: np.asarray(v) for k, v in inputs.items()}

    def blocks(w):
        return np.ascontiguousarray(w.reshape(-1, P, w.shape[1]).transpose(1, 0, 2))

    def column(v):
        return v.reshape(-1, P).T

    order = np.arange(E).reshape(NB, H // NB, DH).transpose(0, 2, 1).reshape(-1)
    row = {n: np.ascontiguousarray(np.broadcast_to(a[k], (P, E))) for n, k in
           (("bv", "L0_cond_bv"), ("gamma", "L1_cond_gamma"), ("beta", "L1_cond_beta"))}
    cols = np.zeros((P, 18 + D + 2), np.float32)
    for at, v in ((0, a["L0_cond_bq"][order]), (2, a["L0_cond_bk"][order]), (4, a["L0_cond_b_self"].reshape(-1)),
                  (6, a["L0_cond_b_prev"].reshape(-1)), (8, a["L0_cond_bo"]), (10, a["L1_cond_bg"]),
                  (12, a["L1_cond_bsoma"]), (14, a["L1_cond_btemp"])):
        cols[:, at:at + 2] = column(v)
    cols[0:HID, 16] = a["L1_cond_bn1"]
    cols[:, 17] = np.tile(a["condB_bn2"], P // D)
    tau = a["condB_tauraws"]
    cols[:, 18:] = np.concatenate([np.broadcast_to(tau, (P, D)), np.tile(tau, P // D)[:, None],
                                   np.broadcast_to(a["L1_cond_tau_ctx"], (P, 1))], 1)

    def rows_t(x):
        return np.ascontiguousarray(x.reshape(B, T, NB, P).transpose(0, 3, 2, 1))

    import ml_dtypes
    feeds = {
        "xt": rows_t(a["x"]), "x2t": rows_t(a["fside_BxSxS_0"]),
        "wq": blocks(a["L0_cond_Wq"][:, order]), "wk": blocks(a["L0_cond_Wk"][:, order]),
        "wv": blocks(a["L0_cond_Wv"]), "wo": blocks(a["L0_cond_Wo"]), "wg": blocks(a["L1_cond_Wg"].T),
        "wn1": blocks(a["L1_cond_Wn1"].T), "wn2": np.ascontiguousarray(np.tile(a["cond_256"].T, (1, P // D))),
        "wsoma": blocks(a["L1_cond_Wsoma"].T), "wtemp": blocks(a["L1_cond_Wtemp"].T),
        "wout": blocks(a["L1_cond_Wout"].T), "cols": cols, "bv": row["bv"],
        "gamma_beta": np.ascontiguousarray(np.stack([row["gamma"], row["beta"]], 1)),
        "blend": blocks(a["cond_1024"].T), "consts": constants(), "ident": np.eye(P, dtype=np.float32),
        "ident_b": np.eye(P, dtype=ml_dtypes.bfloat16),
        "iota": np.ascontiguousarray(np.broadcast_to(np.arange(T, dtype=np.float32), (B, T))),
        "lens": np.ascontiguousarray(a["itok_B_18_1004"].reshape(B, 1)),
    }
    nc = bacc.Bacc("TRN2", target_bir_lowering=False, num_devices=1)
    d = {k: nc.dram_tensor(f"in_{k}", v.shape, mybir.dt.from_np(v.dtype), kind="ExternalInput").ap()
         for k, v in feeds.items()}
    d["mask"] = lambda rows, b: rows[b].unsqueeze(0).unsqueeze(1).to_broadcast([1, H, T])
    out = nc.dram_tensor("out", (B, P, NB, E), F32, kind="ExternalOutput").ap()
    build(nc, d, out)
    r = run_bass_kernel_spmd(nc, [{f"in_{k}": v for k, v in feeds.items()}], core_ids=[0])
    got = np.asarray(r.results[0]["out"])
    return np.ascontiguousarray(got.transpose(0, 2, 1, 3).reshape(B, T, E))
```

```python
from contextlib import ExitStack

import numpy as np

import concourse.bass as bass
from concourse import mybir

ALU = mybir.AluOpType
ACT = mybir.ActivationFunctionType
AX = mybir.AxisListType
F32 = mybir.dt.float32
BF16 = mybir.dt.bfloat16
F32R = mybir.dt.float32r
I32 = mybir.dt.int32

P = 128
B, T, E, H = 16, 256, 256, 16
DH = E // H
NB = E // P
D = 16
HID = 64
CH = 8
NCH = T // CH
NEAR_AT = (5, 6, 8, 11, 13, 15, 16, 17)
SB = 4
SCALE = 1.0 / float(np.sqrt(DH))
EPS = 1e-5
MASKED = -1e30
TOP_BITS = -(1 << 12)
KROWS = 96
PARTS = ((0, 0), (0, 1), (1, 0), (1, 1), (0, 2), (2, 0))

FIRST, LOOP_FIRST, PAIRS, LAST = -1, 5, (B - 2 - 5) // 2, B + 2
STEPS = 32
M_AT = 1
A_AT = 22
A_NOW = STEPS - A_AT


class Step:

    def __init__(self, k, c):
        self.k, self.c, self.par = k, c, c % 2

    def __add__(self, lag):
        return Step(self.k, self.c + lag)

    def number(self):
        return self.c if self.k is None else self.k * 2 + self.c

    def half(self):
        return self.c // 2 if self.k is None else self.k + self.c // 2

    def valid(self):
        return self.k is not None or 0 <= self.c < B

    def first(self):
        return self.before(FIRST + 1)

    def before(self, c):
        return self.k is None and self.c < c

    def is_number(self, c):
        return self.k is None and self.c == c


def iterations(eng, body, before):
    for c in range(FIRST, LOOP_FIRST):
        if c in before:
            before[c]()
        body(Step(None, c))
    with eng.Fori(0, PAIRS) as k:
        body(Step(k, LOOP_FIRST))
        body(Step(k, LOOP_FIRST + 1))
    for c in range(LOOP_FIRST + 2 * PAIRS, LAST + 1):
        body(Step(None, c))


class Signal:

    def __init__(self, sem, per=1):
        self.sem, self.per = sem, per

    def at(self, batch, nth=None):
        return batch.number() * self.per + (self.per if nth is None else nth)


def wait(eng, signal, batch, nth=None):
    if batch.k is None and batch.c < 0:
        return
    eng.wait_ge(signal.sem, signal.at(batch, nth))


def wait_dma(eng, pair, batch, per):
    if batch.k is None and batch.c < 0:
        return
    eng.wait_ge(pair[batch.par], batch.half() * per + per)


class Banks:

    def __init__(self, tiles, uses):
        self.tiles, self.uses = tiles, uses
        self.pos = {use[0]: n for n, use in enumerate(uses)}

    def bank(self, name):
        return self.tiles[self.pos[name] % len(self.tiles)]

    def wait_free(self, eng, name, i):
        at, n = self.pos[name], len(self.tiles)
        same = [q for q in range(len(self.uses)) if q % n == at % n]
        before = [(q, 0) for q in same if q < at]
        while True:
            if not before:
                i, before = i + -1, [(q, 0) for q in same]
                if i.k is None and i.c < FIRST:
                    return
            q = before.pop()[0]
            _, lag, signal, nth = self.uses[q]
            if (i + lag).valid():
                return wait(eng, signal, i + lag, nth)


DVE_WQ, DVE_BIAS, DVE_WK, DVE_MASK, DVE_SP1, DVE_SP2, DVE_EXP, DVE_BLEND, DVE_DECAY, DVE_DONE = (
    3, 7, 10, 15, 16, 17, 22, 27, 34, 37)
ACT_DONE, POOL_DONE, POOL_NEAR = 7, 12, 44


def build(nc, d, out):
    ctx = ExitStack()
    with ctx:
        def sb(name, shape, dt=F32):
            return ctx.enter_context(nc.sbuf_tensor(name, shape, dt))

        def two(name, shape, dt=F32):
            return [sb(f"{name}{p}", shape, dt) for p in range(2)]

        def psum(name, shape):
            return ctx.enter_context(nc.psum_tensor(name, shape, F32))

        def sem(name):
            return ctx.enter_context(nc.semaphore(name))

        def signal(name, per=1):
            return Signal(sem(name), per)

        wo = sb("wo", [P, NB, E])
        wq_parts, wk_parts, wv_parts = ([sb(f"w{n}_{part}", [P, NB, E], F32R) for part in ("top", "rest")]
                                        for n in "qkv")
        wg = sb("wg", [P, 2 * NB, E])
        wn1 = sb("wn1", [P, NB, HID])
        wn2 = sb("wn2", [P, P])
        wsoma, wtemp, wout = (sb(n, [P, NB, E]) for n in ("wsoma", "wtemp", "wout"))
        cols = sb("cols", [P, 18 + D + 2])
        taus = cols[:, 18:18 + D + 2]
        bv_row = sb("bv_row", [P, E])
        gamma_beta = sb("gamma_beta", [P, 2, E])
        gamma_row, beta_row = gamma_beta[:, 0, :], gamma_beta[:, 1, :]
        ident = sb("ident", [P, P])
        ident_b = sb("ident_b", [P, P], BF16)
        bias_q, bias_kp, bias_ks = (sb(n, [P, NB]) for n in ("bias_q", "bias_kp", "bias_ks"))
        half_b = sb("half_b", [P, 5])
        sp, sp_t, sp_u = (sb(n, [P, D + 2]) for n in ("sp", "sp_t", "sp_u"))
        neg_sp = sb("neg_sp", [P, 1])
        decay = sb("decay", [P, T])
        far_in = sb("far_in", [P, 6 * CH, D])
        far_out = sb("far_out", [P, 2, P])
        pow_col = sb("pow_col", [P, CH])
        blend_t = sb("blend_t", [P, NB, D])
        blend_m, blend_s = sb("blend_m", [P, NB]), sb("blend_s", [P, NB])
        blend_8 = sb("blend_8", [P, NB, 8, D])
        blend = sb("blend", [P, E])
        near_w = sb("near_w", [P, CH, E], BF16)
        consts = sb("consts", [P, 2 * 6 * CH * D + 4 * P + CH + 3])
        iota_k, lens_i, lens = sb("iota_k", [B, T]), sb("lens_i", [B, 1], mybir.dt.int32), sb("lens", [B, 1])
        mask_rows = sb("mask_rows", [B, T], BF16)
        minus_half = sb("minus_half", [P, NB])
        mask_dram = nc.dram_tensor("mask_scratch", (B, T), BF16, kind="Internal").ap()

        nA = 6 * CH * D
        c_far_e = consts[:, 0:nA].rearrange("p (j d) -> p j d", d=D)
        c_far_m = consts[:, nA:2 * nA].rearrange("p (j d) -> p j d", d=D)
        c_out_e = consts[:, 2 * nA:2 * nA + 2 * P].rearrange("p (a t) -> p a t", a=2)
        c_out_m = consts[:, 2 * nA + 2 * P:2 * nA + 4 * P].rearrange("p (a t) -> p a t", a=2)
        c_dist = consts[:, 2 * nA + 4 * P:2 * nA + 4 * P + CH]
        c_slot = consts[:, 2 * nA + 4 * P + CH:2 * nA + 4 * P + CH + 3]

        def col(name, n=0):
            at = {"bq": 0, "bk": 2, "b_self": 4, "b_prev": 6, "bo": 8, "bg": 10, "bsoma": 12, "btemp": 14,
                  "bn1": 16, "bn2": 17}[name] + n
            return cols[:, at:at + 1]

        xt, x2t, xe = sb("xt", [P, NB, T]), sb("x2t", [P, NB, T]), two("xe", [P, NB, T])
        x2_parts, x_parts = ([sb(f"{n}_{part}", [P, NB, T], F32R) for part in ("top", "rest")] for n in ("x2", "x"))
        top_bits = sb("top_bits", [P, NB, T])
        qf, kf = sb("qf", [P, NB, T]), sb("kf", [P, NB, T])
        q_res, k_res = sb("q_res", [P, NB, T]), sb("k_res", [P, NB, T])
        q_part = [sb(f"q_part{n}", [P, NB, T], BF16) for n in range(3)]
        k_part = [sb(f"k_part{n}", [P, NB, T], BF16) for n in range(3)]
        q_stack, k_stack = two("q_stack", [P, H, T], BF16), two("k_stack", [P, H, T], BF16)
        self_prod = sb("self_prod", [P, NB, T])
        self_score = two("self_score", [P, NB, H])
        v_ones = two("v_ones", [P, NB, H, 32])
        v_self = two("v_self", [P, NB, E])
        row_max, top, top_res = sb("row_max", [P, NB, H]), sb("top", [P, NB, H]), sb("top_res", [P, NB, H])
        top_part = sb("top_part", [P, NB, 3, H], BF16)
        top_t = sb("top_t", [3 * H, T], BF16)
        self_diff, self_p = sb("self_diff", [P, NB, H]), sb("self_p", [P, NB, H])
        self_pv = sb("self_pv", [P, NB, E])
        probs = sb("probs", [P, 8, NB, T])
        o_t = sb("o_t", [P, 4, T])
        den, rden = sb("den", [P, NB, H]), sb("rden", [P, NB, H])
        num, attn, attn_t = sb("num", [P, NB, E]), sb("attn", [P, NB, E]), sb("attn_t", [P, NB, T])
        x1t = two("x1t", [P, NB, T])
        ctx_t = sb("ctx_t", [P, NB, T])
        gate_g, gated, gated_n = sb("gate_g", [P, NB, T]), sb("gated", [P, NB, T]), sb("gated_n", [P, NB, E])
        hid = sb("hid", [P, T])
        mod, mod_res, mod_mid = sb("mod", [P, T]), sb("mod_res", [P, T]), sb("mod_mid", [P, T], BF16)
        mod_th = sb("mod_th", [P, T])
        mod_stack = sb("mod_stack", [P, T], BF16)
        mod_n = sb("mod_n", [P, NB, D])
        state_in = sb("state_in", [P, 6 * CH, D])
        states = sb("states", [P, SB, E])
        near_p = two("near_p", [P, NB * NCH, CH])
        near_sum = sb("near_sum", [P, NB, T])
        far_n = sb("far_n", [P, NB, E])
        temporal = sb("temporal", [P, NB, T])
        gate_t, soma, mixed = sb("gate_t", [P, NB, T]), sb("soma", [P, NB, T]), sb("mixed", [P, NB, T])
        x1_beta = sb("x1_beta", [P, NB, E])
        stats, mean_var = sb("stats", [P, NB, 6]), sb("mean_var", [P, NB, 2])
        var_eps, rstd = sb("var_eps", [P, NB]), sb("rstd", [P, NB])
        centred = sb("centred", [P, NB, E])
        result = two("result", [P, NB, E])

        wq, wk, wv = soma, mixed, gate_t
        near_f, near_r = gated, gate_g
        near_h, near_m = (t[:, 0, :].bitcast(BF16).rearrange("p (n c) -> p n c", n=2) for t in (near_sum, temporal))

        s_psum = [psum(f"s_psum{n}", [P, 512]) for n in range(2)]
        o_psum = [psum(f"o_psum{n}", [P, 512]) for n in range(2)]
        side_psum = [psum(f"side_psum{n}", [P, 512]) for n in range(4)]

        loaded_1st, loaded_2nd, loaded_3rd, loaded_4th = (sem("loaded_" + n) for n in ("1st", "2nd", "3rd", "4th"))
        set_dve, set_act, set_pe, set_pool = (sem(n) for n in ("set_dve", "set_act", "set_pe", "set_pool"))
        mask_stored = sem("mask_stored")
        pe_passed, dve_passed, pool_passed, sp_passed = (sem(n + "_passed") for n in ("pe", "dve", "pool", "sp"))
        x_in = [sem(f"x_in{p}") for p in range(2)]
        xe_in = [sem(f"xe_in{p}") for p in range(2)]
        q_stacked = [sem(f"q_stacked{p}") for p in range(2)]
        k_stacked = [sem(f"k_stacked{p}") for p in range(2)]
        max_stacked = [sem(f"max_stacked{p}") for p in range(2)]
        stored = [sem(f"stored{p}") for p in range(2)]
        NQ, NK, NM, NX = 16 * len(PARTS), 16 * (len(PARTS) + 1), 16 * 3, 16 * 2
        pe_wg, pe_q, pe_k, pe_ks, pe_vp, pe_vs, pe_prn, pe_gn, pe_h1, pe_soma, pe_x1n, pe_mod, pe_modn, pe_at, \
            pe_wo, pe_y, pe_yt, pe_nm, pe_gate, pe_out = (signal("pe_" + n) for n in (
                "wg", "q", "k", "ks", "vp", "vs", "prn", "gn", "h1", "soma", "x1n", "mod", "modn", "at", "wo",
                "y", "yt", "nm", "gate", "out"))
        pe_on, pe_far, pe_near = signal("pe_on", 2), signal("pe_far", 2), signal("pe_near", CH)
        pe_max, pe_score, pe_av = signal("pe_max", H), signal("pe_score", H), signal("pe_av", 4)
        q_ready, k_ready = signal("q_ready"), signal("k_ready")
        q_high, k_high, q_mid, k_mid = (signal(n) for n in ("q_high", "k_high", "q_mid", "k_mid"))
        probs_ready, o_ready, attn_t_ready = signal("probs_ready", H), signal("o_ready", 2), signal("attn_t_ready")
        gate_g_ready, hid_ready, mod_th_ready, gated_n_ready, far_n_ready, gate_t_ready, soma_ready, top_t_ready, \
            self_p_ready = (signal(n + "_ready") for n in (
                "gate_g", "hid", "mod_th", "gated_n", "far_n", "gate_t", "soma", "top_t", "self_p"))
        max_ready = signal("max_ready", H)
        x2_split, x_split = signal("x2_split", 3), signal("x_split", 3)
        top_chain = signal("top_chain", 6)
        gated_ready, self_prod_ready, self_score_ready, v_ready, v_self_ready, mod_n_ready, x1_ready, ctx_ready, \
            temporal_ready, mixed_ready, x1_beta_ready, result_ready = (signal(n + "_ready") for n in (
                "gated", "self_prod", "self_score", "v", "v_self", "mod_n", "x1", "ctx", "temporal", "mixed",
                "x1_beta", "result"))
        states_ready = signal("states_ready", 2)
        num_chain = signal("num_chain", 5)
        near_prod = signal("near_prod", CH)
        norm_chain = signal("norm_chain", 7)
        q_res_ready, k_res_ready, q_low, k_low, mod_ready, state_in_ready, attn_ready, self_pv_ready, rstd_ready = (
            signal(n) for n in ("q_res_ready", "k_res_ready", "q_low", "k_low", "mod_ready", "state_in_ready",
                                "attn_ready", "self_pv_ready", "rstd_ready"))
        mod_chain = signal("mod_chain", 5)
        near_added = signal("near_added", CH - 1)

        side = Banks(side_psum, [
            ("wg", -2, gate_g_ready, 1), ("q", 1, q_ready, 1), ("k", 1, k_ready, 1), ("gn", -2, gated_n_ready, 1),
            ("near0", -2, near_prod, 1), ("near1", -2, near_prod, 2), ("near2", -2, near_prod, 3), ("on0", -1, num_chain, 2),
            ("on1", -1, num_chain, 4), ("far0", -2, states_ready, 1), ("far1", -2, states_ready, 2),
            ("near3", -2, near_prod, 4), ("at", -1, attn_t_ready, 1), ("y", -2, far_n_ready, 1),
            ("near4", -2, near_prod, 5), ("wo", -1, x1_ready, 1), ("near5", -2, near_prod, 6),
            ("vs", 1, v_self_ready, 1), ("near6", -2, near_prod, 7), ("h1", -1, hid_ready, 1),
            ("near7", -2, near_prod, 8), ("vp", 1, v_ready, 1), ("yt", -2, temporal_ready, 1),
            ("mod", -1, mod_th_ready, 1), ("nm", 0, top_t_ready, 1), ("soma", -2, soma_ready, 1),
            ("gate", -2, gate_t_ready, 1), ("ks", 1, self_prod_ready, 1), ("x1n", -2, x1_beta_ready, 1), ("modn", -1, mod_n_ready, 1), ("prn", 1, self_score_ready, 1),
            ("out", -2, norm_chain, 7)])
        score_uses = []
        for u in range(STEPS):
            if u < H - A_NOW:
                score_uses.append((f"a{A_NOW + u}", -1, probs_ready, A_NOW + u + 1))
            if M_AT <= u < M_AT + H:
                score_uses.append((f"m{u - M_AT}", 0, max_ready, u - M_AT + 1))
            if u >= A_AT:
                score_uses.append((f"a{u - A_AT}", 0, probs_ready, u - A_AT + 1))
        score = Banks(s_psum, score_uses)

        block = ctx.enter_context(nc.Block())
        loads_1st = [(cols[:, :], d["cols"]), (wq[:, :, :], d["wq"]), (wk[:, :, :], d["wk"])]
        loads_2nd = [(iota_k[:, :], d["iota"]), (lens_i[:, :], d["lens"]), (wv[:, :, :], d["wv"]),
                     (bv_row[:, :], d["bv"]), (ident[:, :], d["ident"])]
        loads_3rd = [(blend_t[:, :, :], d["blend"]), (consts[:, :], d["consts"]), (ident_b[:, :], d["ident_b"])]
        loads_4th = [(wo[:, :, :], d["wo"]), (wn1[:, :, :], d["wn1"]), (wn2[0:HID, :], d["wn2"]),
                     (wg[:, :, :], d["wg"]), (wsoma[:, :, :], d["wsoma"]), (wtemp[:, :, :], d["wtemp"]),
                     (wout[:, :, :], d["wout"]), (gamma_beta[:, :, :], d["gamma_beta"])]
        LOADED_1ST, LOADED_2ND, LOADED_3RD, LOADED_4TH = (16 * len(l) for l in (loads_1st, loads_2nd, loads_3rd,
                                                                                loads_4th))

        def passed_by(eng, count):
            eng.sem_inc(count, 1)

        @block.sync
        def _(sp_eng):
            def load_x(b):
                for split in (x2_split, x_split):
                    wait(sp_eng, split, b + -1)
                if not b.before(1):
                    passed_by(sp_eng, sp_passed)
                sp_eng.dma_start(x2t[:, :, :], d["x2t"][b.number()]).then_inc(x_in[b.par], 16)
                sp_eng.dma_start(xt[:, :, :], d["xt"][b.number()]).then_inc(x_in[b.par], 16)

            def load_rest():
                for dst, src in loads_4th:
                    sp_eng.dma_start(dst, src).then_inc(loaded_4th, 16)

            for dst, src in loads_1st:
                sp_eng.dma_start(dst, src).then_inc(loaded_1st, 16)
            load_x(Step(None, 0))
            for dst, src in loads_2nd:
                sp_eng.dma_start(dst, src).then_inc(loaded_2nd, 16)
            for dst, src in loads_3rd:
                sp_eng.dma_start(dst, src).then_inc(loaded_3rd, 16)
            load_x(Step(None, 1))
            sp_eng.wait_ge(set_dve, DVE_MASK)
            sp_eng.dma_start(mask_dram, mask_rows[:, :]).then_inc(mask_stored, 16)

            def body(i):
                b = i + 1
                if b.valid() and not i.before(1):
                    load_x(b)
                b = i
                if b.valid():
                    wait(sp_eng, x1_ready, b + -2)
                    passed_by(sp_eng, sp_passed)
                    sp_eng.dma_start(xe[b.par][:, :, :], d["xt"][b.number()]).then_inc(xe_in[b.par], 16)
                b = i + 1
                if b.valid():
                    wait(sp_eng, pe_score, b + -2)
                    passed_by(sp_eng, sp_passed)
                    for part, stack, ready, dsem, side_of in ((q_part, q_stack, (q_high, q_mid, q_low), q_stacked, 0),
                                                              (k_part, k_stack, (k_high, k_mid, k_low), k_stacked, 1)):
                        for n in range(3):
                            wait(sp_eng, ready[n], b)
                            for row, pair in enumerate(PARTS):
                                if pair[side_of] != n:
                                    continue
                                sp_eng.dma_start(stack[b.par][16 * row:16 * row + 16, :, :],
                                                 part[n][:, :, :]).then_inc(dsem[b.par], 16)
                    if i.first():
                        sp_eng.wait_ge(mask_stored, 16)
                    sp_eng.dma_start(k_stack[b.par][KROWS:KROWS + 1, :, :],
                                     d["mask"](mask_dram, b.number())).then_inc(k_stacked[b.par], 16)
                b = i + -3
                if b.valid():
                    wait(sp_eng, result_ready, b)
                    passed_by(sp_eng, sp_passed)
                    sp_eng.dma_start(out[b.number()], result[b.par][:, :, :]).then_inc(stored[b.par], 16)
                b = i
                if b.valid():
                    wait(sp_eng, top_t_ready, b)
                    for n in range(3):
                        sp_eng.dma_start(q_stack[b.par][KROWS + 1 + n:KROWS + 2 + n, :, :],
                                         top_t[16 * n:16 * n + 16, :]).then_inc(max_stacked[b.par], 16)

            iterations(sp_eng, body, {0: load_rest})
            for p in range(2):
                sp_eng.wait_ge(stored[p], 16 * (B // 2))

        @block.tensor
        def _(pe):
            mm, tr = nc.tensor.matmul, nc.tensor.transpose

            def product(dst, lhs, rhs, kbs, start=True):
                for k in kbs:
                    last = mm(dst, lhs(k), rhs(k), start=(k == kbs[0]), stop=(k == kbs[-1]))
                return last

            def blk(n):
                return slice(P * n, P * n + P)

            pe.wait_ge(loaded_1st, LOADED_1ST)
            for n, (w, c) in enumerate(((wq, "b_self"), (wk, "b_prev"), (wk, "b_self"))):
                for e in range(NB):
                    last = product(o_psum[0][:, 2 * n + e:2 * n + e + 1], lambda k: w[:, k, blk(e)],
                                   lambda k: col(c, k), (0, 1))
            last.then_inc(set_pe, 1)
            pe.wait_ge(set_dve, DVE_WQ)

            def blend_by_trace():
                pe.wait_ge(set_dve, DVE_BLEND)
                for e in range(NB):
                    last = tr(o_psum[1][:, blk(e)], blend_8[:, e, :, :].rearrange("p r d -> p (r d)"), ident[:, :])
                last.then_inc(set_pe, 1)

            def stacks_ready():
                pe.wait_ge(set_pool, POOL_DONE)
                pe.wait_ge(loaded_3rd, LOADED_3RD)

            def decays_ready():
                pe.wait_ge(set_dve, DVE_DECAY + 1)
                pe.wait_ge(loaded_4th, LOADED_4TH)

            def projected(name, done, b, weights, rows, i):
                side.wait_free(pe, name, i)
                ps = side.bank(name)
                for e in range(NB):
                    last = product(ps[:, 256 * e:256 * e + 256], lambda k: weights[:, k, blk(e)],
                                   rows, range(NB))
                last.then_inc(done.sem, 1)

            def product3(dst, lhs, rhs, cols):
                (lt, lr), (rt, rr) = lhs, rhs
                for k in range(NB):
                    for n, (a, b) in enumerate(((lt, rr), (lr, rt), (lt, rt))):
                        last = mm(dst, cols(a, k), b[:, k, :], start=(k == 0 and n == 0), stop=(k == NB - 1 and n == 2))
                return last

            def split_product(name, done, lhs, rhs, i):
                side.wait_free(pe, name, i)
                for n in range(NB):
                    last = product3(side.bank(name)[:, 256 * n:256 * n + 256], lhs, rhs, lambda a, k: a[:, k, blk(n)])
                last.then_inc(done.sem, 1)

            def natural(name, done, rows, weights, i):
                side.wait_free(pe, name, i)
                ps = side.bank(name)
                for t in range(NB):
                    last = product(ps[:, 256 * t:256 * t + 256], lambda k: rows[:, k, blk(t)],
                                   lambda k: weights[:, k, :], (0, 1))
                last.then_inc(done.sem, 1)

            def flipped(name, done, src, i):
                side.wait_free(pe, name, i)
                ps = side.bank(name)
                for a in range(NB):
                    for c in range(NB):
                        last = tr(ps[:, 256 * a + P * c:256 * a + P * c + P], src[:, c, blk(a)], ident[:, :])
                last.then_inc(done.sem, 1)

            def slot(h):
                return h % 8 * NB + h // 8

            def max_scores(b, h, i):
                if h == 0:
                    wait_dma(pe, q_stacked, b, NQ)
                    wait_dma(pe, k_stacked, b, NK)
                score.wait_free(pe, f"m{h}", i)
                ps = score.bank(f"m{h}")
                for t in range(NB):
                    last = mm(ps[:, 256 * t:256 * t + 256], q_stack[b.par][0:KROWS + 1, slot(h), blk(t)],
                              k_stack[b.par][0:KROWS + 1, slot(h), :], start=True, stop=True)
                last.then_inc(pe_max.sem, 1)

            def attend_scores(b, h, i):
                if h == 0:
                    wait_dma(pe, max_stacked, b, NM)
                score.wait_free(pe, f"a{h}", i)
                ps = score.bank(f"a{h}")
                for k in range(NB):
                    last = mm(ps[:, 256 * k:256 * k + 256], k_stack[b.par][0:KROWS + 4, slot(h), blk(k)],
                              q_stack[b.par][0:KROWS + 4, slot(h), :], start=True, stop=True)
                last.then_inc(pe_score.sem, 1)

            def attend_values(b, g):
                wait(pe, probs_ready, b, 4 * g + 4)
                if g == 0:
                    wait(pe, v_ready, b)
                if g % 2 == 0:
                    wait(pe, o_ready, b + -1, g // 2 + 1)
                for k in range(NB):
                    for j in range(4):
                        h = 4 * g + j
                        last = mm(o_psum[g // 2][32 * j:32 * j + 32, 256 * (g % 2):256 * (g % 2) + 256],
                                  v_ones[b.par][:, k, h, :], probs[:, h % 8, k, :], start=(k == 0),
                                  stop=(k == NB - 1))
                last.then_inc(pe_av.sem, 1)

            def near(b, n, i):
                if n == 0:
                    wait(pe, mod_chain, b)
                    if i.is_number(2):
                        pe.wait_ge(set_dve, DVE_DONE)
                        pe.wait_ge(set_pool, POOL_NEAR)
                side.wait_free(pe, f"near{n}", i)
                w = NCH * (CH - n)
                rhs = mod_stack[:, :].rearrange("p (j r) -> p j r", r=CH)[:, :, 0:CH - n]
                for c in range(NB):
                    last = mm(side.bank(f"near{n}")[:, w * c:w * c + w], near_w[:, n, blk(c)], rhs, start=True, stop=True)
                last.then_inc(pe_near.sem, 1)

            def body(i):
                bp, bm, bt, bx = i + 1, i, i + -1, i + -2
                for u in range(STEPS):
                    if u < H - A_NOW and bt.valid():
                        attend_scores(bt, A_NOW + u, i)
                    if M_AT <= u < M_AT + H and bm.valid():
                        max_scores(bm, u - M_AT, i)
                    if u >= A_AT and bm.valid():
                        attend_scores(bm, u - A_AT, i)
                    if u in (0, 1) and bx.valid():
                        if u == 0:
                            wait(pe, ctx_ready, bx)
                            side.wait_free(pe, "wg", i)
                        last = product(side.bank("wg")[:, 256 * u:256 * u + 256], lambda k: wg[:, k, blk(u)],
                                       lambda k: x1t[bx.par][:, k, :] if k < NB else ctx_t[:, k - NB, :],
                                       range(2 * NB))
                        if u == 1:
                            last.then_inc(pe_wg.sem, 1)
                    if u == 2 and bp.valid():
                        wait(pe, x2_split, bp)
                        split_product("q", pe_q, wq_parts, x2_parts, i)
                    if u == 3 and bt.valid():
                        attend_values(bt, 2)
                    if u == 4 and bp.valid():
                        wait(pe, x_split, bp)
                        if i.first():
                            pe.wait_ge(set_dve, DVE_WK)
                        split_product("k", pe_k, wk_parts, x_parts, i)
                    if u == 4 and bx.valid():
                        wait(pe, gated_ready, bx)
                        flipped("gn", pe_gn, gated, i)
                    if u == 7 and bt.valid():
                        attend_values(bt, 3)
                    if u == 9 and bt.valid():
                        wait(pe, o_ready, bt)
                        for t in range(NB):
                            side.wait_free(pe, f"on{t}", i)
                            for g in range(4):
                                last = tr(side.bank(f"on{t}")[:, blk(g)], o_t[:, g, blk(t)], ident[:, :])
                            last.then_inc(pe_on.sem, 1)
                    if u == 10 and bx.valid():
                        wait(pe, state_in_ready, bx)
                        wait(pe, gated_n_ready, bx)
                        for n in range(2):
                            side.wait_free(pe, f"far{n}", i)
                            for a in range(2):
                                last = product(
                                    side.bank(f"far{n}")[:, 256 * a:256 * a + 256],
                                    lambda k: state_in[:, 8 * (2 * n + a + 2 * k):8 * (2 * n + a + 2 * k) + 8, :]
                                    .rearrange("p j d -> p (j d)"),
                                    lambda k: gated_n[:, k, :], range(n + 1))
                            last.then_inc(pe_far.sem, 1)
                    if u in NEAR_AT and bx.valid():
                        near(bx, NEAR_AT.index(u), i)
                    if u == 11 and bt.valid():
                        wait(pe, attn_ready, bt)
                        flipped("at", pe_at, attn, i)
                    if u == 12 and bx.valid():
                        wait(pe, states_ready, bx)
                        side.wait_free(pe, "y", i)
                        for t in range(NB):
                            for a in range(2):
                                last = mm(side.bank("y")[:, 256 * t:256 * t + 256], far_out[:, a, :],
                                          states[:, 2 * t + a, :], start=(a == 0), stop=(a == 1))
                        last.then_inc(pe_y.sem, 1)
                    if u == 14 and bt.valid():
                        wait(pe, attn_t_ready, bt)
                        projected("wo", pe_wo, bt, wo, lambda k: attn_t[:, k, :], i)
                    if u == 15 and bp.valid():
                        if i.first():
                            pe.wait_ge(loaded_2nd, LOADED_2ND)
                            pe.wait_ge(set_dve, DVE_MASK)
                        split_product("vs", pe_vs, x2_parts, wv_parts, i)
                    if u == 16 and bt.valid():
                        wait(pe, x1_ready, bt)
                        side.wait_free(pe, "h1", i)
                        product(side.bank("h1")[0:HID, 0:T], lambda k: wn1[:, k, :],
                                lambda k: x1t[bt.par][:, k, :], (0, 1)).then_inc(pe_h1.sem, 1)
                    if u == 17 and bp.valid():
                        split_product("vp", pe_vp, x_parts, wv_parts, i)
                    if u == 17 and bx.valid():
                        wait(pe, far_n_ready, bx)
                        flipped("yt", pe_yt, far_n, i)
                    if u == 18 and bt.valid():
                        wait(pe, hid_ready, bt)
                        side.wait_free(pe, "mod", i)
                        mm(side.bank("mod")[:, 0:T], wn2[:, :], hid[:, :], start=True,
                           stop=True).then_inc(pe_mod.sem, 1)
                    if u == 19 and bm.valid():
                        wait(pe, top_chain, bm)
                        side.wait_free(pe, "nm", i)
                        passed_by(pe, pe_passed)
                        for t in range(NB):
                            last = tr(side.bank("nm")[0:3 * H, P // 2 * t:P // 2 * t + P // 2].bitcast(BF16),
                                      top_part[:, t, :, :].rearrange("p n h -> p (n h)"), ident_b[:, :])
                        last.then_inc(pe_nm.sem, 1)
                    if u == 20 and bx.valid():
                        projected("soma", pe_soma, bx, wsoma, lambda k: x1t[bx.par][:, k, :], i)
                    if u == 21 and bx.valid():
                        wait(pe, temporal_ready, bx)
                        projected("gate", pe_gate, bx, wtemp, lambda k: temporal[:, k, :], i)
                    if u == 21 and bp.valid():
                        split_product("ks", pe_ks, wk_parts, x2_parts, i)
                    if u == 21 and i.is_number(0):
                        blend_by_trace()
                    if u == 23 and bx.valid():
                        flipped("x1n", pe_x1n, x1t[bx.par], i)
                    if u == 24 and bt.valid():
                        wait(pe, mod_ready, bt)
                        side.wait_free(pe, "modn", i)
                        passed_by(pe, pe_passed)
                        for t in range(NB):
                            last = tr(side.bank("modn")[:, D * t:D * t + D], mod[0:D, blk(t)], ident[0:D, 0:D])
                        last.then_inc(pe_modn.sem, 1)
                    if u == 25 and bp.valid():
                        wait(pe, self_prod_ready, bp)
                        flipped("prn", pe_prn, self_prod, i)
                    if u == 27 and bm.valid():
                        attend_values(bm, 0)
                    if u == 28 and bx.valid():
                        wait(pe, mixed_ready, bx)
                        natural("out", pe_out, mixed, wout, i)
                    if u == 31 and bm.valid():
                        attend_values(bm, 1)

            iterations(pe, body, {0: stacks_ready, 1: decays_ready})

        def halves(bank):
            return bank[:, :].rearrange("p (n t) -> p n t", n=NB)

        def over_blocks(row):
            return row[:, :].unsqueeze(1).to_broadcast([P, NB, E])

        @block.scalar
        def _(act):
            fn = nc.scalar.activation
            done = [0]

            def mark(ins):
                done[0] += 1
                ins.then_inc(set_act, 1)

            def decays():
                act.wait_ge(set_dve, DVE_SP1)
                mark(fn(sp_u[:, :], sp_t[:, :], ACT.Exp))
                act.wait_ge(set_dve, DVE_SP2)
                mark(fn(sp_t[:, :], sp_u[:, :], ACT.Ln))
                act.wait_ge(set_dve, DVE_EXP)
                mark(fn(sp_u[:, 0:1], sp[:, D + 1:D + 2], ACT.Exp, scale=-1.0))
                mark(fn(pow_col[:, :], c_dist, ACT.Exp, scale=neg_sp[:, 0:1]))
                mark(fn(far_out[:, :, :], c_out_e, ACT.Exp, scale=neg_sp[:, 0:1]))
                mark(fn(far_in[:, :, :], far_in[:, :, :], ACT.Exp, scale=-1.0))
                mark(fn(blend_t[:, :, :], blend_t[:, :, :], ACT.Exp))
                assert done[0] == ACT_DONE

            act.wait_ge(set_dve, DVE_BIAS)

            def attend(b, h):
                wait(act, pe_score, b, h + 1)
                if h >= 8:
                    wait(act, pe_av, b, (h - 8) // 4 + 1)
                else:
                    wait(act, pe_av, b + -1, h // 4 + 3)
                fn(probs[:, h % 8, :, :], halves(score.bank(f"a{h}")), ACT.Exp).then_inc(probs_ready.sem, 1)

            def body(i):
                bp, bm, bt, bx = i + 1, i, i + -1, i + -2
                for u in range(STEPS):
                    if u < H - A_NOW and bt.valid():
                        attend(bt, A_NOW + u)
                    if u >= A_AT and bm.valid():
                        attend(bm, u - A_AT)
                    if u == 2 and bx.valid():
                        wait(act, pe_wg, bx)
                        if i.is_number(2):
                            act.wait_ge(set_pool, POOL_NEAR)
                        for e in range(NB):
                            last = fn(gate_g[:, e, :], halves(side.bank("wg"))[:, e, :], ACT.Tanh,
                                      bias=half_b[:, e:e + 1], scale=0.5)
                        last.then_inc(gate_g_ready.sem, 1)
                    if u == 3 and bp.valid():
                        wait(act, pe_q, bp)
                        wait_dma(act, q_stacked, bp + -1, NQ)
                        for e in range(NB):
                            last = fn(qf[:, e, :], halves(side.bank("q"))[:, e, :], ACT.Identity,
                                      bias=bias_q[:, e:e + 1], scale=SCALE)
                        last.then_inc(q_ready.sem, 1)
                        wait(act, q_ready, bp)
                        fn(q_part[0][:, :, :], qf[:, :, :], ACT.Copy).then_inc(q_high.sem, 1)
                    if u == 5 and bp.valid():
                        wait(act, pe_k, bp)
                        wait_dma(act, k_stacked, bp + -1, NK)
                        for e in range(NB):
                            last = fn(kf[:, e, :], halves(side.bank("k"))[:, e, :], ACT.Identity,
                                      bias=bias_kp[:, e:e + 1])
                        last.then_inc(k_ready.sem, 1)
                        wait(act, k_ready, bp)
                        fn(k_part[0][:, :, :], kf[:, :, :], ACT.Copy).then_inc(k_high.sem, 1)
                    if u == 5 and bx.valid():
                        wait(act, pe_gn, bx)
                        fn(gated_n[:, :, :], halves(side.bank("gn")), ACT.Copy).then_inc(gated_n_ready.sem, 1)
                    if u == 5 and bp.valid():
                        wait(act, q_res_ready, bp)
                        fn(q_part[1][:, :, :], q_res[:, :, :], ACT.Copy).then_inc(q_mid.sem, 1)
                    if u == 17 and bt.valid():
                        wait(act, pe_h1, bt)
                        fn(hid[0:HID, :], side.bank("h1")[0:HID, 0:T], ACT.Gelu,
                           bias=col("bn1")[0:HID, :]).then_inc(hid_ready.sem, 1)
                    if u in (1, 8) and bt.valid():
                        n = u // 8
                        wait(act, pe_av, bt, 2 * n + 2)
                        if n == 0:
                            wait(act, pe_on, bt + -1)
                        fn(o_t[:, 2 * n:2 * n + 2, :], halves(o_psum[n]), ACT.Copy).then_inc(o_ready.sem, 1)
                    if u == 21 and bx.valid():
                        wait(act, pe_soma, bx)
                        wait(act, mixed_ready, bx + -1)
                        for e in range(NB):
                            last = fn(soma[:, e, :], halves(side.bank("soma"))[:, e, :], ACT.Gelu,
                                      bias=col("bsoma", e))
                        last.then_inc(soma_ready.sem, 1)
                    if u == 19 and bt.valid():
                        wait(act, pe_mod, bt)
                        fn(mod_th[:, :], side.bank("mod")[:, 0:T], ACT.Tanh, bias=half_b[:, 4:5],
                           scale=0.5).then_inc(mod_th_ready.sem, 1)
                    if u == 10 and bp.valid():
                        wait(act, k_res_ready, bp)
                        fn(k_part[1][:, :, :], k_res[:, :, :], ACT.Copy).then_inc(k_mid.sem, 1)
                    if u == 12 and bt.valid():
                        wait(act, pe_at, bt)
                        fn(attn_t[:, :, :], halves(side.bank("at")), ACT.Copy).then_inc(attn_t_ready.sem, 1)
                    if u == 13 and bx.valid():
                        wait(act, pe_y, bx)
                        fn(far_n[:, :, :], halves(side.bank("y")), ACT.Copy).then_inc(far_n_ready.sem, 1)
                    if u == 20 and bm.valid():
                        wait(act, pe_nm, bm)
                        wait_dma(act, max_stacked, bm + -1, NM)
                        fn(top_t[:, :], side.bank("nm")[0:3 * H, 0:P].bitcast(BF16), ACT.Copy)\
                            .then_inc(top_t_ready.sem, 1)
                    if u == 21 and bm.valid():
                        wait(act, top_chain, bm, 3)
                        fn(self_p[:, :, :], self_diff[:, :, :], ACT.Exp).then_inc(self_p_ready.sem, 1)
                    if u == 22 and bx.valid():
                        wait(act, pe_gate, bx)
                        for e in range(NB):
                            last = fn(gate_t[:, e, :], halves(side.bank("gate"))[:, e, :], ACT.Tanh,
                                      bias=half_b[:, 2 + e:3 + e], scale=0.5)
                        last.then_inc(gate_t_ready.sem, 1)

            iterations(act, body, {0: decays})

        @block.vector
        def _(dve):
            v = nc.vector
            done = [0]

            def step(ins):
                done[0] += 1
                ins.then_inc(set_dve, 1)
                dve.wait_ge(set_dve, done[0])

            def at(mark):
                assert done[0] == mark, (done[0], mark)

            def split_weights(parts, whole):
                step(v.tensor_scalar(top_bits[:, :, :].bitcast(I32), whole[:, :, :].bitcast(I32), TOP_BITS, None,
                                     ALU.bitwise_and))
                step(v.tensor_copy(parts[0][:, :, :], top_bits[:, :, :]))
                step(v.tensor_tensor(parts[1][:, :, :], whole[:, :, :], top_bits[:, :, :], ALU.subtract))

            def split_x(parts, whole, done_, b):
                v.tensor_scalar(top_bits[:, :, :].bitcast(I32), whole[:, :, :].bitcast(I32), TOP_BITS, None,
                                ALU.bitwise_and).then_inc(done_.sem, 1)
                wait(dve, done_, b, 1)
                v.tensor_copy(parts[0][:, :, :], top_bits[:, :, :]).then_inc(done_.sem, 1)
                v.tensor_tensor(parts[1][:, :, :], whole[:, :, :], top_bits[:, :, :],
                                ALU.subtract).then_inc(done_.sem, 1)
                wait(dve, done_, b)

            dve.wait_ge(loaded_1st, LOADED_1ST)
            split_weights(wq_parts, wq)
            at(DVE_WQ)
            wait_dma(dve, x_in, Step(None, 0), NX)
            split_x(x2_parts, x2t, x2_split, Step(None, 0))
            dve.wait_ge(set_pe, 1)
            step(v.tensor_tensor(bias_q[:, :], o_psum[0][:, 0:2], cols[:, 0:2], ALU.add))
            step(v.tensor_scalar(bias_q[:, :], bias_q[:, :], SCALE, None, ALU.mult))
            step(v.tensor_tensor(bias_kp[:, :], o_psum[0][:, 2:4], cols[:, 2:4], ALU.add))
            step(v.tensor_tensor(bias_ks[:, :], o_psum[0][:, 4:6], cols[:, 2:4], ALU.add))
            at(DVE_BIAS)

            split_weights(wk_parts, wk)
            at(DVE_WK)
            split_x(x_parts, xt, x_split, Step(None, 0))
            dve.wait_ge(loaded_2nd, LOADED_2ND)
            split_weights(wv_parts, wv)
            step(v.tensor_copy(lens[:, :], lens_i[:, :]))
            step(v.tensor_scalar(mask_rows[:, :], iota_k[:, :], lens[:, 0:1], MASKED, ALU.is_ge, ALU.mult))
            at(DVE_MASK)
            dve.wait_ge(set_pool, POOL_DONE)

            def decays():
                dve.wait_ge(loaded_3rd, LOADED_3RD)
                step(v.scalar_tensor_tensor(sp_t[:, :], taus[:, :], -1.0, taus[:, :], ALU.mult, ALU.min))
                at(DVE_SP1)
                dve.wait_ge(set_act, 1)
                step(v.tensor_scalar(sp_u[:, :], sp_u[:, :], 1.0, None, ALU.add))
                at(DVE_SP2)
                dve.wait_ge(set_act, 2)
                step(v.scalar_tensor_tensor(sp[:, :], taus[:, :], 0.0, sp_t[:, :], ALU.max, ALU.add))
                step(v.tensor_scalar(neg_sp[:, :], sp[:, D:D + 1], -1.0, None, ALU.mult))
                step(v.tensor_tensor(far_in[:, :, :], c_far_e, sp[:, 0:D].unsqueeze(1).to_broadcast([P, 6 * CH, D]),
                                     ALU.mult))
                step(v.reduce_max(blend_m[:, :], blend_t[:, :, :], AX.X))
                step(v.tensor_tensor(blend_t[:, :, :], blend_t[:, :, :],
                                     blend_m[:, :].unsqueeze(2).to_broadcast([P, NB, D]), ALU.subtract))
                at(DVE_EXP)

            def blend_softmax():
                dve.wait_ge(set_act, ACT_DONE)
                step(v.reduce_sum(blend_s[:, :], blend_t[:, :, :], AX.X))
                step(v.reciprocal(blend_s[:, :], blend_s[:, :]))
                step(v.tensor_scalar(blend_s[:, :], blend_s[:, :], 0.5, None, ALU.mult))
                step(v.tensor_tensor(blend_t[:, :, :], blend_t[:, :, :],
                                     blend_s[:, :].unsqueeze(2).to_broadcast([P, NB, D]), ALU.mult))
                step(v.tensor_copy(blend_8[:, :, :, :], blend_t[:, :, :].unsqueeze(2).to_broadcast([P, NB, 8, D])))
                at(DVE_BLEND)
                step(v.memset(decay[:, :], 0.0))
                step(v.tensor_scalar(decay[:, :], decay[:, :], sp_u[:, 0:1], None, ALU.add))
                step(v.tensor_tensor(far_out[:, :, :], far_out[:, :, :], c_out_m, ALU.mult))
                step(v.tensor_tensor(far_in[:, :, :], far_in[:, :, :], c_far_m, ALU.mult))
                step(v.tensor_scalar(half_b[:, 0:2], cols[:, 10:12], 0.5, None, ALU.mult))
                step(v.tensor_scalar(half_b[:, 2:4], cols[:, 14:16], 0.5, None, ALU.mult))
                step(v.tensor_scalar(half_b[:, 4:5], col("bn2"), 0.5, None, ALU.mult))
                at(DVE_DECAY)

            def blend_made():
                dve.wait_ge(set_pe, 2)
                step(v.tensor_copy(blend[:, :], o_psum[1][:, 0:E]))
                step(v.tensor_scalar(pow_col[:, :], pow_col[:, :], c_slot[:, 0:1], None, ALU.mult))
                dve.wait_ge(loaded_4th, LOADED_4TH)
                step(v.tensor_scalar(wout[:, :, :], wout[:, :, :], 0.5, None, ALU.mult))
                at(DVE_DONE)

            def add_bias_v(dst, name, done_, b):
                v.tensor_tensor(dst, halves(side.bank(name)).rearrange("p n (h d) -> p n h d", d=DH),
                                over_blocks(bv_row).rearrange("p n (h d) -> p n h d", d=DH),
                                ALU.add).then_inc(done_.sem, 1)

            def near(b, n):
                wait(dve, pe_near, b, n + 1)
                if n == 0:
                    v.tensor_tensor(near_sum[:, :, :], gated[:, :, :], halves(side.bank("near0")),
                                    ALU.mult).then_inc(near_prod.sem, 1)
                    return
                if n >= 3:
                    wait(dve, near_added, b, n - 2)
                w = NB * NCH * (CH - n)
                v.tensor_tensor(near_p[n % 2][:, :, 0:CH - n],
                                gated[:, :, :].rearrange("p c (j r) -> p (c j) r", r=CH)[:, :, 0:CH - n],
                                side.bank(f"near{n}")[:, 0:w].rearrange("p (j r) -> p j r", r=CH - n),
                                ALU.mult).then_inc(near_prod.sem, 1)

            def body(i):
                bn, bp, bm, bt, bx, bz = i + 2, i + 1, i, i + -1, i + -2, i + -3
                for u in range(STEPS):
                    if u == 19 and i.is_number(0):
                        blend_softmax()
                    if M_AT <= u < M_AT + H and bm.valid():
                        h = u - M_AT
                        wait(dve, pe_max, bm, h + 1)
                        v.reduce_max(row_max[:, :, h], halves(score.bank(f"m{h}")), AX.X).then_inc(max_ready.sem, 1)
                    if u == 17 and bm.valid():
                        def by_block(heads):
                            return heads.rearrange("p t (e h) -> p t e h", e=NB)

                        def part(n):
                            return top_part[:, :, n, :].rearrange("p t (h e) -> p t e h", e=NB)

                        wait(dve, max_ready, bm)
                        wait(dve, self_score_ready, bm)
                        v.tensor_tensor(top[:, :, :], row_max[:, :, :], self_score[bm.par][:, :, :],
                                        ALU.max).then_inc(top_chain.sem, 1)
                        wait(dve, top_chain, bm, 1)
                        v.tensor_copy(part(0), by_block(top[:, :, :])).then_inc(top_chain.sem, 1)
                        v.tensor_tensor(self_diff[:, :, :], self_score[bm.par][:, :, :], top[:, :, :],
                                        ALU.subtract).then_inc(top_chain.sem, 1)
                        wait(dve, top_chain, bm, 3)
                        v.tensor_tensor(by_block(top_res[:, :, :]), by_block(top[:, :, :]), part(0),
                                        ALU.subtract).then_inc(top_chain.sem, 1)
                        wait(dve, top_chain, bm, 4)
                        v.tensor_copy(part(1), by_block(top_res[:, :, :])).then_inc(top_chain.sem, 1)
                        wait(dve, top_chain, bm, 5)
                        v.tensor_tensor(part(2), by_block(top_res[:, :, :]), part(1),
                                        ALU.subtract).then_inc(top_chain.sem, 1)
                    if u == 3 and bx.valid():
                        wait(dve, gate_g_ready, bx)
                        v.scalar_tensor_tensor(gated[:, :, :], gate_g[:, :, :], 1.0, x1t[bx.par][:, :, :],
                                               ALU.add, ALU.mult).then_inc(gated_ready.sem, 1)
                    if u == 22 and bp.valid():
                        wait(dve, pe_ks, bp)
                        wait(dve, q_ready, bp)
                        for e in range(NB):
                            last = v.scalar_tensor_tensor(self_prod[:, e, :], halves(side.bank("ks"))[:, e, :],
                                                          bias_ks[:, e:e + 1], qf[:, e, :], ALU.add, ALU.mult)
                        last.then_inc(self_prod_ready.sem, 1)
                    if u == 29 and bx.valid():
                        wait(dve, pe_out, bx)
                        for t in range(NB):
                            v.bn_stats(stats[:, t, :], halves(side.bank("out"))[:, t, :]).then_inc(norm_chain.sem, 1)
                        wait(dve, norm_chain, bx, 2)
                        passed_by(dve, dve_passed)
                        for t in range(NB):
                            v.bn_aggr(mean_var[:, t, :], stats[:, t, :]).then_inc(norm_chain.sem, 1)
                        wait(dve, norm_chain, bx, 4)
                        v.tensor_scalar(var_eps[:, :], mean_var[:, :, 1], EPS, None,
                                        ALU.add).then_inc(norm_chain.sem, 1)
                        for t in range(NB):
                            v.scalar_tensor_tensor(centred[:, t, :], halves(side.bank("out"))[:, t, :],
                                                   mean_var[:, t, 0:1], gamma_row[:, :], ALU.subtract,
                                                   ALU.mult).then_inc(norm_chain.sem, 1)
                    if u == 0 and bz.valid():
                        wait(dve, rstd_ready, bz)
                        wait(dve, norm_chain, bz)
                        wait(dve, x1_beta_ready, bz)
                        wait_dma(dve, stored, bz + -2, 16)
                        for t in range(NB):
                            last = v.scalar_tensor_tensor(result[bz.par][:, t, :], centred[:, t, :], rstd[:, t:t + 1],
                                                          x1_beta[:, t, :], ALU.mult, ALU.add)
                        last.then_inc(result_ready.sem, 1)
                    if u == 24 and bx.valid():
                        wait(dve, pe_x1n, bx)
                        wait(dve, result_ready, bx + -1)
                        v.tensor_tensor(x1_beta[:, :, :], halves(side.bank("x1n")), over_blocks(beta_row),
                                        ALU.add).then_inc(x1_beta_ready.sem, 1)
                    if u == 9 and bt.valid():
                        wait(dve, self_pv_ready, bt)
                        for t in range(NB):
                            wait(dve, pe_on, bt, t + 1)
                            o = side.bank(f"on{t}")[:, :].rearrange("p (h c) -> p h c", c=32)
                            v.tensor_tensor(num[:, t, :].rearrange("p (h d) -> p h d", d=DH), o[:, :, 0:DH],
                                            self_pv[:, t, :].rearrange("p (h d) -> p h d", d=DH),
                                            ALU.add).then_inc(num_chain.sem, 1)
                            v.tensor_tensor(den[:, t, :], o[:, :, DH], self_p[:, t, :],
                                            ALU.add).then_inc(num_chain.sem, 1)
                        wait(dve, num_chain, bt, 4)
                        v.reciprocal(rden[:, :, :], den[:, :, :]).then_inc(num_chain.sem, 1)
                    if u == 25 and bt.valid():
                        wait(dve, pe_modn, bt)
                        v.tensor_copy(mod_n[:, :, :], side.bank("modn")[:, 0:NB * D].rearrange(
                            "p (t d) -> p t d", d=D)).then_inc(mod_n_ready.sem, 1)
                    if u == 18 and bp.valid():
                        wait(dve, pe_vp, bp)
                        add_bias_v(v_ones[bp.par][:, :, :, 0:DH], "vp", v_ready, bp)
                    if u in NEAR_AT and bx.valid():
                        near(bx, NEAR_AT.index(u))
                    if u == 10 and bx.valid():
                        for n in range(2):
                            wait(dve, pe_far, bx, n + 1)
                            v.tensor_tensor(states[:, 2 * n:2 * n + 2, :], halves(side.bank(f"far{n}")),
                                            over_blocks(blend), ALU.mult).then_inc(states_ready.sem, 1)
                    if u == 15 and bt.valid():
                        wait(dve, pe_wo, bt)
                        wait_dma(dve, xe_in, bt, 16)
                        for c in range(NB):
                            last = v.scalar_tensor_tensor(x1t[bt.par][:, c, :], halves(side.bank("wo"))[:, c, :],
                                                          col("bo", c), xe[bt.par][:, c, :], ALU.add, ALU.add)
                        last.then_inc(x1_ready.sem, 1)
                    if u == 20 and bt.valid():
                        wait(dve, x1_ready, bt)
                        for c in range(NB):
                            last = v.tensor_tensor_scan(ctx_t[:, c, :], decay[:, :], x1t[bt.par][:, c, :], 0.0,
                                                        ALU.mult, ALU.add)
                        last.then_inc(ctx_ready.sem, 1)
                    if u == 19 and bx.valid():
                        wait(dve, pe_yt, bx)
                        wait(dve, near_added, bx)
                        v.tensor_tensor(temporal[:, :, :], near_sum[:, :, :], halves(side.bank("yt")),
                                        ALU.add).then_inc(temporal_ready.sem, 1)
                    if u == 23 and i.is_number(0):
                        blend_made()
                    if u in (27, 28) and bn.valid():
                        wait(dve, pe_vp, bn + -1)
                        if u == 27:
                            wait_dma(dve, x_in, bn, NX)
                            split_x(x2_parts, x2t, x2_split, bn)
                        else:
                            split_x(x_parts, xt, x_split, bn)
                    if u == 16 and bp.valid():
                        wait(dve, pe_vs, bp)
                        add_bias_v(v_self[bp.par][:, :, :].rearrange("p n (h d) -> p n h d", d=DH), "vs",
                                   v_self_ready, bp)
                    if u == 23 and bx.valid():
                        wait(dve, gate_t_ready, bx)
                        wait(dve, soma_ready, bx)
                        v.scalar_tensor_tensor(mixed[:, :, :], gate_t[:, :, :], 1.0, soma[:, :, :],
                                               ALU.add, ALU.mult).then_inc(mixed_ready.sem, 1)
                    if u == 26 and bp.valid():
                        wait(dve, pe_prn, bp)
                        v.reduce_sum(self_score[bp.par][:, :, :].rearrange("p t (e h) -> p (t e) h", e=NB),
                                     side.bank("prn")[:, :].rearrange("p (x d h) -> p x h d", d=DH, h=8),
                                     AX.X).then_inc(self_score_ready.sem, 1)

            iterations(dve, body, {0: decays})

        @block.gpsimd
        def _(pool):
            g = nc.gpsimd
            done = [0]

            def step(ins):
                done[0] += 1
                ins.then_inc(set_pool, 1)
                pool.wait_ge(set_pool, done[0])

            step(g.memset(wn2[HID:P, :], 0.0))
            step(g.memset(hid[HID:P, :], 0.0))
            step(g.memset(minus_half[:, :], -0.5))
            for p in range(2):
                step(g.memset(v_ones[p][:, :, :, :], 0.0))
                step(g.memset(q_stack[p][KROWS:P, :, :], 1.0))
                step(g.memset(k_stack[p][KROWS:P, :, :], -1.0))
            for p in range(2):
                step(g.memset(v_ones[p][:, :, :, DH:DH + 1], 1.0))
            step(g.memset(mod_res[:, :], 0.0))
            assert done[0] == POOL_DONE

            def near_weights(pairs):
                pool.wait_ge(set_dve, DVE_DONE)
                for pair in pairs:
                    for n in range(2):
                        step(g.tensor_scalar(near_f[:, n, :], blend[:, :], pow_col[:, 2 * pair + n:2 * pair + n + 1],
                                             0.0, ALU.mult, ALU.add))
                    step(g.tensor_scalar(near_h[:, :, :], near_f[:, :, :], 1.0, 0.0, ALU.mult, ALU.add))
                    step(g.tensor_scalar(near_r[:, :, :], near_h[:, :, :], c_slot[:, 1:2], 0.0, ALU.mult, ALU.add))
                    step(g.tensor_tensor(near_r[:, :, :], near_r[:, :, :], near_f[:, :, :], ALU.add))
                    step(g.tensor_scalar(near_m[:, :, :], near_r[:, :, :], 1.0, 0.0, ALU.mult, ALU.add))
                    step(g.tensor_scalar(near_f[:, :, :], near_m[:, :, :], c_slot[:, 2:3], 0.0, ALU.mult, ALU.add))
                    step(g.tensor_tensor(near_w[:, 2 * pair:2 * pair + 2, :], near_f[:, :, :], near_r[:, :, :],
                                         ALU.add))
                if CH // 2 - 1 in pairs:
                    assert done[0] == POOL_NEAR

            def residual(dst, whole, part, done_, b):
                g.tensor_tensor(dst[:, :, :], whole[:, :, :], part[:, :, :], ALU.subtract).then_inc(done_.sem, 1)

            def near_add(b, n):
                wait(pool, near_prod, b, n + 1)
                if n > 1:
                    wait(pool, near_added, b, n - 1)
                rows = near_sum[:, :, :].rearrange("p c (j r) -> p (c j) r", r=CH)[:, :, n:CH]
                g.tensor_tensor(rows, rows, near_p[n % 2][:, :, 0:CH - n], ALU.add).then_inc(near_added.sem, 1)

            def body(i):
                bp, bm, bt, bx = i + 1, i, i + -1, i + -2
                for u in range(STEPS):
                    if u == 28 and i.is_number(0):
                        near_weights((0, 1))
                    if u in (11, 28) and i.is_number(1):
                        near_weights((2 + (u == 28),))
                    if u == 4 and bp.valid():
                        wait(pool, q_high, bp)
                        residual(q_res, qf, q_part[0], q_res_ready, bp)
                    if u == 7 and bp.valid():
                        wait(pool, k_high, bp)
                        residual(k_res, kf, k_part[0], k_res_ready, bp)
                    if u == 6 and bp.valid():
                        wait(pool, q_mid, bp)
                        wait(pool, q_res_ready, bp)
                        residual(q_part[2], q_res, q_part[1], q_low, bp)
                    if u == 10 and bt.valid():
                        wait(pool, num_chain, bt)
                        heads = num[:, :, :].rearrange("p t (h d) -> p (t h) d", d=DH)
                        g.tensor_tensor(attn[:, :, :].rearrange("p t (h d) -> p (t h) d", d=DH), heads,
                                        rden[:, :, :].rearrange("p t h -> p (t h)").unsqueeze(2)
                                        .to_broadcast([P, NB * H, DH]), ALU.mult).then_inc(attn_ready.sem, 1)
                    if u == 11 and bp.valid():
                        wait(pool, k_mid, bp)
                        wait(pool, k_res_ready, bp)
                        residual(k_part[2], k_res, k_part[1], k_low, bp)
                    if u == 26 and bt.valid():
                        wait(pool, mod_n_ready, bt)
                        for k, (lo, hi) in enumerate(((0, 4 * CH), (4 * CH, 6 * CH))):
                            last = g.tensor_tensor(state_in[:, lo:hi, :], far_in[:, lo:hi, :],
                                                   mod_n[:, k, :].unsqueeze(1).to_broadcast([P, hi - lo, D]), ALU.mult)
                        last.then_inc(state_in_ready.sem, 1)
                    if u in NEAR_AT[1:] and bx.valid():
                        near_add(bx, NEAR_AT.index(u))
                    if u == 20 and bt.valid():
                        wait(pool, mod_th_ready, bt)
                        passed_by(pool, pool_passed)
                        g.tensor_scalar(mod[:, :], mod_th[:, :], 0.5, 1.0, ALU.mult, ALU.add)\
                            .then_inc(mod_ready.sem, 1)
                        wait(pool, mod_ready, bt)
                        passed_by(pool, pool_passed)
                        g.tensor_scalar(mod_stack[:, :], mod[:, :], 1.0, 0.0, ALU.mult, ALU.add)\
                            .then_inc(mod_chain.sem, 1)
                        wait(pool, mod_chain, bt, 1)
                        g.tensor_tensor(mod_res[96:P, :], mod[96:P, :], mod_stack[96:P, :], ALU.subtract)\
                            .then_inc(mod_chain.sem, 1)
                        wait(pool, mod_chain, bt, 2)
                        g.tensor_tensor(mod_stack[32:64, :], mod[32:64, :], mod_stack[32:64, :], ALU.subtract)\
                            .then_inc(mod_chain.sem, 1)
                        wait(pool, mod_chain, bt, 3)
                        passed_by(pool, pool_passed)
                        g.tensor_scalar(mod_mid[96:P, :], mod_res[96:P, :], 1.0, 0.0, ALU.mult, ALU.add)\
                            .then_inc(mod_chain.sem, 1)
                        wait(pool, mod_chain, bt, 4)
                        g.tensor_tensor(mod_stack[96:P, :], mod_res[96:P, :], mod_mid[96:P, :], ALU.subtract)\
                            .then_inc(mod_chain.sem, 1)
                        wait(pool, mod_chain, bt)
                    if u == 27 and bm.valid():
                        wait(pool, self_p_ready, bm)
                        wait(pool, v_self_ready, bm)
                        g.tensor_tensor(self_pv[:, :, :].rearrange("p t (h d) -> p (t h) d", d=DH),
                                        v_self[bm.par][:, :, :].rearrange("p t (h d) -> p (t h) d", d=DH),
                                        self_p[:, :, :].rearrange("p t h -> p (t h)").unsqueeze(2)
                                        .to_broadcast([P, NB * H, DH]), ALU.mult).then_inc(self_pv_ready.sem, 1)
                    if u == 29 and bx.valid():
                        wait(pool, norm_chain, bx, 5)
                        g.tensor_tensor(rstd[:, :], var_eps[:, :], minus_half[:, :], ALU.pow)\
                            .then_inc(rstd_ready.sem, 1)

            iterations(pool, body, {})


def constants():
    far_e, far_m = np.zeros((P, 6, CH, 1), np.float32), np.zeros((P, 6, CH, 1), np.float32)
    for blk in range(6):
        i, k = (blk, 0) if blk < SB else (blk - 2, 1)
        start = CH * (CH * i + np.arange(CH))[None, :]
        e = start - 1 - (P * k + np.arange(P)[:, None])
        far_e[:, blk, :, 0], far_m[:, blk, :, 0] = np.maximum(e, 0), e >= 0
    far_e, far_m = (np.broadcast_to(a, (P, 6, CH, D)).reshape(P, -1) for a in (far_e, far_m))
    chunk = (np.arange(P) // D)[:, None]
    out_e, out_m = np.zeros((P, 2, P), np.float32), np.zeros((P, 2, P), np.float32)
    for a in range(2):
        e = np.arange(P)[None, :] - (P // 2 * a + CH * chunk) + 1
        inside = (e >= 1) & (e <= CH)
        out_e[:, a, :], out_m[:, a, :] = np.where(inside, e, 0), inside
    dist = np.broadcast_to(np.arange(CH, dtype=np.float32), (P, CH))
    slot = np.arange(P) // D
    slots = np.stack([sign * np.isin(slot, s) for sign, s in ((1, (0, 1, 2, 3, 4, 6)), (-1, (1, 3, 4)), (-1, (4,)))], 1)
    return np.concatenate([far_e, far_m, out_e.reshape(P, -1), out_m.reshape(P, -1), dist, slots], 1)\
        .astype(np.float32)


def kernel(**inputs):
    import concourse.bacc as bacc
    from concourse.bass_utils import run_bass_kernel_spmd
    a = {k: np.asarray(v) for k, v in inputs.items()}

    def blocks(w):
        return np.ascontiguousarray(w.reshape(-1, P, w.shape[1]).transpose(1, 0, 2))

    def column(v):
        return v.reshape(-1, P).T

    order = np.arange(E).reshape(NB, H // NB, DH).transpose(0, 2, 1).reshape(-1)
    row = {n: np.ascontiguousarray(np.broadcast_to(a[k], (P, E))) for n, k in
           (("bv", "L0_cond_bv"), ("gamma", "L1_cond_gamma"), ("beta", "L1_cond_beta"))}
    cols = np.zeros((P, 18 + D + 2), np.float32)
    for at, v in ((0, a["L0_cond_bq"][order]), (2, a["L0_cond_bk"][order]), (4, a["L0_cond_b_self"].reshape(-1)),
                  (6, a["L0_cond_b_prev"].reshape(-1)), (8, a["L0_cond_bo"]), (10, a["L1_cond_bg"]),
                  (12, a["L1_cond_bsoma"]), (14, a["L1_cond_btemp"])):
        cols[:, at:at + 2] = column(v)
    cols[0:HID, 16] = a["L1_cond_bn1"]
    cols[:, 17] = np.tile(a["condB_bn2"], P // D)
    tau = a["condB_tauraws"]
    cols[:, 18:] = np.concatenate([np.broadcast_to(tau, (P, D)), np.tile(tau, P // D)[:, None],
                                   np.broadcast_to(a["L1_cond_tau_ctx"], (P, 1))], 1)

    def rows_t(x):
        return np.ascontiguousarray(x.reshape(B, T, NB, P).transpose(0, 3, 2, 1))

    import ml_dtypes
    feeds = {
        "xt": rows_t(a["x"]), "x2t": rows_t(a["fside_BxSxS_0"]),
        "wq": blocks(a["L0_cond_Wq"][:, order]), "wk": blocks(a["L0_cond_Wk"][:, order]),
        "wv": blocks(a["L0_cond_Wv"]), "wo": blocks(a["L0_cond_Wo"]), "wg": blocks(a["L1_cond_Wg"].T),
        "wn1": blocks(a["L1_cond_Wn1"].T), "wn2": np.ascontiguousarray(np.tile(a["cond_256"].T, (1, P // D))),
        "wsoma": blocks(a["L1_cond_Wsoma"].T), "wtemp": blocks(a["L1_cond_Wtemp"].T),
        "wout": blocks(a["L1_cond_Wout"].T), "cols": cols, "bv": row["bv"],
        "gamma_beta": np.ascontiguousarray(np.stack([row["gamma"], row["beta"]], 1)),
        "blend": blocks(a["cond_1024"].T), "consts": constants(), "ident": np.eye(P, dtype=np.float32),
        "ident_b": np.eye(P, dtype=ml_dtypes.bfloat16),
        "iota": np.ascontiguousarray(np.broadcast_to(np.arange(T, dtype=np.float32), (B, T))),
        "lens": np.ascontiguousarray(a["itok_B_18_1004"].reshape(B, 1)),
    }
    nc = bacc.Bacc("TRN2", target_bir_lowering=False, num_devices=1)
    d = {k: nc.dram_tensor(f"in_{k}", v.shape, mybir.dt.from_np(v.dtype), kind="ExternalInput").ap()
         for k, v in feeds.items()}
    d["mask"] = lambda rows, b: rows[b].unsqueeze(0).unsqueeze(1).to_broadcast([1, H, T])
    out = nc.dram_tensor("out", (B, P, NB, E), F32, kind="ExternalOutput").ap()
    build(nc, d, out)
    r = run_bass_kernel_spmd(nc, [{f"in_{k}": v for k, v in feeds.items()}], core_ids=[0])
    got = np.asarray(r.results[0]["out"])
    return np.ascontiguousarray(got.transpose(0, 2, 1, 3).reshape(B, T, E))
```
